# Optimizing a Trainium2 kernel written in Bass

```python
import numpy as np
import jax
import jax.numpy as jnp

def _softmax(x, axis=-1):
    return jax.nn.softmax(x, axis=axis)

def _gelu(x):
    return jax.nn.gelu(x, approximate=True)

def _silu(x):
    return jax.nn.silu(x)

def _sigmoid(x):
    return jax.nn.sigmoid(x)

def _layernorm(x, axis=-1, eps=1e-05):
    m = jnp.mean(x, axis=axis, keepdims=True)
    v = jnp.var(x, axis=axis, keepdims=True)
    return (x - m) / jnp.sqrt(v + eps)

def _scatter_add(tgt, idx, src, axis=0):
    return tgt.at[idx].add(src)

def _segment_sum(src, seg, n):
    return jax.ops.segment_sum(src, seg, n)
kernel_name = 'mk_hybrid_d1_jaxref_r8_f1da94'

def setup_inputs(seed: int=0):
    np.random.seed(seed)
    _w = jnp.asarray

    def _L0_attn_a_setup():
        import jax, jax.numpy as jnp
        import numpy as np
        DIM = 128
        HEADS = 16
        HD = DIM // HEADS
        HID = 4 * DIM
        TPF = 1374
        LR = 0.1
        NS_ITERS = 5
        TTT_STEPS = 2
        B, S = (2, 4)
        SN = S * TPF

        def _newton_schulz(G, iters=NS_ITERS):
            a, b, c = (3.4445, -4.775, 2.0315)
            X = G / (jnp.linalg.norm(G) + 1e-07)
            transposed = G.shape[0] > G.shape[1]
            if transposed:
                X = X.T
            for _ in range(iters):
                A = X @ X.T
                X = a * X + (b * A + c * (A @ A)) @ X
            return X.T if transposed else X

        def _muon_update(p, g):
            return p - LR * _newton_schulz(g)
        key = jax.random.key(seed)
        ks = jax.random.split(key, 8)
        inp = {'x': jax.random.normal(ks[0], (B, SN, DIM), jnp.float32), 'qkv_w': jax.random.normal(ks[1], (DIM, 3 * DIM), jnp.float32) * DIM ** (-0.5), 'qkv_b': jnp.zeros((3 * DIM,), jnp.float32), 'qn_scale': jnp.ones((HD,), jnp.float32), 'qn_bias': jnp.zeros((HD,), jnp.float32), 'kn_scale': jnp.ones((HD,), jnp.float32), 'kn_bias': jnp.zeros((HD,), jnp.float32), 'ttt_gate': jax.random.normal(ks[2], (DIM, HID), jnp.float32) * DIM ** (-0.5), 'ttt_val': jax.random.normal(ks[3], (DIM, HID), jnp.float32) * DIM ** (-0.5), 'ttt_proj': jax.random.normal(ks[4], (HID, DIM), jnp.float32) * HID ** (-0.5), 'proj_w': jax.random.normal(ks[5], (DIM, DIM), jnp.float32) * DIM ** (-0.5), 'proj_b': jnp.zeros((DIM,), jnp.float32)}
        return inp
    _L0_attn_a_in = _L0_attn_a_setup()

    def _L0_attn_b_setup():
        import jax, jax.numpy as jnp
        import numpy as np
        DIM = 128
        HEADS = 16
        DIM_HEAD = 64
        NUM_FRAMES = 8
        PATCHES_PER_FRAME = 32
        BATCH = 2
        SEQ = NUM_FRAMES * PATCHES_PER_FRAME
        EPS = 1e-05

        def _block_causal_mask(seq_len: int) -> jnp.ndarray:
            frame = jnp.arange(seq_len) // PATCHES_PER_FRAME
            return frame[:, None] >= frame[None, :]
        key = jax.random.key(seed)
        k1, k2, k3 = jax.random.split(key, 3)
        inner = HEADS * DIM_HEAD
        x = jax.random.normal(k1, (BATCH, SEQ, DIM), dtype=jnp.float32)
        g = jnp.ones((1, 1, DIM), dtype=jnp.float32)
        b = jnp.zeros((1, 1, DIM), dtype=jnp.float32)
        w_qkv = jax.random.normal(k2, (DIM, 3 * inner), dtype=jnp.float32) * DIM ** (-0.5)
        w_out = jax.random.normal(k3, (inner, DIM), dtype=jnp.float32) * inner ** (-0.5)
        b_out = jnp.zeros((DIM,), dtype=jnp.float32)
        return {'x': x, 'g': g, 'b': b, 'w_qkv': w_qkv, 'w_out': w_out, 'b_out': b_out}
    _L0_attn_b_in = _L0_attn_b_setup()

    def _L0_ffn_setup():
        import jax, jax.numpy as jnp
        import numpy as np
        B, S, D = (4, 256, 128)
        O = 128
        E = 8
        K = 2
        key = jax.random.key(seed)
        k1, k2, k3, k4, k5 = jax.random.split(key, 5)
        scale = 1.0 / np.sqrt(D)
        x = jax.random.normal(k1, (B, S, D), dtype=jnp.float32)
        We = jax.random.uniform(k2, (E, D, O), dtype=jnp.float32, minval=-scale, maxval=scale)
        be = jax.random.uniform(k3, (E, O), dtype=jnp.float32, minval=-scale, maxval=scale)
        Wg = jax.random.uniform(k4, (D, E), dtype=jnp.float32, minval=-scale, maxval=scale)
        bg = jax.random.uniform(k5, (E,), dtype=jnp.float32, minval=-scale, maxval=scale)
        return {'x': x, 'We': We, 'be': be, 'Wg': Wg, 'bg': bg}
    _L0_ffn_in = _L0_ffn_setup()
    _d = {'L0_attn_a_x': _L0_attn_a_in['x'], 'L0_attn_a_qkv_w': _L0_attn_a_in['qkv_w'], 'L0_attn_a_qkv_b': _L0_attn_a_in['qkv_b'], 'L0_attn_a_qn_scale': _L0_attn_a_in['qn_scale'], 'L0_attn_a_qn_bias': _L0_attn_a_in['qn_bias'], 'L0_attn_a_kn_scale': _L0_attn_a_in['kn_scale'], 'L0_attn_a_kn_bias': _L0_attn_a_in['kn_bias'], 'L0_attn_a_ttt_gate': _L0_attn_a_in['ttt_gate'], 'L0_attn_a_ttt_val': _L0_attn_a_in['ttt_val'], 'L0_attn_a_ttt_proj': _L0_attn_a_in['ttt_proj'], 'L0_attn_a_proj_w': _L0_attn_a_in['proj_w'], 'L0_attn_a_proj_b': _L0_attn_a_in['proj_b'], 'L0_attn_b_g': _L0_attn_b_in['g'], 'L0_attn_b_b': _L0_attn_b_in['b'], 'L0_attn_b_w_qkv': _L0_attn_b_in['w_qkv'], 'L0_attn_b_w_out': _L0_attn_b_in['w_out'], 'L0_attn_b_b_out': _L0_attn_b_in['b_out'], 'L0_ffn_We': _L0_ffn_in['We'], 'L0_ffn_be': _L0_ffn_in['be'], 'L0_ffn_Wg': _L0_ffn_in['Wg'], 'L0_ffn_bg': _L0_ffn_in['bg']}
    _x0 = _d['L0_attn_a_x']
    _d['L0_attn_a_x'] = jax.random.normal(jax.random.fold_in(jax.random.key(seed), 1), (4, 512, 128), dtype=_x0.dtype)
    del _x0
    return _d

def reference(L0_attn_a_x, L0_attn_a_qkv_w, L0_attn_a_qkv_b, L0_attn_a_qn_scale, L0_attn_a_qn_bias, L0_attn_a_kn_scale, L0_attn_a_kn_bias, L0_attn_a_ttt_gate, L0_attn_a_ttt_val, L0_attn_a_ttt_proj, L0_attn_a_proj_w, L0_attn_a_proj_b, L0_attn_b_g, L0_attn_b_b, L0_attn_b_w_qkv, L0_attn_b_w_out, L0_attn_b_b_out, L0_ffn_We, L0_ffn_be, L0_ffn_Wg, L0_ffn_bg):

    def _L0_attn_a_ref(x, qkv_w, qkv_b, qn_scale, qn_bias, kn_scale, kn_bias, ttt_gate, ttt_val, ttt_proj, proj_w, proj_b):
        import jax, jax.numpy as jnp
        import numpy as np
        DIM = 128
        HEADS = 16
        HD = DIM // HEADS
        HID = 4 * DIM
        TPF = 1374
        LR = 0.1
        NS_ITERS = 5
        TTT_STEPS = 2
        B, S = (2, 4)
        SN = S * TPF

        def _newton_schulz(G, iters=NS_ITERS):
            a, b, c = (3.4445, -4.775, 2.0315)
            X = G / (jnp.linalg.norm(G) + 1e-07)
            transposed = G.shape[0] > G.shape[1]
            if transposed:
                X = X.T
            for _ in range(iters):
                A = X @ X.T
                X = a * X + (b * A + c * (A @ A)) @ X
            return X.T if transposed else X

        def _muon_update(p, g):
            return p - LR * _newton_schulz(g)
        Bx, SNx, _ = x.shape
        qkv = x @ qkv_w + qkv_b
        q, k, v = jnp.split(qkv, 3, axis=-1)
        q = q.reshape(Bx, SNx, HEADS, HD)
        k = k.reshape(Bx, SNx, HEADS, HD)
        q = q / (jnp.linalg.norm(q, axis=-1, keepdims=True) + 1e-06) * qn_scale + qn_bias
        k = k / (jnp.linalg.norm(k, axis=-1, keepdims=True) + 1e-06) * kn_scale + kn_bias
        q_ttt = q.reshape(-1, DIM)
        k_ttt = k.reshape(-1, DIM)
        v_ttt = v.reshape(-1, DIM)
        theta = {'gate': ttt_gate, 'val': ttt_val, 'proj': ttt_proj}

        def loss_fn(p):
            h = jax.nn.swish(k_ttt @ p['gate']) * (k_ttt @ p['val'])
            pred = h @ p['proj']
            return jnp.mean((pred - v_ttt) ** 2)
        for _ in range(TTT_STEPS):
            grads = jax.grad(loss_fn)(theta)
            theta = {kk: _muon_update(theta[kk], grads[kk]) for kk in theta}
        h_q = jax.nn.swish(q_ttt @ theta['gate']) * (q_ttt @ theta['val'])
        o = h_q @ theta['proj'] @ proj_w + proj_b
        return o.reshape(Bx, SNx, DIM)

    def _L0_attn_b_ref(x, g, b, w_qkv, w_out, b_out):
        import jax, jax.numpy as jnp
        import numpy as np
        DIM = 128
        HEADS = 16
        DIM_HEAD = 64
        NUM_FRAMES = 8
        PATCHES_PER_FRAME = 32
        BATCH = 2
        SEQ = NUM_FRAMES * PATCHES_PER_FRAME
        EPS = 1e-05

        def _block_causal_mask(seq_len: int) -> jnp.ndarray:
            frame = jnp.arange(seq_len) // PATCHES_PER_FRAME
            return frame[:, None] >= frame[None, :]
        mean = jnp.mean(x, axis=-1, keepdims=True)
        var = jnp.var(x, axis=-1, keepdims=True)
        xn = (x - mean) / jnp.sqrt(var + EPS) * g + b
        qkv = xn @ w_qkv
        q, k, v = jnp.split(qkv, 3, axis=-1)
        split_heads = lambda t: t.reshape(t.shape[0], t.shape[1], HEADS, DIM_HEAD).transpose(0, 2, 1, 3)
        q, k, v = (split_heads(q), split_heads(k), split_heads(v))
        scale = DIM_HEAD ** (-0.5)
        dots = jnp.einsum('bhqd,bhkd->bhqk', q, k) * scale
        mask = _block_causal_mask(x.shape[1])
        dots = jnp.where(mask[None, None], dots, -jnp.inf)
        attn = jax.nn.softmax(dots, axis=-1)
        out = jnp.einsum('bhqk,bhkd->bhqd', attn, v)
        out = out.transpose(0, 2, 1, 3).reshape(x.shape[0], x.shape[1], HEADS * DIM_HEAD)
        return out @ w_out + b_out

    def _L0_ffn_ref(x, We, be, Wg, bg):
        import jax, jax.numpy as jnp
        import numpy as np
        B, S, D = (4, 256, 128)
        O = 128
        E = 8
        K = 2
        b, s, d = x.shape
        x_flat = x.reshape(-1, d)
        gates = jax.nn.softmax(x_flat @ Wg + bg, axis=-1)
        topk_gates, topk_idx = jax.lax.top_k(gates, K)
        topk_gates = topk_gates / jnp.sum(topk_gates, axis=1, keepdims=True)
        expert_out = jnp.einsum('nd,edo->neo', x_flat, We) + be
        selected = jnp.take_along_axis(expert_out, topk_idx[:, :, None], axis=1)
        out = jnp.sum(selected * topk_gates[:, :, None], axis=1)
        return out.reshape(b, s, -1)
    x = L0_attn_a_x
    x = x + _L0_attn_a_ref(_layernorm(x, axis=-1), L0_attn_a_qkv_w, L0_attn_a_qkv_b, L0_attn_a_qn_scale, L0_attn_a_qn_bias, L0_attn_a_kn_scale, L0_attn_a_kn_bias, L0_attn_a_ttt_gate, L0_attn_a_ttt_val, L0_attn_a_ttt_proj, L0_attn_a_proj_w, L0_attn_a_proj_b)
    x = x + _L0_ffn_ref(_layernorm(x, axis=-1), L0_ffn_We, L0_ffn_be, L0_ffn_Wg, L0_ffn_bg)
    x = x + _L0_attn_b_ref(_layernorm(x, axis=-1), L0_attn_b_g, L0_attn_b_b, L0_attn_b_w_qkv, L0_attn_b_w_out, L0_attn_b_b_out)
    x = x + _L0_ffn_ref(_layernorm(x, axis=-1), L0_ffn_We, L0_ffn_be, L0_ffn_Wg, L0_ffn_bg)
    return x

_drawn_inputs = setup_inputs


def setup_inputs(seed=0):
    import zlib

    import numpy as np

    out = dict(_drawn_inputs(seed))
    spreads = {'L0_attn_a_qkv_b': (0.0, 0.1),
     'L0_attn_a_qn_scale': (1.0, 0.2),
     'L0_attn_a_qn_bias': (0.0, 0.1),
     'L0_attn_a_kn_scale': (1.0, 0.2),
     'L0_attn_a_kn_bias': (0.0, 0.1),
     'L0_attn_a_proj_b': (0.0, 0.1),
     'L0_attn_b_g': (1.0, 0.2),
     'L0_attn_b_b': (0.0, 0.1),
     'L0_attn_b_b_out': (0.0, 0.1)}
    factors = {}
    for name, (base, spread) in spreads.items():
        noise = np.random.default_rng([zlib.crc32(name.encode()), seed]).standard_normal(out[name].shape)
        drawn = base * np.exp(spread * noise) if base else spread * noise
        out[name] = jnp.asarray(drawn.astype(out[name].dtype))
    for name, factor in factors.items():
        out[name] = (out[name] * factor).astype(out[name].dtype)
    return out
```

```python
from contextlib import ExitStack

import concourse.bass as bass
from concourse import mybir

F32 = mybir.dt.float32
F32R = mybir.dt.float32r
BF16 = mybir.dt.bfloat16
ALU = mybir.AluOpType
ACT = mybir.ActivationFunctionType
AX = mybir.AxisListType

P = 128
BATCH, SEQ = 4, 512
TOK = BATCH * SEQ
NT = TOK // P
TPB = SEQ // P
QH, QD = 16, 8
HID = 4 * P
NC = HID // P
TTT_STEPS = 2
LR = 0.1
NS_A, NS_B, NS_C = 3.4445, -4.775, 2.0315
LOSS_SCALE = 2.0 / (TOK * P)
HEADS, DH = 16, 64
NP = HEADS // 2
FRAME = 32
NE = 8
LN_EPS = 1e-5
NEG = -1e30


class Tile:

    def __init__(self, i, j, base=0):
        self.i, self.j, self.base = i, j, base
        self.ring = j % 2

    def done(self, n=1, k=1):
        return self.i * (2 * k) + (self.j * k + n + self.base * k)

    def cols(self, width=P):
        return bass.ds(self.i * (2 * width) + self.j * width, width)

    def next(self, n=1):
        return Tile(self.i, self.j + n, self.base)


def each_tile(e, body, base=0):
    with e.Fori(0, NT // 2) as i:
        for j in range(2):
            body(Tile(i, j, base))


def pipeline(e, *stages):
    last = max(lag for lag, _ in stages)
    start = last + last % 2

    def turn(i, j, base):
        for lag, step in stages:
            if i is not None or 0 <= j - lag < NT:
                step(Tile(0 if i is None else i, j - lag, base))

    def run(base=0):
        for s in range(start):
            turn(None, s, base)
        with e.Fori(start // 2, NT // 2) as i:
            for j in range(2):
                turn(i, j, base)
        for s in range(NT, NT + last):
            turn(None, s, base)

    return run


class Slot:

    N = HEADS * TPB
    TURN = 2 * TPB

    def __init__(self, b, i, j):
        self.b, self.i, self.j = b, i, j
        self.u = j % TPB
        self.qt = TPB - 1 - self.u
        self.par = (j // TPB) % 2
        self.keys = (self.qt + 1) * P

    def done(self, n=1):
        return self.i * self.TURN + self.b * self.N + (self.j + n)

    def head_done(self, n=1, k=1):
        return self.i * (2 * k) + self.b * (HEADS * k) + ((self.j // TPB) * k + n)

    def head_cols(self):
        return bass.ds(self.i * (2 * DH) + (self.j // TPB) * DH, DH)


def slots(e, b, *stages):
    lags = [lag for lag, _ in stages]
    first = -(-max(lags) // Slot.TURN)
    last = (Slot.N + min(0, min(lags))) // Slot.TURN

    def at(i, s, whole):
        for lag, step in stages:
            if whole or 0 <= s - lag < Slot.N:
                step(Slot(b, i, s - lag))

    for s in range(min(0, min(lags)), first * Slot.TURN):
        at(0, s, False)
    with e.Fori(first, last) as i:
        for j in range(Slot.TURN):
            at(i, j, True)
    for s in range(last * Slot.TURN, Slot.N + max(lags)):
        at(0, s, False)


class Chain:

    def __init__(self, e, sem, start=0):
        self.e, self.sem, self.n = e, sem, start

    def __call__(self, ins):
        ins.then_inc(self.sem, 1)
        self.n += 1
        self.e.wait_ge(self.sem, self.n)
        return self.n


def mm3(e, out, ah, al, bh, bl, start=True, stop=True):
    e.matmul(out, ah, bh, start=start, stop=False)
    e.matmul(out, ah, bl, start=False, stop=False)
    return e.matmul(out, al, bh, start=False, stop=stop)


class Kernel:
    def __init__(self, nc, ctx, args, out):
        self.nc, self.ctx = nc, ctx
        self.a, self.out = args, out
        sb, ps = self.sb, self.ps
        self.x = sb("x", [P, NT, P])
        self.qkv = sb("qkv", [P, NT, 3 * P])
        self.qkT = sb("qkT", [P, 2, TOK])
        self.ident = sb("ident", [P, P])
        self.ones = sb("ones", [P, P])
        self.ssq = sb("ssq", [P, NT * 2 * QH])
        self.gv = sb("gv", [P, 2 * HID])
        self.gvh, self.gvl = sb("gvh", [P, 2 * HID], F32R), sb("gvl", [P, 2 * HID], F32R)
        self.proj, self.projT = sb("proj", [P, NC, P]), sb("projT", [P, HID])
        self.pTh, self.pTl = sb("pTh", [P, HID], F32R), sb("pTl", [P, HID], F32R)
        self.zeros = sb("zeros", [P, HID], BF16)
        self.mean = sb("mean", [P, NT])
        self.rstd = sb("rstd", [P, NT])
        self.stats = sb("stats", [P, NT, 6])
        self.lnw = sb("lnw", [P, 4, NT])
        self.gradient_sems()
        self.schulz_sems()

    def sb(self, name, shape, dt=F32):
        return self.ctx.enter_context(self.nc.sbuf_tensor(name, shape, dt))

    def ps(self, name, shape, dt=F32):
        return self.ctx.enter_context(self.nc.psum_tensor(name, shape, dt))

    def sem(self, name):
        return self.ctx.enter_context(self.nc.semaphore(name))

    def ln_vector(self, e, s_stat, s_var, s_root, s_ln, x_ready=None):
        x, st, w = self.x, self.stats, self.lnw

        def stat(t):
            if x_ready:
                x_ready(t)
            e.bn_stats(st[:, bass.ds(t.i * 2 + t.j, 1), :], x[:, bass.ds(t.i * 2 + t.j, 1), :]).then_inc(s_stat, 1)

        each_tile(e, stat)
        e.wait_ge(s_stat, NT)
        c = Chain(e, s_ln)
        c(e.tensor_tensor(w[:, 0, :], st[:, :, 1], st[:, :, 4], ALU.subtract))
        c(e.tensor_tensor(w[:, 1, :], w[:, 0, :], w[:, 0, :], ALU.mult))
        c(e.tensor_tensor(w[:, 2, :], st[:, :, 2], st[:, :, 5], ALU.add))
        c(e.scalar_tensor_tensor(w[:, 3, :], w[:, 1, :], P / 4.0, w[:, 2, :], ALU.mult, ALU.add))
        c(e.tensor_scalar(w[:, 3, :], w[:, 3, :], 1.0 / P, LN_EPS, ALU.mult, ALU.add))
        e.sem_inc(s_var, 1)
        c(e.tensor_tensor(w[:, 0, :], st[:, :, 1], st[:, :, 4], ALU.add))
        c(e.tensor_scalar(self.mean[:, :], w[:, 0, :], 0.5, None, ALU.mult))
        e.wait_ge(s_root, 1)
        c(e.reciprocal(self.rstd[:, :], w[:, 1, :]))
        return c.n

    def ln_scalar(self, e, s_var, s_root):
        e.wait_ge(s_var, 1)
        e.activation(self.lnw[:, 1, :], self.lnw[:, 3, :], ACT.Sqrt).then_inc(s_root, 1)

    def qkv_phase(self):
        nc, sem = self.nc, self.sem
        x, qkv, ident = self.x, self.qkv, self.ident
        s_x, s_w, s_cst = sem("p0_x"), sem("p0_w"), sem("p0_cst")
        s_stat, s_var, s_root, s_ln = sem("p0_stat"), sem("p0_var"), sem("p0_root"), sem("p0_ln")
        s_xn, s_xT, s_xTs, s_qkv, s_out, s_sq, s_ss = (
            sem("p0_" + n) for n in ("xn", "xT", "xTs", "qkv", "out", "sq", "ss"))
        with ExitStack() as c:
            sb = lambda n, s, d=F32: c.enter_context(nc.sbuf_tensor(n, s, d))
            ps = lambda n, s, d=F32: c.enter_context(nc.psum_tensor(n, s, d))
            w = sb("p0_w_", [P, 3 * P])
            bias = sb("p0_bias", [P, 3 * P])
            xn = sb("p0_xn_", [P, 2, P])
            xTs = sb("p0_xTs_", [P, 2, P])
            sq = sb("p0_sq_", [P, 2, 2 * P])
            psT = [ps(f"p0_T{r}", [P, P]) for r in range(2)]
            psQ = [ps(f"p0_Q{r}", [P, 3 * P]) for r in range(2)]
            block = c.enter_context(nc.Block())
            xsrc = self.a["L0_attn_a_x"].rearrange("b (t p) d -> p (b t) d", p=P)

            @block.sync
            def _(sp):
                for g in range(4):
                    sp.dma_start(x[:, 4 * g:4 * g + 4, :], xsrc[:, 4 * g:4 * g + 4, :]).then_inc(s_x, 16)
                sp.dma_start(w[:, :], self.a["L0_attn_a_qkv_w"]).then_inc(s_w, 16)
                sp.dma_start(bias[:, :], self.a["L0_attn_a_qkv_b"].rearrange("(a n) -> a n", a=1).broadcast_to([P, 3 * P])).then_inc(s_w, 16)
                sp.wait_ge(s_w, 32)

            @block.gpsimd
            def _(pool):
                pool.memset(self.ones[:, :], 1.0).then_inc(s_cst, 1)
                pool.memset(ident[:, :], 0.0).then_inc(s_cst, 1)
                pool.wait_ge(s_cst, 2)
                pool.affine_select(out=ident[:, :], in_=ident[:, :], compare_op=ALU.not_equal, fill=1.0, base=0,
                                   pattern=[[-1, P]], channel_multiplier=1).then_inc(s_cst, 1)

            @block.scalar
            def _(act):
                self.ln_scalar(act, s_var, s_root)

                def copy(t):
                    act.wait_ge(s_xT, t.done() + 2)
                    act.activation(xTs[:, t.ring, :], psT[t.ring][:, :], ACT.Copy).then_inc(s_xTs, 1)

                def square(t):
                    act.wait_ge(s_out, t.done() + 2)
                    act.activation(sq[:, t.ring, :], qkv[:, bass.ds(t.i * 2 + t.j, 1), 0:2 * P], ACT.Square).then_inc(s_sq, 1)

                pipeline(act, (0, copy), (2, square))()

            @block.tensor
            def _(pe):
                pe.wait_ge(s_cst, 3)

                def turn(t):
                    pe.wait_ge(s_xn, t.done())
                    pe.transpose(psT[t.ring][:, :], xn[:, t.ring, :], ident[:, :]).then_inc(s_xT, 1)

                def project(t):
                    pe.wait_ge(s_xTs, t.done())
                    pe.wait_ge(s_out, t.done())
                    pe.matmul(psQ[t.ring][:, :], xTs[:, t.ring, :], w[:, :], start=True, stop=True).then_inc(s_qkv, 1)

                pe.wait_ge(s_w, 32)
                pipeline(pe, (0, turn), (1, project))()

            @block.vector
            def _(dve):
                n = self.ln_vector(dve, s_stat, s_var, s_root, s_ln, lambda t: dve.wait_ge(s_x, 64))
                dve.sem_inc(s_xT, 2)
                dve.sem_inc(s_out, 2)
                dve.wait_ge(s_w, 32)

                def norm(t):
                    dve.wait_ge(s_xT, t.done())
                    tt = bass.ds(t.i * 2 + t.j, 1)
                    dve.tensor_scalar(xn[:, t.ring, :], x[:, tt, :].rearrange("p a d -> p (a d)"), self.mean[:, tt],
                                      self.rstd[:, tt], ALU.subtract, ALU.mult).then_inc(s_xn, 1)

                def bias_add(t):
                    dve.wait_ge(s_qkv, t.done())
                    dve.tensor_tensor(qkv[:, bass.ds(t.i * 2 + t.j, 1), :], psQ[t.ring][:, :], bias[:, :], ALU.add).then_inc(s_out, 1)

                def sumsq(t):
                    dve.wait_ge(s_sq, t.done())
                    dve.tensor_reduce(self.ssq[:, bass.ds(t.i * 64 + t.j * 32, 32)],
                                      sq[:, t.ring, :].rearrange("p (g d) -> p g d", d=QD), AX.X, ALU.add).then_inc(s_ss, 1)

                pipeline(dve, (0, norm), (2, bias_add), (3, sumsq))()
                dve.wait_ge(s_ss, NT)


    def unit_phase(self):
        nc, sem, qkv, qkT, ident = self.nc, self.sem, self.qkv, self.qkT, self.ident
        s_w, s_rt, s_inv, s_st = sem("p1_w"), sem("p1_rt"), sem("p1_inv"), sem("p1_st")
        s_m, s_s, s_b, s_T, s_e, s_k = (sem("p1_" + n) for n in ("m", "s", "b", "T", "e", "k"))
        s_gh, s_pt, s_ptc, s_pth = sem("p1_gh"), sem("p1_pt"), sem("p1_ptc"), sem("p1_pth")
        with ExitStack() as c:
            sb = lambda n, s, d=F32: c.enter_context(nc.sbuf_tensor(n, s, d))
            ps = lambda n, s, d=F32: c.enter_context(nc.psum_tensor(n, s, d))
            scale, bias = sb("p1_scale", [P, 2, QD]), sb("p1_bias", [P, 2, QD])
            scale_all, bias_all = sb("p1_scale_all", [P, 2 * P]), sb("p1_bias_all", [P, 2 * P])
            inv = sb("p1_inv_", [P, NT * 32])
            m, sc, u = sb("p1_m_", [P, 2, 2 * P]), sb("p1_s_", [P, 2, 2 * P]), sb("p1_u_", [P, 2, 2 * P])
            psT = [ps(f"p1_T{r}", [P, 2, P]) for r in range(2)]
            psP = ps("p1_P", [P, NC, P])
            block = c.enter_context(nc.Block())

            @block.sync
            def _(sp):
                for n, w in enumerate(("qn", "kn")):
                    for dst, what in ((scale, "scale"), (bias, "bias")):
                        sp.dma_start(dst[:, n, :], self.a[f"L0_attn_a_{w}_{what}"].rearrange("(a n) -> a n", a=1)
                                     .broadcast_to([P, QD])).then_inc(s_w, 16)
                sp.dma_start(self.gv[:, 0:HID], self.a["L0_attn_a_ttt_gate"]).then_inc(s_w, 16)
                sp.dma_start(self.gv[:, HID:2 * HID], self.a["L0_attn_a_ttt_val"]).then_inc(s_w, 16)
                sp.dma_start(self.proj[:, :, :], self.a["L0_attn_a_ttt_proj"].rearrange("(c p) d -> p c d", p=P)).then_inc(s_w, 16)

            @block.gpsimd
            def _(pool):
                pool.sem_inc(s_b, 2)

                def scaled(t):
                    pool.wait_ge(s_m, t.done())
                    pool.wait_ge(s_b, t.done())
                    pool.tensor_tensor(sc[:, t.ring, :], m[:, t.ring, :], scale_all[:, :], ALU.mult).then_inc(s_s, 1)

                pipeline(pool, (0, scaled))()

            @block.scalar
            def _(act):
                act.wait_ge(s_w, 7 * 16)
                act.activation(self.gvh[:, :], self.gv[:, :], ACT.Copy).then_inc(s_gh, 1)
                act.activation(self.ssq[:, :], self.ssq[:, :], ACT.Sqrt).then_inc(s_rt, 1)
                act.wait_ge(s_ptc, 1)
                act.activation(self.pTh[:, :], self.projT[:, :], ACT.Copy).then_inc(s_pth, 1)

                def copy(t):
                    act.wait_ge(s_T, t.done() + 2)
                    act.activation(qkT[:, :, t.cols()], psT[t.ring][:, :, :], ACT.Copy).then_inc(s_e, 1)

                def keep(t):
                    act.wait_ge(s_b, t.done() + 2)
                    act.activation(qkv[:, bass.ds(t.i * 2 + t.j, 1), P:2 * P], u[:, t.ring, P:2 * P], ACT.Copy).then_inc(s_k, 1)

                act.sem_inc(s_e, 2)
                act.sem_inc(s_k, 2)
                pipeline(act, (0, copy), (0, keep))()

            @block.tensor
            def _(pe):
                pe.wait_ge(s_w, 7 * 16)
                for n in range(NC):
                    last = pe.transpose(psP[:, n, :], self.proj[:, n, :], ident[:, :])
                last.then_inc(s_pt, 1)

                def turn(t):
                    pe.wait_ge(s_b, t.done() + 2)
                    pe.wait_ge(s_e, t.done())
                    pe.transpose(psT[t.ring][:, 0, :], u[:, t.ring, 0:P], ident[:, :])
                    pe.transpose(psT[t.ring][:, 1, :], u[:, t.ring, P:2 * P], ident[:, :]).then_inc(s_T, 1)

                pipeline(pe, (0, turn))()

            @block.vector
            def _(dve):
                c = Chain(dve, s_st)
                dve.wait_ge(s_w, 7 * 16)
                for dst, src in ((scale_all, scale), (bias_all, bias)):
                    for n in range(2):
                        c(dve.tensor_copy(dst[:, n * P:n * P + P].rearrange("p (g d) -> p g d", d=QD),
                                          src[:, n:n + 1, :].broadcast_to([P, QH, QD])))
                dve.wait_ge(s_gh, 1)
                c(dve.tensor_tensor(self.gvl[:, :], self.gv[:, :], self.gvh[:, :].bitcast(F32), ALU.subtract))
                dve.wait_ge(s_pt, 1)
                dve.tensor_copy(self.projT[:, :], psP[:, :, :].rearrange("p c d -> p (c d)")).then_inc(s_ptc, 1)
                dve.wait_ge(s_pth, 1)
                c(dve.tensor_tensor(self.pTl[:, :], self.projT[:, :], self.pTh[:, :].bitcast(F32), ALU.subtract))
                dve.wait_ge(s_rt, 1)
                c(dve.tensor_scalar(self.ssq[:, :], self.ssq[:, :], 1e-6, None, ALU.add))
                c(dve.reciprocal(inv[:, :], self.ssq[:, :]))
                dve.sem_inc(s_s, 2)

                def unit(t):
                    dve.wait_ge(s_s, t.done())
                    r = inv[:, bass.ds(t.i * 64 + t.j * 32, 32)]
                    dve.tensor_tensor(m[:, t.ring, :].rearrange("p (g d) -> p g d", d=QD),
                                      qkv[:, bass.ds(t.i * 2 + t.j, 1), 0:2 * P].rearrange("p a (g d) -> p (a g) d", d=QD),
                                      r.unsqueeze(2).broadcast_to([P, 32, QD]), ALU.mult).then_inc(s_m, 1)

                def shift(t):
                    dve.wait_ge(s_s, t.done() + 2)
                    dve.wait_ge(s_T, t.done())
                    dve.wait_ge(s_k, t.done())
                    dve.tensor_tensor(u[:, t.ring, :], sc[:, t.ring, :], bias_all[:, :], ALU.add).then_inc(s_b, 1)

                dve.sem_inc(s_T, 2)
                pipeline(dve, (0, unit), (2, shift))()

    def gradient_sems(self):
        names = "kh kl F sig u sw h t1 sp w1 HT hT PR d DT dTh dTl DH du dg G zero".split()
        self.g = {n: self.sem("g_" + n) for n in names}

    def gradient_phase(self, step):
        nc, qkv, qkT, g = self.nc, self.qkv, self.qkT, self.g
        base = step * NT
        with ExitStack() as c:
            sb = lambda n, s, d=F32: c.enter_context(nc.sbuf_tensor(f"g{step}_{n}", s, d))
            ps = lambda n, s, d=F32: c.enter_context(nc.psum_tensor(f"g{step}_{n}", s, d))
            kh, kl = sb("kh", [P, 2, P], F32R), sb("kl", [P, 2, P], F32R)
            s_, u_, sw, h, t1, sp_, w1, hT, du, dg = (sb(n, [P, 2, HID]) for n in
                                                      ("s", "u", "sw", "h", "t1", "sp", "w1", "hT", "du", "dg"))
            d = sb("d", [P, 2, P])
            dTh, dTl = sb("dTh", [P, 2, P], F32R), sb("dTl", [P, 2, P], F32R)
            psG, psU, psH, psD = (ps(n, [P, HID]) for n in ("G", "U", "H", "D"))
            psPT = ps("PT", [P, 4, P])
            pred, dTp = psPT[:, 0, :], psPT[:, 1, :]
            gvh, gvl = self.gvh, self.gvl
            block = c.enter_context(nc.Block())

            @block.gpsimd
            def _(pool):
                if step == 0:
                    pool.sem_inc(g["sp"], 2)
                    pool.sem_inc(g["w1"], 2)
                    pool.memset(self.zeros[:, :], 0.0).then_inc(g["zero"], 1)

                def k_low(t):
                    pool.wait_ge(g["kh"], t.done())
                    pool.tensor_tensor(kl[:, t.ring, :], qkT[:, 1, t.cols()], kh[:, t.ring, :].bitcast(F32),
                                       ALU.subtract).then_inc(g["kl"], 1)

                def slope(t):
                    pool.wait_ge(g["t1"], t.done())
                    pool.tensor_tensor(sp_[:, t.ring, :], s_[:, t.ring, :], t1[:, t.ring, :], ALU.subtract).then_inc(g["sp"], 1)

                def gate_factor(t):
                    pool.wait_ge(g["sp"], t.done() + 2)
                    pool.wait_ge(g["dg"], t.done(0))
                    pool.tensor_tensor(w1[:, t.ring, :], u_[:, t.ring, :], sp_[:, t.ring, :], ALU.mult).then_inc(g["w1"], 1)

                pipeline(pool, (0, k_low), (1, slope), (1, gate_factor))(base)

            @block.scalar
            def _(act):
                if step == 0:
                    act.sem_inc(g["u"], 1)
                    act.sem_inc(g["hT"], 1)
                act.preload_act_table(ACT.Sigmoid)

                def k_high(t):
                    act.wait_ge(g["F"], t.done(2, 2))
                    act.activation(kh[:, t.ring, :], qkT[:, 1, t.cols()], ACT.Copy).then_inc(g["kh"], 1)

                def sigmoid(t):
                    act.wait_ge(g["F"], t.done(1, 2) + 4)
                    act.wait_ge(g["sp"], t.done())
                    act.activation(s_[:, t.ring, :], psG[:, :], ACT.Sigmoid).then_inc(g["sig"], 1)

                def keep_u(t):
                    act.wait_ge(g["F"], t.done(2, 2) + 4)
                    act.wait_ge(g["w1"], t.done())
                    act.activation(u_[:, t.ring, :], psU[:, :], ACT.Copy).then_inc(g["u"], 1)

                def keep_hT(t):
                    act.wait_ge(g["HT"], t.done())
                    act.activation(hT[:, t.ring, :], psH[:, :], ACT.Copy).then_inc(g["hT"], 1)

                def dT_high(t):
                    act.wait_ge(g["DT"], t.done())
                    act.activation(dTh[:, t.ring, :], dTp, ACT.Copy).then_inc(g["dTh"], 1)

                pipeline(act, (2, keep_hT), (0, k_high), (1, sigmoid), (1, keep_u), (2, dT_high))(base)

            @block.tensor
            def _(pe):
                if step == 0:
                    pe.sem_inc(g["F"], 4)
                    pe.sem_inc(g["G"], 6)
                pe.wait_ge(g["zero"], 1)
                for n in range(3):
                    pe.matmul(self.acc[:, n, :, :].rearrange("p c d -> p (c d)"), self.zeros[:, 0:P], self.zeros[:, :],
                              start=True, stop=False, skip_group_check=True)

                def forward(t):
                    pe.wait_ge(g["kh"], t.done())
                    pe.wait_ge(g["kl"], t.done())
                    a, b = kh[:, t.ring, :], kl[:, t.ring, :]
                    pe.wait_ge(g["sw"], t.done())
                    mm3(pe, psG[:, :], a, b, gvh[:, 0:HID], gvl[:, 0:HID]).then_inc(g["F"], 1)
                    pe.wait_ge(g["u"], t.done())
                    mm3(pe, psU[:, :], a, b, gvh[:, HID:2 * HID], gvl[:, HID:2 * HID]).then_inc(g["F"], 1)

                def turn_h(t):
                    pe.wait_ge(g["h"], t.done())
                    pe.wait_ge(g["hT"], t.done())
                    for n in range(NC):
                        last = pe.transpose(psH[:, n * P:n * P + P], h[:, t.ring, n * P:n * P + P], self.ident[:, :])
                    last.then_inc(g["HT"], 1)

                def predict(t):
                    pe.wait_ge(g["hT"], t.done() + 1)
                    pe.wait_ge(g["dTl"], t.done())
                    for n in range(NC):
                        last = pe.matmul(pred, hT[:, t.ring, n * P:n * P + P], self.proj[:, n, :],
                                         start=(n == 0), stop=(n == NC - 1))
                    last.then_inc(g["PR"], 1)

                def turn_d(t):
                    pe.wait_ge(g["d"], t.done())
                    pe.transpose(dTp, d[:, t.ring, :], self.ident[:, :]).then_inc(g["DT"], 1)

                def back(t):
                    pe.wait_ge(g["dTh"], t.done())
                    pe.wait_ge(g["dTl"], t.done() + 1)
                    pe.wait_ge(g["dg"], t.done())
                    mm3(pe, psD[:, :], dTh[:, t.ring, :], dTl[:, t.ring, :], self.pTh[:, :], self.pTl[:, :]).then_inc(g["DH"], 1)

                def add(n, src, ready):
                    def step_(t):
                        pe.wait_ge(*ready(t))
                        k = qkv[:, bass.ds(t.i * 2 + t.j, 1), P:2 * P]
                        for m in range(NC):
                            last = pe.matmul(self.acc[:, n, m, :], src[:, t.ring, m * P:m * P + P],
                                             d[:, t.ring, :] if n == 2 else k, start=False, stop=False, skip_group_check=True)
                        last.then_inc(g["G"], 1)
                    return step_

                add_proj = add(2, h, lambda t: (g["d"], t.done()))
                add_val = add(1, du, lambda t: (g["du"], t.done() + 2))
                add_gate = add(0, dg, lambda t: (g["dg"], t.done() + 1))
                pipeline(pe, (2, turn_h), (3, add_proj), (1, forward), (2, predict), (3, add_val), (2, turn_d),
                         (3, add_gate), (2, back))(base)

            @block.vector
            def _(dve):
                if step == 0:
                    for n in ("sw", "dTl", "dg"):
                        dve.sem_inc(g[n], 1)
                    dve.sem_inc(g["du"], 2)

                def swish(t):
                    dve.wait_ge(g["sig"], t.done())
                    dve.wait_ge(g["du"], t.done())
                    dve.tensor_tensor(sw[:, t.ring, :], psG[:, :], s_[:, t.ring, :], ALU.mult).then_inc(g["sw"], 1)

                def hidden(t):
                    dve.wait_ge(g["u"], t.done() + 1)
                    dve.wait_ge(g["sw"], t.done() + 1)
                    dve.wait_ge(g["G"], t.done(1, 3))
                    dve.tensor_tensor(h[:, t.ring, :], sw[:, t.ring, :], u_[:, t.ring, :], ALU.mult).then_inc(g["h"], 1)

                def fall(t):
                    dve.scalar_tensor_tensor(t1[:, t.ring, :], s_[:, t.ring, :], 1.0, sw[:, t.ring, :],
                                             ALU.subtract, ALU.mult).then_inc(g["t1"], 1)

                def error(t):
                    dve.wait_ge(g["PR"], t.done())
                    dve.tensor_tensor(d[:, t.ring, :], pred, qkv[:, bass.ds(t.i * 2 + t.j, 1), 2 * P:3 * P],
                                      ALU.subtract).then_inc(g["d"], 1)

                def dT_low(t):
                    dve.wait_ge(g["dTh"], t.done())
                    dve.tensor_tensor(dTl[:, t.ring, :], dTp, dTh[:, t.ring, :].bitcast(F32), ALU.subtract).then_inc(g["dTl"], 1)

                def grad_val(t):
                    dve.wait_ge(g["DH"], t.done())
                    dve.tensor_tensor(du[:, t.ring, :], psD[:, :], sw[:, t.ring, :], ALU.mult).then_inc(g["du"], 1)

                def grad_gate(t):
                    dve.wait_ge(g["w1"], t.done() + 2)
                    dve.tensor_tensor(dg[:, t.ring, :], psD[:, :], w1[:, t.ring, :], ALU.mult).then_inc(g["dg"], 1)

                pipeline(dve, (1, swish), (2, error), (1, hidden), (1, fall), (2, dT_low), (2, grad_val), (2, grad_gate))(base)


    USED = ("xt", "x", "scaled", "p0", "t0", "a1", "p1", "q1", "xt2", "x2", "a2",
            "p2", "t2", "a3", "p3", "t3", "a4", "p4", "q4", "new", "newT")

    def schulz_sems(self):
        self.used = [self.sem(f"ns_used{m}") for m in range(3)]
        self.made = [self.sem(f"ns_made{m}") for m in range(3)]
        self.s_trace, self.s_norm, self.s_root, self.s_rate, self.s_nsv = (
            self.sem("ns_" + n) for n in ("trace", "norm", "root", "rate", "v"))
        self.s_gh, self.s_ph, self.s_lo = self.sem("ns_gh"), self.sem("ns_ph"), self.sem("ns_lo")

    def schulz_phase(self, step):
        nc, acc, ident = self.nc, self.acc, self.ident
        used, made = self.used, self.made

        def after(m, name):
            names = self.USED[:len(self.USED) - (m < 2)]
            return step * len(names) + names.index(name) + 1

        def result(m, name):
            names = [n for n in self.USED[:len(self.USED) - (m < 2)] if n not in ("xt", "scaled")]
            return step * len(names) + names.index(name) + 1

        with ExitStack() as c:
            sb = lambda n, s, d=F32: c.enter_context(nc.sbuf_tensor(f"n{step}_{n}", s, d))
            XT, X, XT2, X2 = (sb(n, [P, 3, NC, P]) for n in ("XT", "X", "XT2", "X2"))
            A, T1, T, Q = (sb(n, [P, 3, P]) for n in ("A", "T1", "T", "Q"))
            Pm = sb("P", [P, 2, 3, P])
            aI, junk = sb("aI", [P, P]), sb("junk", [P, P])
            tr, nrm, r, r2, rate = (sb(n, [P, 3]) for n in ("tr", "nrm", "r", "r2", "rate"))
            small = [c.enter_context(nc.psum_tensor(f"n{step}_small{m}", [P, 4, P], F32)) for m in range(3)]
            big = [acc[:, m, :, :] for m in range(3)]
            flat = lambda ap: ap.rearrange("p c d -> p (c d)")
            block = c.enter_context(nc.Block())

            @block.tensor
            def _(pe):
                def gram(m, src, name):
                    for n in range(NC):
                        last = pe.matmul(small[m][:, 0, :], src[:, m, n, :], src[:, m, n, :], start=(n == 0), stop=(n == NC - 1))
                    return last

                def square(k):
                    for m in range(3):
                        pe.wait_ge(used[m], after(m, f"a{k}" if k else "scaled"))
                        pe.matmul(small[m][:, 1, :], A[:, m, :], A[:, m, :], start=True, stop=True).then_inc(made[m], 1)

                def times_a(k, with_q=False):
                    for m in range(3):
                        pe.wait_ge(used[m], after(m, f"p{k}"))
                        if with_q:
                            pe.matmul(small[m][:, 3, :], Pm[:, k % 2, m, :], Pm[:, 1 - k % 2, m, :], start=True, stop=True)
                        pe.matmul(small[m][:, 2, :], Pm[:, k % 2, m, :], A[:, m, :], start=True, stop=True).then_inc(made[m], 1)

                def next_a(k):
                    for m in range(3):
                        pe.wait_ge(used[m], after(m, f"t{k}"))
                        pe.matmul(small[m][:, 0, :], Pm[:, k % 2, m, :], T[:, m, :], start=True, stop=True).then_inc(made[m], 1)

                def last_q(k, before):
                    for m in range(3):
                        pe.wait_ge(used[m], after(m, f"p{k}"))
                        pe.matmul(small[m][:, 3, :], Pm[:, k % 2, m, :], before(m), start=True, stop=True).then_inc(made[m], 1)

                for m in range(3):
                    pe.wait_ge(used[m], after(m, "xt"))
                    gram(m, XT, "trace").then_inc(self.s_norm, 1)
                for m in range(3):
                    for n in range(NC):
                        last = pe.transpose(big[m][:, n, :], XT[:, m, n, :], ident[:, :])
                    last.then_inc(made[m], 1)
                pe.wait_ge(self.s_trace, 3 * step + 3)
                pe.matmul(small[0][:, 3, 0:3], self.ones[:, :], tr[:, :], start=True, stop=True).then_inc(self.s_norm, 1)
                square(0)
                times_a(0)
                next_a(0)
                square(1)
                last_q(1, lambda m: Pm[:, 0, m, :])
                for m in range(3):
                    pe.wait_ge(used[m], after(m, "q1"))
                    for n in range(NC):
                        last = pe.matmul(big[m][:, n, :], X[:, m, n, :], Q[:, m, :], start=True, stop=True)
                    last.then_inc(made[m], 1)
                for m in range(3):
                    pe.wait_ge(used[m], after(m, "xt2"))
                    pe.matmul(flat(big[m]), Q[:, m, :], flat(X[:, m, :, :]), start=True, stop=True).then_inc(made[m], 1)
                for m in range(3):
                    pe.wait_ge(used[m], after(m, "x2"))
                    gram(m, XT2, "a2").then_inc(made[m], 1)
                square(2)
                times_a(2)
                next_a(2)
                square(3)
                times_a(3, True)
                next_a(3)
                square(4)
                last_q(4, lambda m: Q[:, m, :])
                for m in range(3):
                    pe.wait_ge(used[m], after(m, "q4"))
                    pe.matmul(flat(big[m]), Q[:, m, :], flat(X2[:, m, :, :]), start=True, stop=True).then_inc(made[m], 1)
                pe.wait_ge(used[2], after(2, "new"))
                for n in range(NC):
                    last = pe.matmul(big[2][:, n, :], X2[:, 2, n, :], Q[:, 2, :], start=True, stop=True)
                last.then_inc(made[2], 1)

            @block.scalar
            def _(act):
                def copy(m, dst, src, name):
                    if name != "xt":
                        act.wait_ge(made[m], result(m, name))
                    act.activation(dst, src, ACT.Copy).then_inc(used[m], 1)

                for m in (0, 2):
                    copy(m, flat(XT[:, m, :, :]), flat(big[m]), "xt")
                for m in range(3):
                    copy(m, flat(X[:, m, :, :]), flat(big[m]), "x")
                act.wait_ge(self.s_norm, 4 * step + 4)
                act.activation(nrm[:, :], small[0][:, 3, 0:3], ACT.Sqrt).then_inc(self.s_root, 1)

                def small_copy(dst, slot, name):
                    for m in range(3):
                        copy(m, dst[:, m, :], small[m][:, slot, :], name)

                small_copy(T, 2, "t0")
                small_copy(Q, 3, "q1")
                for name, dst in (("xt2", XT2), ("x2", X2)):
                    for m in range(3):
                        copy(m, flat(dst[:, m, :, :]), flat(big[m]), name)
                small_copy(T, 2, "t2")
                for m in range(3):
                    act.wait_ge(made[m], result(m, "t3"))
                    act.activation(Q[:, m, :], small[m][:, 3, :], ACT.Copy)
                    act.activation(T[:, m, :], small[m][:, 2, :], ACT.Copy).then_inc(used[m], 1)
                small_copy(Q, 3, "q4")
                for m in range(2):
                    act.wait_ge(used[m], after(m, "new"))
                    half = slice(m * HID, (m + 1) * HID)
                    act.activation(self.gvh[:, half], self.gv[:, half], ACT.Copy).then_inc(self.s_gh, 1)
                act.wait_ge(used[2], after(2, "new"))
                act.activation(self.pTh[:, :], self.projT[:, :], ACT.Copy).then_inc(self.s_ph, 1)

            @block.vector
            def _(dve):
                dve.tensor_copy(flat(XT[:, 1, :, :]), flat(big[1])).then_inc(used[1], 1)
                dve.tensor_scalar(aI[:, :], ident[:, :], NS_A, None, ALU.mult).then_inc(self.s_nsv, 1)
                for m in range(3):
                    dve.wait_ge(self.s_norm, 4 * step + m + 1)
                    if m:
                        dve.wait_ge(self.s_trace, 3 * step + m)
                    dve.tensor_tensor_reduce(junk[:, :], small[m][:, 0, :], ident[:, :], 1.0, 0.0, ALU.mult, ALU.add,
                                             tr[:, m:m + 1]).then_inc(self.s_trace, 1)
                dve.wait_ge(self.s_root, step + 1)
                c = Chain(dve, self.s_nsv, 4 * step + 1)
                c(dve.tensor_scalar(nrm[:, :], nrm[:, :], 1e-7 / LOSS_SCALE, None, ALU.add))
                c(dve.reciprocal(r[:, :], nrm[:, :]))
                dve.tensor_scalar(rate[:, :], r[:, :], -LR, None, ALU.mult).then_inc(self.s_rate, 1)
                c(dve.tensor_tensor(r2[:, :], r[:, :], r[:, :], ALU.mult))

                def scaled(m, name):
                    dve.wait_ge(made[m], result(m, name))
                    dve.tensor_scalar(A[:, m, :], small[m][:, 0, :], r2[:, m:m + 1], None, ALU.mult).then_inc(self.s_rate, 1)

                def mixed(m):
                    dve.scalar_tensor_tensor(T1[:, m, :], A[:, m, :], NS_B, aI[:, :], ALU.mult, ALU.add).then_inc(used[m], 1)

                def scale_all(name, done):
                    for m in range(3):
                        scaled(m, name)
                    for m in range(3):
                        dve.wait_ge(self.s_rate, 7 * step + 1 + done + m + 1)
                        mixed(m)

                def poly(k):
                    for m in range(3):
                        dve.wait_ge(made[m], result(m, f"p{k}"))
                        dve.scalar_tensor_tensor(Pm[:, k % 2, m, :], small[m][:, 1, :], NS_C, T1[:, m, :],
                                                 ALU.mult, ALU.add).then_inc(used[m], 1)

                def next_a(k):
                    for m in range(3):
                        dve.wait_ge(made[m], result(m, f"a{k}"))
                        dve.scalar_tensor_tensor(T1[:, m, :], small[m][:, 0, :], NS_B, aI[:, :], ALU.mult, ALU.add)
                        dve.tensor_copy(A[:, m, :], small[m][:, 0, :]).then_inc(used[m], 1)

                for m in range(3):
                    dve.wait_ge(used[m], after(m, "x"))
                scale_all("x", 0)
                poly(0)
                next_a(1)
                poly(1)
                scale_all("a2", 3)
                poly(2)
                next_a(3)
                poly(3)
                next_a(4)
                poly(4)
                for m in range(3):
                    dve.wait_ge(made[m], result(m, "new"))
                    dst = self.gv[:, m * HID:(m + 1) * HID] if m < 2 else self.projT[:, :]
                    dve.scalar_tensor_tensor(dst, flat(big[m]), rate[:, m:m + 1], dst, ALU.mult, ALU.add).then_inc(used[m], 1)
                dve.wait_ge(made[2], result(2, "newT"))
                dve.scalar_tensor_tensor(flat(self.proj[:, :, :]), flat(big[2]), rate[:, 2:3], flat(self.proj[:, :, :]),
                                         ALU.mult, ALU.add).then_inc(used[2], 1)
                for m in range(2):
                    half = slice(m * HID, (m + 1) * HID)
                    dve.wait_ge(self.s_gh, 2 * step + m + 1)
                    dve.tensor_tensor(self.gvl[:, half], self.gv[:, half], self.gvh[:, half].bitcast(F32), ALU.subtract).then_inc(self.s_lo, 1)
                dve.wait_ge(self.s_ph, step + 1)
                dve.tensor_tensor(self.pTl[:, :], self.projT[:, :], self.pTh[:, :].bitcast(F32), ALU.subtract).then_inc(self.s_lo, 1)


    def query_phase(self):
        nc, sem, x, qkT = self.nc, self.sem, self.x, self.qkT
        names = "w pw pwc qh ql gu sig sw h o xb x".split()
        q = {n: sem("q_" + n) for n in names}
        with ExitStack() as c:
            sb = lambda n, s, d=F32: c.enter_context(nc.sbuf_tensor("q_" + n + "_", s, d))
            ps = lambda n, s, d=F32: c.enter_context(nc.psum_tensor("q_" + n + "_", s, d))
            w, pb, pw = sb("w", [P, P]), sb("pb", [P, 1, P]), sb("pw", [P, NC, P])
            qh, ql = sb("qh", [P, SEQ], F32R), sb("ql", [P, SEQ], F32R)
            sg, sw, hT = sb("sg", [P, 2, SEQ]), sb("sw", [P, 2, SEQ]), sb("hT", [P, NC, SEQ])
            psG, psU = ps("G", [P, 2, SEQ]), ps("U", [P, 2, SEQ])
            psO, psW = ps("O", [P, TPB, P]), ps("W", [P, NC, P])
            block = c.enter_context(nc.Block())

            def batches(e, body):
                with e.Fori(0, BATCH) as b:
                    body(b)

            def rows(b):
                return x[:, bass.ds(b * TPB, TPB), :]

            @block.sync
            def _(sp):
                sp.dma_start(w[:, :], self.a["L0_attn_a_proj_w"]).then_inc(q["w"], 16)
                sp.dma_start(pb[:, 0, :], self.a["L0_attn_a_proj_b"].rearrange("(a n) -> a n", a=1)
                             .broadcast_to([P, P])).then_inc(q["w"], 16)

            @block.gpsimd
            def _(pool):
                pool.wait_ge(q["w"], 32)

                def add_bias(b):
                    pool.tensor_tensor(rows(b), rows(b), pb[:, :, :].broadcast_to([P, TPB, P]), ALU.add).then_inc(q["xb"], 1)

                batches(pool, add_bias)

            @block.scalar
            def _(act):
                act.preload_act_table(ACT.Sigmoid)
                act.wait_ge(q["pw"], 1)
                act.activation(pw[:, :, :], psW[:, :, :], ACT.Copy).then_inc(q["pwc"], 1)
                act.sem_inc(q["gu"], 4)

                def body(b):
                    act.wait_ge(q["gu"], b * 4 + 4)
                    act.activation(qh[:, :], qkT[:, 0, bass.ds(b * SEQ, SEQ)], ACT.Copy).then_inc(q["qh"], 1)
                    for n in range(NC):
                        act.wait_ge(q["gu"], b * 4 + n + 5)
                        act.wait_ge(q["sw"], b * 4 + n + 1)
                        act.activation(sg[:, n % 2, :], psG[:, n % 2, :], ACT.Sigmoid).then_inc(q["sig"], 1)

                batches(act, body)

            @block.tensor
            def _(pe):
                pe.wait_ge(q["w"], 32)
                for n in range(NC):
                    last = pe.matmul(psW[:, n, :], self.projT[:, n * P:n * P + P], w[:, :], start=True, stop=True)
                last.then_inc(q["pw"], 1)
                pe.wait_ge(q["pwc"], 1)

                def gate_up(b, n):
                    pe.wait_ge(q["h"], b * 4 + n + 1)
                    for half, ps_ in ((0, psG), (1, psU)):
                        cols = slice(half * HID + n * P, half * HID + n * P + P)
                        last = mm3(pe, ps_[:, n % 2, :], self.gvh[:, cols], self.gvl[:, cols], qh[:, :], ql[:, :])
                    last.then_inc(q["gu"], 1)

                def output(b):
                    pe.wait_ge(q["h"], b * 4 + 4 + 2)
                    pe.wait_ge(q["x"], b + 1)
                    for t in range(TPB):
                        for n in range(NC):
                            last = pe.matmul(psO[:, t, :], hT[:, n, t * P:t * P + P], pw[:, n, :],
                                             start=(n == 0), stop=(n == NC - 1))
                    last.then_inc(q["o"], 1)

                def body(b, before):
                    pe.wait_ge(q["ql"], b + 1)
                    gate_up(b, 0)
                    if before:
                        output(b - 1)
                    for n in range(1, NC):
                        gate_up(b, n)

                body(0, False)
                with pe.Fori(1, BATCH) as b:
                    body(b, True)
                output(BATCH - 1)

            @block.vector
            def _(dve):
                dve.sem_inc(q["sw"], 2)
                dve.sem_inc(q["h"], 2)
                dve.sem_inc(q["x"], 1)
                dve.sem_inc(q["o"], 1)

                def low(b):
                    dve.wait_ge(q["qh"], b + 1)
                    dve.tensor_tensor(ql[:, :], qkT[:, 0, bass.ds(b * SEQ, SEQ)], qh[:, :].bitcast(F32), ALU.subtract).then_inc(q["ql"], 1)

                def chunks(b):
                    for n in range(NC):
                        dve.wait_ge(q["sig"], b * 4 + n + 1)
                        dve.wait_ge(q["h"], b * 4 + n + 1)
                        dve.tensor_tensor(sw[:, n % 2, :], psG[:, n % 2, :], sg[:, n % 2, :], ALU.mult).then_inc(q["sw"], 1)
                        dve.wait_ge(q["sw"], b * 4 + n + 3)
                        if n == 0:
                            dve.wait_ge(q["o"], b + 1)
                        dve.tensor_tensor(hT[:, n, :], psU[:, n % 2, :], sw[:, n % 2, :], ALU.mult).then_inc(q["h"], 1)

                def add(b):
                    dve.wait_ge(q["o"], b + 2)
                    dve.wait_ge(q["xb"], b + 1)
                    dve.tensor_tensor(rows(b), rows(b), psO[:, :, :], ALU.add).then_inc(q["x"], 1)

                low(0)
                chunks(0)
                with dve.Fori(1, BATCH) as b:
                    low(b)
                    chunks(b)
                    add(b - 1)
                add(BATCH - 1)


    def moe_phase(self, nth):
        nc, x, ident = self.nc, self.x, self.ident
        own = []

        def sem(n):
            own.append(nc.alloc_semaphore(f"m{nth}_{n}"))
            return own[-1]

        s_stat, s_var, s_root, s_ln, s_load = sem("stat"), sem("var"), sem("root"), sem("ln"), sem("load")
        s_xn, s_xT, s_xTs, s_keep, s_L, s_l = (sem(n) for n in ("xn", "xT", "xTs", "keep", "L", "l"))
        s_sh, s_e, s_c, s_wT, s_wTs, s_B, s_xb = (sem(n) for n in ("sh", "e", "c", "wT", "wTs", "B", "xb"))
        s_hi, s_lo, s_E, s_y, s_z, s_z2, s_z3, s_x, s_out = (sem(n) for n in ("hi", "lo", "E", "y", "z", "z2", "z3", "x", "out"))
        s_prio, s_split, s_we, s_be = sem("prio"), sem("split"), sem("we"), sem("be")
        with ExitStack() as c:
            sb = lambda n, s, d=F32: c.enter_context(nc.sbuf_tensor(f"m{nth}_{n}_", s, d))
            ps = lambda n, s, d=F32: c.enter_context(nc.psum_tensor(f"m{nth}_{n}_", s, d))
            we = sb("we", [P, NE * P])
            weh, wel = sb("weh", [P, NE * P], F32R), sb("wel", [P, NE * P], F32R)
            wg, bg, be = sb("wg", [P, NE]), sb("bg", [P, 1, NE]), sb("be", [P, NT, P])
            xn, xTs, xnT = sb("xn", [P, 2, P]), sb("xTs", [P, 2, P]), sb("xnT", [P, TOK])
            prio, logit, gate, gate2, eq, sel, sel2, wt = (sb(n, [P, NT, NE]) for n in
                                                           ("prio", "logit", "gate", "gate2", "eq", "sel", "sel2", "wt"))
            m1, m2, pm, tot, rtot = (sb(n, [P, NT]) for n in ("m1", "m2", "pm", "tot", "rtot"))
            wT = sb("wT", [P, P])
            xh, xl = sb("xh", [P, 2, P], F32R), sb("xl", [P, 2, P], F32R)
            y, z, z2, z3 = sb("y", [P, 2, NE * P]), sb("z", [P, 2, 4 * P]), sb("z2", [P, 2, 2 * P]), sb("z3", [P, 2, P])
            psT, psL = ps("T", [P, 2, 512]), ps("L", [P, 2, 512])
            psE = ps("E", [P, 2, NE * P])
            block = c.enter_context(nc.Block())
            tile = lambda t: bass.ds(t.i * 2 + t.j, 1)

            @block.sync
            def _(sp):
                sp.dma_start(we[:, :].rearrange("d (e o) -> d e o", e=NE), self.a["L0_ffn_We"].rearrange("e d o -> d e o")).then_inc(s_we, 16)
                sp.dma_start(wg[:, :], self.a["L0_ffn_Wg"]).then_inc(s_load, 16)
                sp.dma_start(bg[:, 0, :], self.a["L0_ffn_bg"].rearrange("(a n) -> a n", a=1).broadcast_to([P, NE])).then_inc(s_load, 16)
                sp.wait_ge(s_prio, 1)
                for t in range(NT):
                    sp.dma_start(be[t * NE:(t + 1) * NE, t, :], self.a["L0_ffn_be"]).then_inc(s_be, 16)
                if nth == 1:
                    dst = self.out.rearrange("b (t p) d -> p (b t) d", p=P)
                    for g in range(BATCH):
                        sp.wait_ge(s_x, (g + 1) * TPB + 2)
                        sp.dma_start(dst[:, g * TPB:(g + 1) * TPB, :], x[:, g * TPB:(g + 1) * TPB, :]).then_inc(s_out, 16)
                    sp.wait_ge(s_out, 16 * BATCH)

            @block.gpsimd
            def _(pool):
                pool.memset(be[:, :, :], 0.0).then_inc(s_prio, 1)
                for n in range(NE):
                    last = pool.memset(prio[:, :, n:n + 1], float(NE - n))
                last.then_inc(s_prio, 1)
                pool.sem_inc(s_keep, 2)

                def keep(t):
                    pool.wait_ge(s_xTs, t.done())
                    pool.tensor_tensor(xnT[:, t.cols()], xTs[:, t.ring, :], self.ones[:, :], ALU.mult).then_inc(s_keep, 1)

                pipeline(pool, (0, keep))()

                def low(t):
                    pool.wait_ge(s_hi, t.done())
                    pool.tensor_tensor(xl[:, t.ring, :], xnT[:, t.cols()], xh[:, t.ring, :].bitcast(F32), ALU.subtract).then_inc(s_lo, 1)

                def add_half(t):
                    pool.wait_ge(s_y, t.done() + 2)
                    pool.wait_ge(s_z2, t.done())
                    pool.tensor_tensor(z[:, t.ring, :], y[:, t.ring, 0:4 * P], y[:, t.ring, 4 * P:8 * P], ALU.add).then_inc(s_z, 1)

                pool.sem_inc(s_z, 2)
                pipeline(pool, (0, low), (2, add_half))()

            @block.scalar
            def _(act):
                act.wait_ge(s_we, 16)
                act.activation(weh[:, :], we[:, :], ACT.Copy).then_inc(s_split, 1)
                self.ln_scalar(act, s_var, s_root)

                def copy(t):
                    act.wait_ge(s_xT, t.done() + 2)
                    act.wait_ge(s_keep, t.done())
                    act.wait_ge(s_L, t.done())
                    act.activation(xTs[:, t.ring, :], psT[:, t.ring, 0:P], ACT.Copy).then_inc(s_xTs, 1)

                act.sem_inc(s_L, 2)
                pipeline(act, (0, copy))()
                act.wait_ge(s_sh, 1)
                act.activation(gate[:, :, :], logit[:, :, :], ACT.Exp).then_inc(s_e, 1)
                act.wait_ge(s_keep, NT + 2)

                def high(t):
                    act.wait_ge(s_E, t.done())
                    act.activation(xh[:, t.ring, :], xnT[:, t.cols()], ACT.Copy).then_inc(s_hi, 1)

                act.sem_inc(s_E, 2)
                act.wait_ge(s_wT, 1)
                act.activation(wT[:, :], psT[:, 0, 0:P], ACT.Copy).then_inc(s_wTs, 1)
                pipeline(act, (0, high))()

            @block.tensor
            def _(pe):
                pe.wait_ge(s_load, 32)

                def turn(t):
                    pe.wait_ge(s_xn, t.done())
                    if t.j > 1 or not isinstance(t.i, int):
                        pe.wait_ge(s_xTs, t.done(-1))
                    pe.transpose(psT[:, t.ring, 0:P], xn[:, t.ring, :], ident[:, :]).then_inc(s_xT, 1)

                def logits(t):
                    pe.wait_ge(s_xTs, t.done())
                    pe.wait_ge(s_l, t.done())
                    pe.matmul(psL[:, t.ring, 0:NE], xTs[:, t.ring, :], wg[:, :], start=True, stop=True).then_inc(s_L, 1)

                pipeline(pe, (0, turn), (1, logits))()
                pe.wait_ge(s_c, 1)
                pe.transpose(psT[:, 0, 0:P], wt[:, :, :].rearrange("p t e -> p (t e)"), ident[:, :]).then_inc(s_wT, 1)
                pe.wait_ge(s_wTs, 1)
                pe.wait_ge(s_be, 16 * NT)
                for n in range(NT // TPB):
                    last = pe.matmul(psE[:, n // 2, (n % 2) * 512:(n % 2) * 512 + 512], wT[:, :],
                                     be[:, n * TPB:(n + 1) * TPB, :].rearrange("p t d -> p (t d)"), start=True, stop=True)
                last.then_inc(s_B, 1)
                pe.wait_ge(s_split, 2)
                pe.wait_ge(s_xb, 1)

                def experts(t):
                    pe.wait_ge(s_lo, t.done())
                    pe.wait_ge(s_y, t.done())
                    for half in range(2):
                        cols = slice(half * 512, half * 512 + 512)
                        last = mm3(pe, psE[:, t.ring, cols], xh[:, t.ring, :], xl[:, t.ring, :], weh[:, cols], wel[:, cols])
                    last.then_inc(s_E, 1)

                pipeline(pe, (1, experts))()

            @block.vector
            def _(dve):
                dve.wait_ge(s_split, 1)
                dve.tensor_tensor(wel[:, :], we[:, :], weh[:, :].bitcast(F32), ALU.subtract).then_inc(s_split, 1)
                n = self.ln_vector(dve, s_stat, s_var, s_root, s_ln)
                dve.wait_ge(s_load, 32)
                dve.sem_inc(s_xT, 2)
                dve.sem_inc(s_l, 2)

                def norm(t):
                    dve.wait_ge(s_xT, t.done())
                    dve.tensor_scalar(xn[:, t.ring, :], x[:, tile(t), :].rearrange("p a d -> p (a d)"), self.mean[:, tile(t)],
                                      self.rstd[:, tile(t)], ALU.subtract, ALU.mult).then_inc(s_xn, 1)

                def bias(t):
                    dve.wait_ge(s_L, t.done() + 2)
                    dve.tensor_tensor(logit[:, tile(t), :], psL[:, t.ring, 0:NE], bg[:, :, :], ALU.add).then_inc(s_l, 1)

                pipeline(dve, (0, norm), (2, bias))()
                wide = lambda ap: ap[:, :].unsqueeze(2).broadcast_to([P, NT, NE])
                g = Chain(dve, s_ln, n)
                dve.wait_ge(s_l, NT + 2)
                g(dve.tensor_reduce(m1[:, :], logit[:, :, :], AX.X, ALU.max))
                dve.tensor_tensor(logit[:, :, :], logit[:, :, :], wide(m1), ALU.subtract).then_inc(s_sh, 1)
                dve.wait_ge(s_e, 1)
                g(dve.tensor_reduce(tot[:, :], gate[:, :, :], AX.X, ALU.add))
                g(dve.reciprocal(rtot[:, :], tot[:, :]))
                g(dve.tensor_tensor(gate[:, :, :], gate[:, :, :], wide(rtot), ALU.mult))
                dve.wait_ge(s_prio, 2)

                def best(m, src, chosen):
                    g(dve.tensor_reduce(m[:, :], src[:, :, :], AX.X, ALU.max))
                    g(dve.tensor_tensor(eq[:, :, :], src[:, :, :], wide(m), ALU.is_equal))
                    g(dve.tensor_tensor(eq[:, :, :], eq[:, :, :], prio[:, :, :], ALU.mult))
                    g(dve.tensor_reduce(pm[:, :], eq[:, :, :], AX.X, ALU.max))
                    g(dve.tensor_tensor(chosen[:, :, :], eq[:, :, :], wide(pm), ALU.is_equal))

                best(m1, gate, sel)
                g(dve.scalar_tensor_tensor(gate2[:, :, :], sel[:, :, :], -2.0, gate[:, :, :], ALU.mult, ALU.add))
                best(m2, gate2, sel2)
                g(dve.tensor_tensor(tot[:, :], m1[:, :], m2[:, :], ALU.add))
                g(dve.reciprocal(rtot[:, :], tot[:, :]))
                g(dve.tensor_tensor(sel[:, :, :], sel[:, :, :], sel2[:, :, :], ALU.add))
                g(dve.tensor_tensor(sel[:, :, :], sel[:, :, :], gate[:, :, :], ALU.mult))
                dve.tensor_tensor(wt[:, :, :], sel[:, :, :], wide(rtot), ALU.mult).then_inc(s_c, 1)
                dve.wait_ge(s_c, 1)
                dve.wait_ge(s_B, 1)
                dve.tensor_tensor(x[:, :, :].rearrange("p (a t) d -> p a (t d)", a=2), psE[:, :, :],
                                  x[:, :, :].rearrange("p (a t) d -> p a (t d)", a=2), ALU.add).then_inc(s_xb, 1)
                dve.wait_ge(s_xb, 1)
                dve.sem_inc(s_y, 2)
                dve.sem_inc(s_z2, 2)
                dve.sem_inc(s_z3, 2)
                dve.sem_inc(s_x, 2)

                def weigh(t):
                    dve.wait_ge(s_E, t.done() + 2)
                    dve.wait_ge(s_z, t.done())
                    dve.tensor_tensor(y[:, t.ring, :].rearrange("p (e o) -> p e o", e=NE),
                                      psE[:, t.ring, :].rearrange("p (e o) -> p e o", e=NE),
                                      wt[:, tile(t), :].rearrange("p a e -> p (a e)").unsqueeze(2).broadcast_to([P, NE, P]),
                                      ALU.mult).then_inc(s_y, 1)

                def add_quarter(t):
                    dve.wait_ge(s_z, t.done() + 2)
                    dve.wait_ge(s_z3, t.done())
                    dve.tensor_tensor(z2[:, t.ring, :], z[:, t.ring, 0:2 * P], z[:, t.ring, 2 * P:4 * P], ALU.add).then_inc(s_z2, 1)

                def add_eighth(t):
                    dve.wait_ge(s_z2, t.done() + 2)
                    dve.wait_ge(s_x, t.done())
                    dve.tensor_tensor(z3[:, t.ring, :], z2[:, t.ring, 0:P], z2[:, t.ring, P:2 * P], ALU.add).then_inc(s_z3, 1)

                def add_x(t):
                    dve.wait_ge(s_z3, t.done() + 2)
                    dve.tensor_tensor(x[:, tile(t), :], x[:, tile(t), :], z3[:, t.ring, :], ALU.add).then_inc(s_x, 1)

                pipeline(dve, (1, weigh), (2, add_quarter), (3, add_eighth), (4, add_x))()

        if nth == 0:
            nc.clear_and_free_semaphores(own)
            nc.all_engine_barrier()


    def attention_phase(self):
        nc, x, ident = self.nc, self.x, self.ident
        names = ("kk load stat var root ln scale vsplit cst xn xT xa xh xl V va vd wh wl pr qh kh ql kl S mx ex T ea ed PV nr "
                 "oT oTa oTd out res rs").split()
        t = {n: self.sem("t_" + n) for n in names}
        with ExitStack() as c:
            sb = lambda n, s, d=F32: c.enter_context(nc.sbuf_tensor("t_" + n + "_", s, d))
            ps = lambda n, s, d=F32: c.enter_context(nc.psum_tensor("t_" + n + "_", s, d))
            w = sb("w", [P, 3, HEADS, DH])
            wvh, wvl = sb("wvh", [P, HEADS * DH], F32R), sb("wvl", [P, HEADS * DH], F32R)
            wout, bout = sb("wout", [P, NP, P]), sb("bout", [P, 1, P])
            lng, lnb = sb("lng", [P, 1]), sb("lnb", [P, 1])
            mask, identb = sb("mask", [P, P], BF16), sb("identb", [P, P], BF16)
            xn, xT = sb("xn", [P, TPB, P]), sb("xT", [P, SEQ])
            xh, xl = sb("xh", [P, SEQ], F32R), sb("xl", [P, SEQ], F32R)
            v, o = sb("v", [P, TPB, HEADS * DH]), sb("o", [P, TPB, HEADS * DH])
            oT = sb("oT", [P, NP, SEQ])
            wh, wl = sb("wh", [P, 2, 2 * DH], F32R), sb("wl", [P, 2, 2 * DH], F32R)
            qs, ks, kl = sb("qs", [P, 2, SEQ], F32R), sb("ks", [P, 2, SEQ], F32R), sb("kl", [DH, 2, SEQ], F32R)
            pr, pT = sb("p", [P, 8, SEQ]), sb("pT", [P, 4, TPB, P])
            nmax, rsum, rinv = sb("nmax", [P, 2, TPB]), sb("rsum", [P, 2, TPB]), sb("rinv", [P, 2, TPB])
            psS, psT, psO, psP = ps("S", [P, 4, 512]), ps("T", [P, 2, 512]), ps("O", [P, 512]), ps("P", [P, 512])
            AHEAD = -6
            ON_ACT = (2, 3)
            block = c.enter_context(nc.Block())
            wv = w[:, 2, :, :].rearrange("p h d -> p (h d)")
            flat = lambda ap: ap.rearrange("p a d -> p (a d)")

            def batches(e, body):
                with e.Fori(0, BATCH) as b:
                    body(b)

            @block.sync
            def _(sp):
                sp.dma_start(w[:, :, :, :].rearrange("p a h d -> p (a h d)"), self.a["L0_attn_b_w_qkv"]).then_inc(t["load"], 16)
                sp.dma_start(wout[:, :, :], self.a["L0_attn_b_w_out"].rearrange("(n p) d -> p n d", p=P)).then_inc(t["load"], 16)
                sp.dma_start(bout[:, 0, :], self.a["L0_attn_b_b_out"].rearrange("(a n) -> a n", a=1).broadcast_to([P, P])).then_inc(t["load"], 16)
                sp.dma_start(lng[:, :], self.a["L0_attn_b_g"].rearrange("a b d -> d (a b)")).then_inc(t["load"], 16)
                sp.dma_start(lnb[:, :], self.a["L0_attn_b_b"].rearrange("a b d -> d (a b)")).then_inc(t["load"], 16)
                sp.wait_ge(t["load"], 80)

            @block.gpsimd
            def _(pool):
                g = Chain(pool, t["cst"])
                g(pool.memset(mask[:, :], 0.0))
                for n in range(P // FRAME - 1):
                    g(pool.memset(mask[n * FRAME:(n + 1) * FRAME, (n + 1) * FRAME:P], NEG))
                g(pool.tensor_copy(identb[:, :], ident[:, :]))
                pool.wait_ge(t["scale"], 1)
                pool.sem_inc(t["kk"], 1)

                def w_low(s):
                    if s.u == 0:
                        pool.wait_ge(t["wh"], s.head_done())
                        pool.wait_ge(t["kk"], s.head_done())
                        pool.tensor_tensor(wl[:, s.par, :].rearrange("p (a d) -> p a d", a=2),
                                           w[:, 0:2, :, :].rearrange("p a h d -> p a (h d)")[:, :, s.head_cols()],
                                           wh[:, s.par, :].bitcast(F32).rearrange("p (a d) -> p a d", a=2),
                                           ALU.subtract).then_inc(t["wl"], 1)

                def repeat_k(s):
                    if s.u == 2:
                        pool.wait_ge(t["kh"], s.head_done())
                        pool.wait_ge(t["wl"], s.head_done())
                        pool.tensor_tensor(ks[DH:P, s.par, :].rearrange("p (a d) -> p a d", d=P),
                                           ks[0:DH, s.par, :].bitcast(F32).rearrange("p (a d) -> p a d", d=P),
                                           self.ones[0:DH, :].unsqueeze(1).broadcast_to([DH, TPB, P]), ALU.mult).then_inc(t["kk"], 1)

                batches(pool, lambda b: slots(pool, b, (AHEAD, w_low), (AHEAD, repeat_k)))

            @block.scalar
            def _(act):
                self.ln_scalar(act, t["var"], t["root"])
                act.preload_act_table(ACT.Exp)
                act.wait_ge(t["load"], 80)
                act.activation(wvh[:, :], wv, ACT.Copy).then_inc(t["vsplit"], 1)
                act.wait_ge(t["scale"], 1)
                act.sem_inc(t["pr"], 2)

                def w_high(s):
                    if s.u == 0:
                        act.wait_ge(t["pr"], s.head_done())
                        act.activation(wh[:, s.par, :].rearrange("p (a d) -> p a d", a=2),
                                       w[:, 0:2, :, :].rearrange("p a h d -> p a (h d)")[:, :, s.head_cols()],
                                       ACT.Copy).then_inc(t["wh"], 1)

                def qk_high(s):
                    if s.u == 2:
                        act.wait_ge(t["pr"], s.head_done() + 2)
                        act.activation(qs[0:DH, s.par, :], psP[0:DH, :], ACT.Copy).then_inc(t["qh"], 1)
                        act.activation(ks[0:DH, s.par, :], psP[DH:P, :], ACT.Copy).then_inc(t["kh"], 1)

                def exps(s):
                    act.wait_ge(t["mx"], s.done())
                    if not isinstance(s.i, int) or s.j > 7:
                        act.wait_ge(t["T"], s.done(-7))
                        if s.u == 0:
                            act.wait_ge(t["rs"], s.head_done(-1))
                    act.activation(pr[:, s.j % 8, 0:s.keys], psS[:, s.j % 4, 0:s.keys], ACT.Exp,
                                   bias=nmax[:, s.par, s.qt:s.qt + 1],
                                   accum_out=rsum[:, s.par, s.qt:s.qt + 1]).then_inc(t["ex"], 1)

                def take_p(s):
                    if s.u in ON_ACT:
                        act.wait_ge(t["T"], s.done())
                        act.activation(flat(pT[:, s.j % 4, 0:s.qt + 1, :]), psT[:, s.j % 2, 0:s.keys], ACT.Copy).then_inc(t["ea"], 1)

                def body(b):
                    act.wait_ge(t["xT"], b + 1)
                    act.activation(xT[:, :], psP[:, :], ACT.Identity, bias=lnb[:, :], scale=lng[:, :]).then_inc(t["xa"], 1)
                    act.wait_ge(t["xa"], b + 1)
                    act.activation(xh[:, :], xT[:, :], ACT.Copy).then_inc(t["xh"], 1)
                    for n in (0, 2):
                        act.wait_ge(t["V"], b * 4 + n + 1)
                        act.activation(v[:, n, :].rearrange("p (a d) -> p a d", a=2), psS[:, 0:2, :], ACT.Copy).then_inc(t["va"], 1)
                    slots(act, b, (4, take_p), (1, exps), (AHEAD, w_high), (AHEAD, qk_high))
                    for n in range(0, NP, 2):
                        act.wait_ge(t["oT"], b * NP + n + 1)
                        act.activation(oT[:, n, :], psS[:, n % 4, :], ACT.Copy).then_inc(t["oTa"], 1)

                batches(act, body)

            @block.tensor
            def _(pe):
                pe.wait_ge(t["load"], 80)
                pe.wait_ge(t["cst"], P // FRAME + 1)
                pe.wait_ge(t["vsplit"], 2)

                def project(s):
                    if s.u == 1:
                        pe.wait_ge(t["wl"], s.head_done())
                        pe.wait_ge(t["kl"], s.head_done() + 1)
                        mm3(pe, psP[:, :], wh[:, s.par, :], wl[:, s.par, :], xh[:, :], xl[:, :]).then_inc(t["pr"], 1)

                def scores(s):
                    if s.u == 0:
                        pe.wait_ge(t["kl"], s.head_done() + 2)
                        pe.wait_ge(t["kk"], s.head_done() + 1)
                    pe.wait_ge(t["ex"], s.done())
                    rows = slice(s.qt * P, s.qt * P + P)
                    n = max(s.keys, 2 * P)
                    out = psS[:, s.j % 4, 0:n]
                    pe.matmul(out, qs[:, s.par, rows], ks[:, s.par, 0:n], start=True, stop=False)
                    pe.matmul(out, qs[0:DH, s.par, rows], kl[:, s.par, 0:n], start=False, stop=False)
                    pe.matmul(psS[:, s.j % 4, s.keys - P:s.keys], identb[:, :], mask[:, :], start=False, stop=True).then_inc(t["S"], 1)

                def p_out(s):
                    on_act = s.u in ON_ACT
                    return t["ea" if on_act else "ed"], s.head_done(s.u % 2 + 1, 2)

                def turn(s):
                    pe.wait_ge(t["ex"], s.done() + 4)
                    if not isinstance(s.i, int) or s.j > 1:
                        pe.wait_ge(*p_out(Slot(s.b, s.i, s.j - 2)))
                    for n in range(s.qt + 1):
                        last = pe.transpose(psT[:, s.j % 2, n * P:n * P + P], pr[:, s.j % 8, n * P:n * P + P], ident[:, :])
                    last.then_inc(t["T"], 1)

                def weigh(s):
                    pe.wait_ge(*p_out(s))
                    if s.u == 0:
                        pe.wait_ge(t["nr"], s.head_done())
                    for n in range(s.qt + 1):
                        last = pe.matmul(psO[:, s.qt * DH:s.qt * DH + DH], pT[:, s.j % 4, n, :], v[:, n, s.head_cols()],
                                         start=(n == 0), stop=(n == s.qt))
                    last.then_inc(t["PV"], 1)

                def body(b):
                    pe.wait_ge(t["xn"], b + 1)
                    for n in range(TPB):
                        last = pe.transpose(psP[:, n * P:n * P + P], xn[:, n, :], ident[:, :])
                    last.then_inc(t["xT"], 1)
                    pe.wait_ge(t["xl"], b + 1)
                    for n in range(TPB):
                        bank = (psS[:, 0:2, :], psT[:, :, :])[n % 2]
                        if n >= 2:
                            pe.wait_ge(t[("va", "vd")[n % 2]], b * 2 + 1)
                        for half in range(2):
                            cols = slice(half * 512, half * 512 + 512)
                            last = mm3(pe, bank[:, half, :], xh[:, n * P:n * P + P], xl[:, n * P:n * P + P], wvh[:, cols], wvl[:, cols])
                        last.then_inc(t["V"], 1)
                    pe.wait_ge(t["va"], b * 2 + 2)
                    pe.wait_ge(t["vd"], b * 2 + 2)
                    slots(pe, b, (0, scores), (3, turn), (5, weigh), (AHEAD, project))
                    pe.wait_ge(t["nr"], b * HEADS + HEADS + 1)
                    for n in range(NP):
                        if n >= 4:
                            pe.wait_ge(t[("oTa", "oTd")[n % 2]], b * 4 + n // 2 - 1)
                        for m in range(TPB):
                            last = pe.transpose(psS[:, n % 4, m * P:m * P + P], o[:, m, n * P:n * P + P], ident[:, :])
                        last.then_inc(t["oT"], 1)
                    pe.wait_ge(t["oTa"], b * 4 + 4)
                    pe.wait_ge(t["oTd"], b * 4 + 4)
                    for m in range(TPB):
                        for n in range(NP):
                            last = pe.matmul(psP[:, m * P:m * P + P], oT[:, n, m * P:m * P + P], wout[:, n, :],
                                             start=(n == 0), stop=(n == NP - 1))
                    last.then_inc(t["out"], 1)
                    pe.wait_ge(t["res"], b * 2 + 2)

                batches(pe, body)

            @block.vector
            def _(dve):
                n = self.ln_vector(dve, t["stat"], t["var"], t["root"], t["ln"])
                dve.wait_ge(t["load"], 80)
                dve.tensor_scalar(w[:, 0, :, :], w[:, 0, :, :], DH ** -0.5, None, ALU.mult).then_inc(t["scale"], 1)
                dve.wait_ge(t["vsplit"], 1)
                dve.tensor_tensor(wvl[:, :], wv, wvh[:, :].bitcast(F32), ALU.subtract).then_inc(t["vsplit"], 1)
                dve.sem_inc(t["kl"], 2)
                dve.sem_inc(t["ex"], 4)
                dve.sem_inc(t["nr"], 1)

                def q_low(s):
                    if s.u == 2:
                        dve.wait_ge(t["kh"], s.head_done())
                        dve.tensor_tensor(qs[DH:P, s.par, :], psP[0:DH, :], qs[0:DH, s.par, :].bitcast(F32), ALU.subtract).then_inc(t["ql"], 1)

                def k_low(s):
                    if s.u == 2:
                        dve.tensor_tensor(kl[:, s.par, :], psP[DH:P, :], ks[0:DH, s.par, :].bitcast(F32), ALU.subtract).then_inc(t["kl"], 1)

                def row_max(s):
                    dve.wait_ge(t["S"], s.done())
                    dve.tensor_reduce(nmax[:, s.par, s.qt:s.qt + 1], psS[:, s.j % 4, 0:s.keys], AX.X, ALU.max, negate=True).then_inc(t["mx"], 1)

                def take_p(s):
                    if s.u not in ON_ACT:
                        dve.wait_ge(t["T"], s.done())
                        dve.tensor_copy(flat(pT[:, s.j % 4, 0:s.qt + 1, :]), psT[:, s.j % 2, 0:s.keys]).then_inc(t["ed"], 1)

                def invert(s):
                    if s.u == 3:
                        dve.wait_ge(t["ex"], s.done() + 4)
                        dve.reciprocal(rinv[:, s.par, :], rsum[:, s.par, :]).then_inc(t["rs"], 1)

                def norm(s):
                    if s.u == 3:
                        dve.wait_ge(t["PV"], s.done())
                        dve.wait_ge(t["rs"], s.head_done())
                        dve.tensor_tensor(o[:, :, s.head_cols()], psO[:, 0:TPB * DH].rearrange("p (t d) -> p t d", t=TPB),
                                          rinv[:, s.par, :].unsqueeze(2).broadcast_to([P, TPB, DH]), ALU.mult).then_inc(t["nr"], 1)

                def body(b):
                    for n in range(TPB):
                        r = bass.ds(b * TPB + n, 1)
                        last = dve.tensor_scalar(xn[:, n, :], x[:, r, :].rearrange("p a d -> p (a d)"), self.mean[:, r],
                                                 self.rstd[:, r], ALU.subtract, ALU.mult)
                    last.then_inc(t["xn"], 1)
                    dve.wait_ge(t["xh"], b + 1)
                    dve.tensor_tensor(xl[:, :], xT[:, :], xh[:, :].bitcast(F32), ALU.subtract).then_inc(t["xl"], 1)
                    for n in (1, 3):
                        dve.wait_ge(t["V"], b * 4 + n + 1)
                        dve.tensor_copy(v[:, n, :].rearrange("p (a d) -> p a d", a=2), psT[:, :, :]).then_inc(t["vd"], 1)
                    slots(dve, b, (6, norm), (4, take_p), (0, row_max), (3, invert), (AHEAD + 1, q_low), (AHEAD + 2, k_low))
                    for n in range(1, NP, 2):
                        dve.wait_ge(t["oT"], b * NP + n + 1)
                        dve.tensor_copy(oT[:, n, :], psS[:, n % 4, :]).then_inc(t["oTd"], 1)
                    rows = x[:, bass.ds(b * TPB, TPB), :]
                    dve.tensor_tensor(rows, rows, bout[:, :, :].broadcast_to([P, TPB, P]), ALU.add).then_inc(t["res"], 1)
                    dve.wait_ge(t["out"], b + 1)
                    dve.wait_ge(t["res"], b * 2 + 1)
                    dve.tensor_tensor(flat(rows), flat(rows), psP[:, :], ALU.add).then_inc(t["res"], 1)

                batches(dve, body)


def hybrid_block_kernel(nc, *tensors):
    args, out = dict(zip(_INS, tensors)), tensors[len(_INS)]
    with ExitStack() as ctx:
        k = Kernel(nc, ctx, args, out)
        k.qkv_phase()
        k.unit_phase()
        with ExitStack() as sums:
            k.acc = sums.enter_context(nc.psum_tensor("acc", [P, 3, NC, P], F32))
            for step in range(TTT_STEPS):
                k.gradient_phase(step)
                k.schulz_phase(step)
        k.query_phase()
        k.moe_phase(0)
        k.attention_phase()
        k.moe_phase(1)


_INS = ["L0_attn_a_x", "L0_attn_a_qkv_w", "L0_attn_a_qkv_b", "L0_attn_a_qn_scale", "L0_attn_a_qn_bias",
        "L0_attn_a_kn_scale", "L0_attn_a_kn_bias", "L0_attn_a_ttt_gate", "L0_attn_a_ttt_val", "L0_attn_a_ttt_proj",
        "L0_attn_a_proj_w", "L0_attn_a_proj_b", "L0_attn_b_g", "L0_attn_b_b", "L0_attn_b_w_qkv", "L0_attn_b_w_out",
        "L0_attn_b_b_out", "L0_ffn_We", "L0_ffn_be", "L0_ffn_Wg", "L0_ffn_bg"]
_OUTS = [((BATCH, SEQ, P), "float32")]


def kernel(**inputs):
    import numpy as _np
    import concourse.bacc as _bacc
    from concourse import mybir as _mybir
    from concourse.bass_utils import run_bass_kernel_spmd as _run

    nc = _bacc.Bacc("TRN2", target_bir_lowering=False, num_devices=1)
    arrays, args = {}, []
    for name in _INS:
        a = _np.ascontiguousarray(inputs[name])
        arrays[f"in_{name}_dram"] = a
        args.append(nc.dram_tensor(f"in_{name}_dram", a.shape, _mybir.dt.from_np(a.dtype), kind="ExternalInput").ap())
    for i, (shape, dtype) in enumerate(_OUTS):
        dt = _mybir.dt.from_np(_np.dtype(dtype))
        args.append(nc.dram_tensor(f"out_{i}_dram", shape, dt, kind="ExternalOutput").ap())
    hybrid_block_kernel(nc, *args)
    r = _run(nc, [arrays], core_ids=[0])
    return r.results[0]["out_0_dram"]
```

```python
from contextlib import ExitStack

import concourse.bass as bass
from concourse import mybir

F32 = mybir.dt.float32
F32R = mybir.dt.float32r
BF16 = mybir.dt.bfloat16
ALU = mybir.AluOpType
ACT = mybir.ActivationFunctionType
AX = mybir.AxisListType

P = 128
BATCH, SEQ = 4, 512
TOK = BATCH * SEQ
NT = TOK // P
TPB = SEQ // P
QH, QD = 16, 8
HID = 4 * P
NC = HID // P
TTT_STEPS = 2
LR = 0.1
NS_A, NS_B, NS_C = 3.4445, -4.775, 2.0315
LOSS_SCALE = 2.0 / (TOK * P)
HEADS, DH = 16, 64
NP = HEADS // 2
FRAME = 32
NE = 8
LN_EPS = 1e-5
NEG = -1e30


class Tile:

    def __init__(self, i, j, base=0):
        self.i, self.j, self.base = i, j, base
        self.ring = j % 2

    def done(self, n=1, k=1):
        return self.i * (2 * k) + (self.j * k + n + self.base * k)

    def cols(self, width=P):
        return bass.ds(self.i * (2 * width) + self.j * width, width)

    def next(self, n=1):
        return Tile(self.i, self.j + n, self.base)


def each_tile(e, body, base=0):
    with e.Fori(0, NT // 2) as i:
        for j in range(2):
            body(Tile(i, j, base))


def pipeline(e, *stages, count=NT):
    last = max(lag for lag, _ in stages)
    start = last + last % 2

    def turn(i, j, base):
        for lag, step in stages:
            if i is not None or 0 <= j - lag < count:
                step(Tile(0 if i is None else i, j - lag, base))

    def run(base=0):
        for s in range(start):
            turn(None, s, base)
        with e.Fori(start // 2, count // 2) as i:
            for j in range(2):
                turn(i, j, base)
        for s in range(max(start, count), count + last):
            turn(None, s, base)

    return run


class Slot:

    N = HEADS * TPB
    TURN = 2 * TPB

    def __init__(self, b, i, j):
        self.b, self.i, self.j = b, i, j
        self.u = j % TPB
        self.qt = TPB - 1 - self.u
        self.par = (j // TPB) % 2
        self.keys = (self.qt + 1) * P

    def done(self, n=1):
        return self.i * self.TURN + self.b * self.N + (self.j + n)

    def head_done(self, n=1, k=1):
        return self.i * (2 * k) + self.b * (HEADS * k) + ((self.j // TPB) * k + n)

    def head_cols(self):
        return bass.ds(self.i * (2 * DH) + (self.j // TPB) * DH, DH)


def slots(e, b, *stages):
    lags = [lag for lag, _ in stages]
    first = -(-max(lags) // Slot.TURN)
    last = (Slot.N + min(0, min(lags))) // Slot.TURN

    def at(i, s, whole):
        for lag, step in stages:
            if whole or 0 <= s - lag < Slot.N:
                step(Slot(b, i, s - lag))

    for s in range(min(0, min(lags)), first * Slot.TURN):
        at(0, s, False)
    with e.Fori(first, last) as i:
        for j in range(Slot.TURN):
            at(i, j, True)
    for s in range(last * Slot.TURN, Slot.N + max(lags)):
        at(0, s, False)


class Chain:

    def __init__(self, e, sem, start=0):
        self.e, self.sem, self.n = e, sem, start

    def __call__(self, ins):
        ins.then_inc(self.sem, 1)
        self.n += 1
        self.e.wait_ge(self.sem, self.n)
        return self.n


def mm3(e, out, ah, al, bh, bl, start=True, stop=True):
    e.matmul(out, ah, bh, start=start, stop=False)
    e.matmul(out, ah, bl, start=False, stop=False)
    return e.matmul(out, al, bh, start=False, stop=stop)


class Kernel:
    def __init__(self, nc, ctx, args, out):
        self.nc, self.ctx = nc, ctx
        self.a, self.out = args, out
        sb, ps = self.sb, self.ps
        self.x = sb("x", [P, NT, P])
        self.ident = sb("ident", [P, P])
        self.ones = sb("ones", [P, P])
        self.mean = sb("mean", [P, NT])
        self.rstd = sb("rstd", [P, NT])
        self.stats = sb("stats", [P, NT, 6])
        self.lnw = sb("lnw", [P, 4, NT])
        self.we = sb("we", [P, NE * P])
        self.weh, self.wel = sb("weh", [P, NE * P], F32R), sb("wel", [P, NE * P], F32R)
        self.wg, self.bg = sb("wg", [P, NE]), sb("bg", [P, 1, NE])
        self.beh, self.bel = sb("beh", [P, NT * P], F32R), sb("bel", [P, NT * P], F32R)
        self.wqkv = sb("wqkv", [P, 3, HEADS, DH])
        self.wvh, self.wvl = sb("wvh", [P, HEADS * DH], F32R), sb("wvl", [P, HEADS * DH], F32R)
        self.wout, self.bout = sb("wout", [P, NP, P]), sb("bout", [P, 1, P])
        self.lng, self.lnb = sb("lng", [P, 1]), sb("lnb", [P, 1])
        self.factor = sb("factor", [P, P])
        self.s_late, self.s_bias, self.s_parts = self.sem("late"), self.sem("bias"), self.sem("parts")
        self.gradient_sems()
        self.schulz_sems()

    def first_attention_tensors(self, ctx):
        sb = lambda name, shape, dt=F32: ctx.enter_context(self.nc.sbuf_tensor(name, shape, dt))
        self.qkv = sb("qkv", [P, NT, 3 * P])
        self.qkT = sb("qkT", [P, 2, TOK])
        self.ssq = sb("ssq", [P, NT * 2 * QH])
        self.gv = sb("gv", [P, 2 * HID])
        self.gvh, self.gvl = sb("gvh", [P, 2 * HID], F32R), sb("gvl", [P, 2 * HID], F32R)
        self.proj, self.projT = sb("proj", [P, NC, P]), sb("projT", [P, HID])
        self.pTh, self.pTl = sb("pTh", [P, HID], F32R), sb("pTl", [P, HID], F32R)
        self.zeros = sb("zeros", [P, HID], BF16)
        self.be = sb("be", [P, NT, P])

    def sb(self, name, shape, dt=F32):
        return self.ctx.enter_context(self.nc.sbuf_tensor(name, shape, dt))

    def ps(self, name, shape, dt=F32):
        return self.ctx.enter_context(self.nc.psum_tensor(name, shape, dt))

    def sem(self, name):
        return self.ctx.enter_context(self.nc.semaphore(name))

    def take_stats(self, e, tile):
        return e.bn_stats(self.stats[:, bass.ds(tile, 1), :], self.x[:, bass.ds(tile, 1), :])

    def ln_vector(self, e, s_var, s_root, s_ln):
        st, w = self.stats, self.lnw
        c = Chain(e, s_ln)
        c(e.tensor_tensor(w[:, 0, :], st[:, :, 1], st[:, :, 4], ALU.subtract))
        c(e.tensor_tensor(w[:, 1, :], w[:, 0, :], w[:, 0, :], ALU.mult))
        c(e.tensor_tensor(w[:, 2, :], st[:, :, 2], st[:, :, 5], ALU.add))
        c(e.scalar_tensor_tensor(w[:, 3, :], w[:, 1, :], P / 4.0, w[:, 2, :], ALU.mult, ALU.add))
        c(e.tensor_scalar(w[:, 3, :], w[:, 3, :], 1.0 / P, LN_EPS, ALU.mult, ALU.add))
        e.sem_inc(s_var, 1)
        c(e.tensor_tensor(w[:, 0, :], st[:, :, 1], st[:, :, 4], ALU.add))
        c(e.tensor_scalar(self.mean[:, :], w[:, 0, :], 0.5, None, ALU.mult))
        e.wait_ge(s_root, 1)
        c(e.reciprocal(self.rstd[:, :], w[:, 1, :]))
        return c.n

    def ln_scalar(self, e, s_var, s_root):
        e.preload_act_table(ACT.Sqrt)
        e.wait_ge(s_var, 1)
        e.activation(self.lnw[:, 1, :], self.lnw[:, 3, :], ACT.Sqrt).then_inc(s_root, 1)

    def qkv_phase(self):
        nc, sem = self.nc, self.sem
        x, qkv, ident = self.x, self.qkv, self.ident
        s_x, s_w, s_cst = sem("p0_x"), sem("p0_w"), sem("p0_cst")
        s_stat, s_var, s_root, s_ln = sem("p0_stat"), sem("p0_var"), sem("p0_root"), sem("p0_ln")
        s_xn, s_xT, s_xTs, s_qkv, s_out, s_sq, s_ss = (
            sem("p0_" + n) for n in ("xn", "xT", "xTs", "qkv", "out", "sq", "ss"))
        with ExitStack() as c:
            sb = lambda n, s, d=F32: c.enter_context(nc.sbuf_tensor(n, s, d))
            ps = lambda n, s, d=F32: c.enter_context(nc.psum_tensor(n, s, d))
            w = sb("p0_w_", [P, 3 * P])
            bias = sb("p0_bias", [P, 3 * P])
            xn = sb("p0_xn_", [P, 2, P])
            xTs = sb("p0_xTs_", [P, 2, P])
            sq = sb("p0_sq_", [P, 2, 2 * P])
            psT = [ps(f"p0_T{r}", [P, P]) for r in range(2)]
            psQ = [ps(f"p0_Q{r}", [P, 3 * P]) for r in range(2)]
            block = c.enter_context(nc.Block())
            xsrc = self.a["L0_attn_a_x"].rearrange("b (t p) d -> p (b t) d", p=P)

            @block.sync
            def _(sp):
                for g in range(4):
                    sp.dma_start(x[:, 4 * g:4 * g + 4, :], xsrc[:, 4 * g:4 * g + 4, :]).then_inc(s_x, 16)
                sp.dma_start(w[:, :], self.a["L0_attn_a_qkv_w"]).then_inc(s_w, 16)
                sp.dma_start(bias[:, :], self.a["L0_attn_a_qkv_b"].rearrange("(a n) -> a n", a=1).broadcast_to([P, 3 * P])).then_inc(s_w, 16)
                sp.wait_ge(s_w, 32)

            @block.gpsimd
            def _(pool):
                pool.memset(self.ones[:, :], 1.0).then_inc(s_cst, 1)
                pool.memset(ident[:, :], 0.0).then_inc(s_cst, 1)
                pool.wait_ge(s_cst, 2)
                pool.affine_select(out=ident[:, :], in_=ident[:, :], compare_op=ALU.not_equal, fill=1.0, base=0,
                                   pattern=[[-1, P]], channel_multiplier=1).then_inc(s_cst, 1)
                pool.memset(self.be[:, :, :], 0.0).then_inc(self.s_bias, 1)
                pool.memset(self.factor[:, :], DH ** -0.5).then_inc(self.s_bias, 1)

            @block.scalar
            def _(act):
                self.ln_scalar(act, s_var, s_root)

                def copy(t):
                    act.wait_ge(s_xT, t.done() + 2)
                    act.activation(xTs[:, t.ring, :], psT[t.ring][:, :], ACT.Copy).then_inc(s_xTs, 1)

                def square(t):
                    act.wait_ge(s_out, t.done() + 2)
                    act.activation(sq[:, t.ring, :], qkv[:, bass.ds(t.i * 2 + t.j, 1), 0:2 * P], ACT.Square).then_inc(s_sq, 1)

                pipeline(act, (0, copy), (2, square))()

            @block.tensor
            def _(pe):
                pe.wait_ge(s_cst, 3)

                def turn(t):
                    pe.wait_ge(s_xn, t.done())
                    pe.transpose(psT[t.ring][:, :], xn[:, t.ring, :], ident[:, :]).then_inc(s_xT, 1)

                def project(t):
                    pe.wait_ge(s_xTs, t.done())
                    pe.wait_ge(s_out, t.done())
                    pe.matmul(psQ[t.ring][:, :], xTs[:, t.ring, :], w[:, :], start=True, stop=True).then_inc(s_qkv, 1)

                pe.wait_ge(s_w, 32)
                pipeline(pe, (0, turn), (1, project))()

            @block.vector
            def _(dve):
                dve.wait_ge(s_x, 64)
                each_tile(dve, lambda t: self.take_stats(dve, t.i * 2 + t.j).then_inc(s_stat, 1))
                dve.wait_ge(s_stat, NT)
                self.ln_vector(dve, s_var, s_root, s_ln)
                dve.sem_inc(s_xT, 2)
                dve.sem_inc(s_out, 2)
                dve.wait_ge(s_w, 32)

                def norm(t):
                    dve.wait_ge(s_xT, t.done())
                    tt = bass.ds(t.i * 2 + t.j, 1)
                    dve.tensor_scalar(xn[:, t.ring, :], x[:, tt, :].rearrange("p a d -> p (a d)"), self.mean[:, tt],
                                      self.rstd[:, tt], ALU.subtract, ALU.mult).then_inc(s_xn, 1)

                def bias_add(t):
                    dve.wait_ge(s_qkv, t.done())
                    dve.tensor_tensor(qkv[:, bass.ds(t.i * 2 + t.j, 1), :], psQ[t.ring][:, :], bias[:, :], ALU.add).then_inc(s_out, 1)

                def sumsq(t):
                    dve.wait_ge(s_sq, t.done())
                    dve.tensor_reduce(self.ssq[:, bass.ds(t.i * 64 + t.j * 32, 32)],
                                      sq[:, t.ring, :].rearrange("p (g d) -> p g d", d=QD), AX.X, ALU.add).then_inc(s_ss, 1)

                pipeline(dve, (0, norm), (2, bias_add), (3, sumsq))()
                dve.wait_ge(s_ss, NT)


    def unit_phase(self):
        nc, sem, qkv, qkT, ident = self.nc, self.sem, self.qkv, self.qkT, self.ident
        s_w, s_rt, s_inv, s_st = sem("p1_w"), sem("p1_rt"), sem("p1_inv"), sem("p1_st")
        s_m, s_s, s_b, s_T, s_e, s_k = (sem("p1_" + n) for n in ("m", "s", "b", "T", "e", "k"))
        s_gh, s_pt, s_ptc, s_pth = sem("p1_gh"), sem("p1_pt"), sem("p1_ptc"), sem("p1_pth")
        with ExitStack() as c:
            sb = lambda n, s, d=F32: c.enter_context(nc.sbuf_tensor(n, s, d))
            ps = lambda n, s, d=F32: c.enter_context(nc.psum_tensor(n, s, d))
            scale, bias = sb("p1_scale", [P, 2, QD]), sb("p1_bias", [P, 2, QD])
            scale_all, bias_all = sb("p1_scale_all", [P, 2 * P]), sb("p1_bias_all", [P, 2 * P])
            inv = sb("p1_inv_", [P, NT * 32])
            m, sc, u = sb("p1_m_", [P, 2, 2 * P]), sb("p1_s_", [P, 2, 2 * P]), sb("p1_u_", [P, 2, 2 * P])
            psT = [ps(f"p1_T{r}", [P, 2, P]) for r in range(2)]
            psP = ps("p1_P", [P, NC, P])
            block = c.enter_context(nc.Block())

            @block.sync
            def _(sp):
                for n, w in enumerate(("qn", "kn")):
                    for dst, what in ((scale, "scale"), (bias, "bias")):
                        sp.dma_start(dst[:, n, :], self.a[f"L0_attn_a_{w}_{what}"].rearrange("(a n) -> a n", a=1)
                                     .broadcast_to([P, QD])).then_inc(s_w, 16)
                sp.dma_start(self.gv[:, 0:HID], self.a["L0_attn_a_ttt_gate"]).then_inc(s_w, 16)
                sp.dma_start(self.gv[:, HID:2 * HID], self.a["L0_attn_a_ttt_val"]).then_inc(s_w, 16)
                sp.dma_start(self.proj[:, :, :], self.a["L0_attn_a_ttt_proj"].rearrange("(c p) d -> p c d", p=P)).then_inc(s_w, 16)

            @block.gpsimd
            def _(pool):
                pool.sem_inc(s_b, 2)

                def scaled(t):
                    pool.wait_ge(s_m, t.done())
                    pool.wait_ge(s_b, t.done())
                    pool.tensor_tensor(sc[:, t.ring, :], m[:, t.ring, :], scale_all[:, :], ALU.mult).then_inc(s_s, 1)

                pipeline(pool, (0, scaled))()

            @block.scalar
            def _(act):
                act.wait_ge(s_w, 7 * 16)
                act.activation(self.gvh[:, :], self.gv[:, :], ACT.Copy).then_inc(s_gh, 1)
                act.activation(self.ssq[:, :], self.ssq[:, :], ACT.Sqrt).then_inc(s_rt, 1)
                act.wait_ge(s_ptc, 1)
                act.activation(self.pTh[:, :], self.projT[:, :], ACT.Copy).then_inc(s_pth, 1)

                def copy(t):
                    act.wait_ge(s_T, t.done() + 2)
                    act.activation(qkT[:, :, t.cols()], psT[t.ring][:, :, :], ACT.Copy).then_inc(s_e, 1)

                def keep(t):
                    act.wait_ge(s_b, t.done() + 2)
                    act.activation(qkv[:, bass.ds(t.i * 2 + t.j, 1), P:2 * P], u[:, t.ring, P:2 * P], ACT.Copy).then_inc(s_k, 1)

                act.sem_inc(s_e, 2)
                act.sem_inc(s_k, 2)
                pipeline(act, (0, copy), (0, keep))()

            @block.tensor
            def _(pe):
                pe.wait_ge(s_w, 7 * 16)
                for n in range(NC):
                    last = pe.transpose(psP[:, n, :], self.proj[:, n, :], ident[:, :])
                last.then_inc(s_pt, 1)

                def turn(t):
                    pe.wait_ge(s_b, t.done() + 2)
                    pe.wait_ge(s_e, t.done())
                    pe.transpose(psT[t.ring][:, 0, :], u[:, t.ring, 0:P], ident[:, :])
                    pe.transpose(psT[t.ring][:, 1, :], u[:, t.ring, P:2 * P], ident[:, :]).then_inc(s_T, 1)

                pipeline(pe, (0, turn))()

            @block.vector
            def _(dve):
                c = Chain(dve, s_st)
                dve.wait_ge(s_w, 7 * 16)
                for dst, src in ((scale_all, scale), (bias_all, bias)):
                    for n in range(2):
                        c(dve.tensor_copy(dst[:, n * P:n * P + P].rearrange("p (g d) -> p g d", d=QD),
                                          src[:, n:n + 1, :].broadcast_to([P, QH, QD])))
                dve.wait_ge(s_gh, 1)
                c(dve.tensor_tensor(self.gvl[:, :], self.gv[:, :], self.gvh[:, :].bitcast(F32), ALU.subtract))
                dve.wait_ge(s_pt, 1)
                dve.tensor_copy(self.projT[:, :], psP[:, :, :].rearrange("p c d -> p (c d)")).then_inc(s_ptc, 1)
                dve.wait_ge(s_pth, 1)
                c(dve.tensor_tensor(self.pTl[:, :], self.projT[:, :], self.pTh[:, :].bitcast(F32), ALU.subtract))
                dve.wait_ge(s_rt, 1)
                c(dve.tensor_scalar(self.ssq[:, :], self.ssq[:, :], 1e-6, None, ALU.add))
                c(dve.reciprocal(inv[:, :], self.ssq[:, :]))
                dve.sem_inc(s_s, 2)

                def unit(t):
                    dve.wait_ge(s_s, t.done())
                    r = inv[:, bass.ds(t.i * 64 + t.j * 32, 32)]
                    dve.tensor_tensor(m[:, t.ring, :].rearrange("p (g d) -> p g d", d=QD),
                                      qkv[:, bass.ds(t.i * 2 + t.j, 1), 0:2 * P].rearrange("p a (g d) -> p (a g) d", d=QD),
                                      r.unsqueeze(2).broadcast_to([P, 32, QD]), ALU.mult).then_inc(s_m, 1)

                def shift(t):
                    dve.wait_ge(s_s, t.done() + 2)
                    dve.wait_ge(s_T, t.done())
                    dve.wait_ge(s_k, t.done())
                    dve.tensor_tensor(u[:, t.ring, :], sc[:, t.ring, :], bias_all[:, :], ALU.add).then_inc(s_b, 1)

                dve.sem_inc(s_T, 2)
                pipeline(dve, (0, unit), (2, shift))()

    def gradient_sems(self):
        names = "kh kl F sig u sw h t1 sp w1 HT hT PR d DT dTh dTl DH du dg G zero".split()
        self.g = {n: self.sem("g_" + n) for n in names}

    def gradient_phase(self, step):
        nc, qkv, qkT, g = self.nc, self.qkv, self.qkT, self.g
        base = step * NT
        with ExitStack() as c:
            sb = lambda n, s, d=F32: c.enter_context(nc.sbuf_tensor(f"g{step}_{n}", s, d))
            ps = lambda n, s, d=F32: c.enter_context(nc.psum_tensor(f"g{step}_{n}", s, d))
            kh, kl = sb("kh", [P, 2, P], F32R), sb("kl", [P, 2, P], F32R)
            s_, u_, sw, h, t1, sp_, w1, hT, du, dg = (sb(n, [P, 2, HID]) for n in
                                                      ("s", "u", "sw", "h", "t1", "sp", "w1", "hT", "du", "dg"))
            d = sb("d", [P, 2, P])
            dTh, dTl = sb("dTh", [P, 2, P], F32R), sb("dTl", [P, 2, P], F32R)
            psG, psU, psH, psD = (ps(n, [P, HID]) for n in ("G", "U", "H", "D"))
            psPT = ps("PT", [P, 4, P])
            pred, dTp = psPT[:, 0, :], psPT[:, 1, :]
            gvh, gvl = self.gvh, self.gvl
            block = c.enter_context(nc.Block())

            @block.sync
            def _(sp):
                if step == 0:
                    self.load_later_weights(sp)

            @block.gpsimd
            def _(pool):
                if step == 0:
                    pool.sem_inc(g["sp"], 2)
                    pool.sem_inc(g["w1"], 2)
                    pool.memset(self.zeros[:, :], 0.0).then_inc(g["zero"], 1)

                def k_low(t):
                    pool.wait_ge(g["kh"], t.done())
                    pool.tensor_tensor(kl[:, t.ring, :], qkT[:, 1, t.cols()], kh[:, t.ring, :].bitcast(F32),
                                       ALU.subtract).then_inc(g["kl"], 1)

                def slope(t):
                    pool.wait_ge(g["t1"], t.done())
                    pool.tensor_tensor(sp_[:, t.ring, :], s_[:, t.ring, :], t1[:, t.ring, :], ALU.subtract).then_inc(g["sp"], 1)

                def gate_factor(t):
                    pool.wait_ge(g["sp"], t.done() + 2)
                    pool.wait_ge(g["dg"], t.done(0))
                    pool.tensor_tensor(w1[:, t.ring, :], u_[:, t.ring, :], sp_[:, t.ring, :], ALU.mult).then_inc(g["w1"], 1)

                pipeline(pool, (0, k_low), (1, slope), (1, gate_factor))(base)

            @block.scalar
            def _(act):
                if step == 0:
                    act.sem_inc(g["u"], 1)
                    act.sem_inc(g["hT"], 1)
                act.preload_act_table(ACT.Sigmoid)

                def k_high(t):
                    act.wait_ge(g["F"], t.done(2, 2))
                    act.activation(kh[:, t.ring, :], qkT[:, 1, t.cols()], ACT.Copy).then_inc(g["kh"], 1)

                def sigmoid(t):
                    act.wait_ge(g["F"], t.done(1, 2) + 4)
                    act.wait_ge(g["sp"], t.done())
                    act.activation(s_[:, t.ring, :], psG[:, :], ACT.Sigmoid).then_inc(g["sig"], 1)

                def keep_u(t):
                    act.wait_ge(g["F"], t.done(2, 2) + 4)
                    act.wait_ge(g["w1"], t.done())
                    act.activation(u_[:, t.ring, :], psU[:, :], ACT.Copy).then_inc(g["u"], 1)

                def keep_hT(t):
                    act.wait_ge(g["HT"], t.done())
                    act.activation(hT[:, t.ring, :], psH[:, :], ACT.Copy).then_inc(g["hT"], 1)

                def dT_high(t):
                    act.wait_ge(g["DT"], t.done())
                    act.activation(dTh[:, t.ring, :], dTp, ACT.Copy).then_inc(g["dTh"], 1)

                pipeline(act, (2, keep_hT), (0, k_high), (1, sigmoid), (1, keep_u), (2, dT_high))(base)

            @block.tensor
            def _(pe):
                if step == 0:
                    pe.sem_inc(g["F"], 4)
                    pe.sem_inc(g["G"], 6)
                pe.wait_ge(g["zero"], 1)
                for n in range(3):
                    pe.matmul(self.acc[:, n, :, :].rearrange("p c d -> p (c d)"), self.zeros[:, 0:P], self.zeros[:, :],
                              start=True, stop=False, skip_group_check=True)

                def forward(t):
                    pe.wait_ge(g["kh"], t.done())
                    pe.wait_ge(g["kl"], t.done())
                    a, b = kh[:, t.ring, :], kl[:, t.ring, :]
                    pe.wait_ge(g["sw"], t.done())
                    mm3(pe, psG[:, :], a, b, gvh[:, 0:HID], gvl[:, 0:HID]).then_inc(g["F"], 1)
                    pe.wait_ge(g["u"], t.done())
                    mm3(pe, psU[:, :], a, b, gvh[:, HID:2 * HID], gvl[:, HID:2 * HID]).then_inc(g["F"], 1)

                def turn_h(t):
                    pe.wait_ge(g["h"], t.done())
                    pe.wait_ge(g["hT"], t.done())
                    for n in range(NC):
                        last = pe.transpose(psH[:, n * P:n * P + P], h[:, t.ring, n * P:n * P + P], self.ident[:, :])
                    last.then_inc(g["HT"], 1)

                def predict(t):
                    pe.wait_ge(g["hT"], t.done() + 1)
                    pe.wait_ge(g["dTl"], t.done())
                    for n in range(NC):
                        last = pe.matmul(pred, hT[:, t.ring, n * P:n * P + P], self.proj[:, n, :],
                                         start=(n == 0), stop=(n == NC - 1))
                    last.then_inc(g["PR"], 1)

                def turn_d(t):
                    pe.wait_ge(g["d"], t.done())
                    pe.transpose(dTp, d[:, t.ring, :], self.ident[:, :]).then_inc(g["DT"], 1)

                def back(t):
                    pe.wait_ge(g["dTh"], t.done())
                    pe.wait_ge(g["dTl"], t.done() + 1)
                    pe.wait_ge(g["dg"], t.done())
                    mm3(pe, psD[:, :], dTh[:, t.ring, :], dTl[:, t.ring, :], self.pTh[:, :], self.pTl[:, :]).then_inc(g["DH"], 1)

                def add(n, src, ready):
                    def step_(t):
                        pe.wait_ge(*ready(t))
                        k = qkv[:, bass.ds(t.i * 2 + t.j, 1), P:2 * P]
                        for m in range(NC):
                            last = pe.matmul(self.acc[:, n, m, :], src[:, t.ring, m * P:m * P + P],
                                             d[:, t.ring, :] if n == 2 else k, start=False, stop=False, skip_group_check=True)
                        last.then_inc(g["G"], 1)
                    return step_

                add_proj = add(2, h, lambda t: (g["d"], t.done()))
                add_val = add(1, du, lambda t: (g["du"], t.done() + 2))
                add_gate = add(0, dg, lambda t: (g["dg"], t.done() + 1))
                pipeline(pe, (2, turn_h), (3, add_proj), (1, forward), (2, predict), (3, add_val), (2, turn_d),
                         (3, add_gate), (2, back))(base)

            @block.vector
            def _(dve):
                if step == 0:
                    for n in ("sw", "dTl", "dg"):
                        dve.sem_inc(g[n], 1)
                    dve.sem_inc(g["du"], 2)

                def swish(t):
                    dve.wait_ge(g["sig"], t.done())
                    dve.wait_ge(g["du"], t.done())
                    dve.tensor_tensor(sw[:, t.ring, :], psG[:, :], s_[:, t.ring, :], ALU.mult).then_inc(g["sw"], 1)

                def hidden(t):
                    dve.wait_ge(g["u"], t.done() + 1)
                    dve.wait_ge(g["sw"], t.done() + 1)
                    dve.wait_ge(g["G"], t.done(1, 3))
                    dve.tensor_tensor(h[:, t.ring, :], sw[:, t.ring, :], u_[:, t.ring, :], ALU.mult).then_inc(g["h"], 1)

                def fall(t):
                    dve.scalar_tensor_tensor(t1[:, t.ring, :], s_[:, t.ring, :], 1.0, sw[:, t.ring, :],
                                             ALU.subtract, ALU.mult).then_inc(g["t1"], 1)

                def error(t):
                    dve.wait_ge(g["PR"], t.done())
                    dve.tensor_tensor(d[:, t.ring, :], pred, qkv[:, bass.ds(t.i * 2 + t.j, 1), 2 * P:3 * P],
                                      ALU.subtract).then_inc(g["d"], 1)

                def dT_low(t):
                    dve.wait_ge(g["dTh"], t.done())
                    dve.tensor_tensor(dTl[:, t.ring, :], dTp, dTh[:, t.ring, :].bitcast(F32), ALU.subtract).then_inc(g["dTl"], 1)

                def grad_val(t):
                    dve.wait_ge(g["DH"], t.done())
                    dve.tensor_tensor(du[:, t.ring, :], psD[:, :], sw[:, t.ring, :], ALU.mult).then_inc(g["du"], 1)

                def grad_gate(t):
                    dve.wait_ge(g["w1"], t.done() + 2)
                    dve.tensor_tensor(dg[:, t.ring, :], psD[:, :], w1[:, t.ring, :], ALU.mult).then_inc(g["dg"], 1)

                pipeline(dve, (1, swish), (2, error), (1, hidden), (1, fall), (2, dT_low), (2, grad_val), (2, grad_gate))(base)


    USED = ("xt", "x", "scaled", "p0", "t0", "a1", "p1", "q1", "xt2", "x2", "a2",
            "p2", "t2", "a3", "p3", "t3", "a4", "p4", "q4", "new", "newT")

    LATE_LOADS = 8 + NT

    def load_later_weights(self, sp):
        row = lambda name: self.a[name].rearrange("(a n) -> a n", a=1)
        loads = [
            (self.we[:, :].rearrange("d (e o) -> d e o", e=NE), self.a["L0_ffn_We"].rearrange("e d o -> d e o")),
            (self.wqkv[:, :, :, :].rearrange("p a h d -> p (a h d)"), self.a["L0_attn_b_w_qkv"]),
            (self.wout[:, :, :], self.a["L0_attn_b_w_out"].rearrange("(n p) d -> p n d", p=P)),
            (self.wg[:, :], self.a["L0_ffn_Wg"]),
            (self.bg[:, 0, :], row("L0_ffn_bg").broadcast_to([P, NE])),
            (self.bout[:, 0, :], row("L0_attn_b_b_out").broadcast_to([P, P])),
            (self.lng[:, :], self.a["L0_attn_b_g"].rearrange("a b d -> d (a b)")),
            (self.lnb[:, :], self.a["L0_attn_b_b"].rearrange("a b d -> d (a b)")),
        ]
        for dst, src in loads:
            sp.dma_start(dst, src).then_inc(self.s_late, 16)
        sp.wait_ge(self.s_bias, 2)
        for t in range(NT):
            sp.dma_start(self.be[t * NE:(t + 1) * NE, t, :], self.a["L0_ffn_be"]).then_inc(self.s_late, 16)

    def part_later_weights(self, pool):
        wide = lambda ap: ap.rearrange("p (a d) -> p a d", d=P)
        times = lambda ap, n=NE: ap[:, :].unsqueeze(1).broadcast_to([P, n, P])
        wq, wv = (self.wqkv[:, n, :, :].rearrange("p h d -> p (h d)") for n in (0, 2))
        pool.wait_ge(self.s_late, 16 * self.LATE_LOADS)
        c = Chain(pool, self.s_parts)
        for src, high, low in ((self.we[:, :], self.weh, self.wel), (wv, self.wvh, self.wvl)):
            c(pool.tensor_tensor(wide(high[:, :]), wide(src), times(self.ones), ALU.mult))
            c(pool.tensor_tensor(low[:, :], src, high[:, :].bitcast(F32), ALU.subtract))
        be = self.be[:, :, :].rearrange("p t d -> p (t d)")
        c(pool.tensor_tensor(wide(self.beh[:, :]), self.be[:, :, :], times(self.ones, NT), ALU.mult))
        c(pool.tensor_tensor(self.bel[:, :], be, self.beh[:, :].bitcast(F32), ALU.subtract))
        c(pool.tensor_tensor(wide(wq), wide(wq), times(self.factor), ALU.mult))

    def schulz_sems(self):
        self.used = [self.sem(f"ns_used{m}") for m in range(3)]
        self.made = [self.sem(f"ns_made{m}") for m in range(3)]
        self.s_trace, self.s_norm, self.s_root, self.s_rate, self.s_nsv = (
            self.sem("ns_" + n) for n in ("trace", "norm", "root", "rate", "v"))
        self.s_gh, self.s_ph, self.s_lo = self.sem("ns_gh"), self.sem("ns_ph"), self.sem("ns_lo")

    def schulz_phase(self, step):
        nc, acc, ident = self.nc, self.acc, self.ident
        used, made = self.used, self.made

        def after(m, name):
            names = self.USED[:len(self.USED) - (m < 2)]
            return step * len(names) + names.index(name) + 1

        def result(m, name):
            names = [n for n in self.USED[:len(self.USED) - (m < 2)] if n not in ("xt", "scaled")]
            return step * len(names) + names.index(name) + 1

        with ExitStack() as c:
            sb = lambda n, s, d=F32: c.enter_context(nc.sbuf_tensor(f"n{step}_{n}", s, d))
            XT, X, XT2, X2 = (sb(n, [P, 3, NC, P]) for n in ("XT", "X", "XT2", "X2"))
            A, T1, T, Q = (sb(n, [P, 3, P]) for n in ("A", "T1", "T", "Q"))
            Pm = sb("P", [P, 2, 3, P])
            aI, junk = sb("aI", [P, P]), sb("junk", [P, P])
            tr, nrm, r, r2, rate = (sb(n, [P, 3]) for n in ("tr", "nrm", "r", "r2", "rate"))
            small = [c.enter_context(nc.psum_tensor(f"n{step}_small{m}", [P, 4, P], F32)) for m in range(3)]
            big = [acc[:, m, :, :] for m in range(3)]
            flat = lambda ap: ap.rearrange("p c d -> p (c d)")
            block = c.enter_context(nc.Block())

            @block.gpsimd
            def _(pool):
                if step == TTT_STEPS - 1:
                    self.part_later_weights(pool)

            @block.tensor
            def _(pe):
                def gram(m, src, name):
                    for n in range(NC):
                        last = pe.matmul(small[m][:, 0, :], src[:, m, n, :], src[:, m, n, :], start=(n == 0), stop=(n == NC - 1))
                    return last

                def square(k):
                    for m in range(3):
                        pe.wait_ge(used[m], after(m, f"a{k}" if k else "scaled"))
                        pe.matmul(small[m][:, 1, :], A[:, m, :], A[:, m, :], start=True, stop=True).then_inc(made[m], 1)

                def times_a(k, with_q=False):
                    for m in range(3):
                        pe.wait_ge(used[m], after(m, f"p{k}"))
                        if with_q:
                            pe.matmul(small[m][:, 3, :], Pm[:, k % 2, m, :], Pm[:, 1 - k % 2, m, :], start=True, stop=True)
                        pe.matmul(small[m][:, 2, :], Pm[:, k % 2, m, :], A[:, m, :], start=True, stop=True).then_inc(made[m], 1)

                def next_a(k):
                    for m in range(3):
                        pe.wait_ge(used[m], after(m, f"t{k}"))
                        pe.matmul(small[m][:, 0, :], Pm[:, k % 2, m, :], T[:, m, :], start=True, stop=True).then_inc(made[m], 1)

                def last_q(k, before):
                    for m in range(3):
                        pe.wait_ge(used[m], after(m, f"p{k}"))
                        pe.matmul(small[m][:, 3, :], Pm[:, k % 2, m, :], before(m), start=True, stop=True).then_inc(made[m], 1)

                for m in range(3):
                    pe.wait_ge(used[m], after(m, "xt"))
                    gram(m, XT, "trace").then_inc(self.s_norm, 1)
                for m in range(3):
                    for n in range(NC):
                        last = pe.transpose(big[m][:, n, :], XT[:, m, n, :], ident[:, :])
                    last.then_inc(made[m], 1)
                pe.wait_ge(self.s_trace, 3 * step + 3)
                pe.matmul(small[0][:, 3, 0:3], self.ones[:, :], tr[:, :], start=True, stop=True).then_inc(self.s_norm, 1)
                square(0)
                times_a(0)
                next_a(0)
                square(1)
                last_q(1, lambda m: Pm[:, 0, m, :])
                for m in range(3):
                    pe.wait_ge(used[m], after(m, "q1"))
                    for n in range(NC):
                        last = pe.matmul(big[m][:, n, :], X[:, m, n, :], Q[:, m, :], start=True, stop=True)
                    last.then_inc(made[m], 1)
                for m in range(3):
                    pe.wait_ge(used[m], after(m, "xt2"))
                    pe.matmul(flat(big[m]), Q[:, m, :], flat(X[:, m, :, :]), start=True, stop=True).then_inc(made[m], 1)
                for m in range(3):
                    pe.wait_ge(used[m], after(m, "x2"))
                    gram(m, XT2, "a2").then_inc(made[m], 1)
                square(2)
                times_a(2)
                next_a(2)
                square(3)
                times_a(3, True)
                next_a(3)
                square(4)
                last_q(4, lambda m: Q[:, m, :])
                for m in range(3):
                    pe.wait_ge(used[m], after(m, "q4"))
                    pe.matmul(flat(big[m]), Q[:, m, :], flat(X2[:, m, :, :]), start=True, stop=True).then_inc(made[m], 1)
                pe.wait_ge(used[2], after(2, "new"))
                for n in range(NC):
                    last = pe.matmul(big[2][:, n, :], X2[:, 2, n, :], Q[:, 2, :], start=True, stop=True)
                last.then_inc(made[2], 1)

            @block.scalar
            def _(act):
                def copy(m, dst, src, name):
                    if name != "xt":
                        act.wait_ge(made[m], result(m, name))
                    act.activation(dst, src, ACT.Copy).then_inc(used[m], 1)

                for m in (0, 2):
                    copy(m, flat(XT[:, m, :, :]), flat(big[m]), "xt")
                for m in range(3):
                    copy(m, flat(X[:, m, :, :]), flat(big[m]), "x")
                act.wait_ge(self.s_norm, 4 * step + 4)
                act.activation(nrm[:, :], small[0][:, 3, 0:3], ACT.Sqrt).then_inc(self.s_root, 1)

                def small_copy(dst, slot, name):
                    for m in range(3):
                        copy(m, dst[:, m, :], small[m][:, slot, :], name)

                small_copy(T, 2, "t0")
                small_copy(Q, 3, "q1")
                for name, dst in (("xt2", XT2), ("x2", X2)):
                    for m in range(3):
                        copy(m, flat(dst[:, m, :, :]), flat(big[m]), name)
                small_copy(T, 2, "t2")
                for m in range(3):
                    act.wait_ge(made[m], result(m, "t3"))
                    act.activation(Q[:, m, :], small[m][:, 3, :], ACT.Copy)
                    act.activation(T[:, m, :], small[m][:, 2, :], ACT.Copy).then_inc(used[m], 1)
                small_copy(Q, 3, "q4")
                for m in range(2):
                    act.wait_ge(used[m], after(m, "new"))
                    half = slice(m * HID, (m + 1) * HID)
                    act.activation(self.gvh[:, half], self.gv[:, half], ACT.Copy).then_inc(self.s_gh, 1)
                act.wait_ge(used[2], after(2, "new"))
                act.activation(self.pTh[:, :], self.projT[:, :], ACT.Copy).then_inc(self.s_ph, 1)

            @block.vector
            def _(dve):
                dve.tensor_copy(flat(XT[:, 1, :, :]), flat(big[1])).then_inc(used[1], 1)
                dve.tensor_scalar(aI[:, :], ident[:, :], NS_A, None, ALU.mult).then_inc(self.s_nsv, 1)
                for m in range(3):
                    dve.wait_ge(self.s_norm, 4 * step + m + 1)
                    if m:
                        dve.wait_ge(self.s_trace, 3 * step + m)
                    dve.tensor_tensor_reduce(junk[:, :], small[m][:, 0, :], ident[:, :], 1.0, 0.0, ALU.mult, ALU.add,
                                             tr[:, m:m + 1]).then_inc(self.s_trace, 1)
                dve.wait_ge(self.s_root, step + 1)
                c = Chain(dve, self.s_nsv, 4 * step + 1)
                c(dve.tensor_scalar(nrm[:, :], nrm[:, :], 1e-7 / LOSS_SCALE, None, ALU.add))
                c(dve.reciprocal(r[:, :], nrm[:, :]))
                dve.tensor_scalar(rate[:, :], r[:, :], -LR, None, ALU.mult).then_inc(self.s_rate, 1)
                c(dve.tensor_tensor(r2[:, :], r[:, :], r[:, :], ALU.mult))

                def scaled(m, name):
                    dve.wait_ge(made[m], result(m, name))
                    dve.tensor_scalar(A[:, m, :], small[m][:, 0, :], r2[:, m:m + 1], None, ALU.mult).then_inc(self.s_rate, 1)

                def mixed(m):
                    dve.scalar_tensor_tensor(T1[:, m, :], A[:, m, :], NS_B, aI[:, :], ALU.mult, ALU.add).then_inc(used[m], 1)

                def scale_all(name, done):
                    for m in range(3):
                        scaled(m, name)
                    for m in range(3):
                        dve.wait_ge(self.s_rate, 7 * step + 1 + done + m + 1)
                        mixed(m)

                def poly(k):
                    for m in range(3):
                        dve.wait_ge(made[m], result(m, f"p{k}"))
                        dve.scalar_tensor_tensor(Pm[:, k % 2, m, :], small[m][:, 1, :], NS_C, T1[:, m, :],
                                                 ALU.mult, ALU.add).then_inc(used[m], 1)

                def next_a(k):
                    for m in range(3):
                        dve.wait_ge(made[m], result(m, f"a{k}"))
                        dve.scalar_tensor_tensor(T1[:, m, :], small[m][:, 0, :], NS_B, aI[:, :], ALU.mult, ALU.add)
                        dve.tensor_copy(A[:, m, :], small[m][:, 0, :]).then_inc(used[m], 1)

                for m in range(3):
                    dve.wait_ge(used[m], after(m, "x"))
                scale_all("x", 0)
                poly(0)
                next_a(1)
                poly(1)
                scale_all("a2", 3)
                poly(2)
                next_a(3)
                poly(3)
                next_a(4)
                poly(4)
                for m in range(3):
                    dve.wait_ge(made[m], result(m, "new"))
                    dst = self.gv[:, m * HID:(m + 1) * HID] if m < 2 else self.projT[:, :]
                    dve.scalar_tensor_tensor(dst, flat(big[m]), rate[:, m:m + 1], dst, ALU.mult, ALU.add).then_inc(used[m], 1)
                dve.wait_ge(made[2], result(2, "newT"))
                dve.scalar_tensor_tensor(flat(self.proj[:, :, :]), flat(big[2]), rate[:, 2:3], flat(self.proj[:, :, :]),
                                         ALU.mult, ALU.add).then_inc(used[2], 1)
                for m in range(2):
                    half = slice(m * HID, (m + 1) * HID)
                    dve.wait_ge(self.s_gh, 2 * step + m + 1)
                    dve.tensor_tensor(self.gvl[:, half], self.gv[:, half], self.gvh[:, half].bitcast(F32), ALU.subtract).then_inc(self.s_lo, 1)
                dve.wait_ge(self.s_ph, step + 1)
                dve.tensor_tensor(self.pTl[:, :], self.projT[:, :], self.pTh[:, :].bitcast(F32), ALU.subtract).then_inc(self.s_lo, 1)


    def query_phase(self):
        nc, sem, x, qkT = self.nc, self.sem, self.x, self.qkT
        names = "w pw pwc qh ql gu sig sw h o xb x".split()
        q = {n: sem("q_" + n) for n in names}
        with ExitStack() as c:
            sb = lambda n, s, d=F32: c.enter_context(nc.sbuf_tensor("q_" + n + "_", s, d))
            ps = lambda n, s, d=F32: c.enter_context(nc.psum_tensor("q_" + n + "_", s, d))
            w, pb, pw = sb("w", [P, P]), sb("pb", [P, 1, P]), sb("pw", [P, NC, P])
            qh, ql = sb("qh", [P, SEQ], F32R), sb("ql", [P, SEQ], F32R)
            sg, sw, hT = sb("sg", [P, 2, SEQ]), sb("sw", [P, 2, SEQ]), sb("hT", [P, NC, SEQ])
            psG, psU = ps("G", [P, 2, SEQ]), ps("U", [P, 2, SEQ])
            psO, psW = ps("O", [P, TPB, P]), ps("W", [P, NC, P])
            block = c.enter_context(nc.Block())

            def batches(e, body):
                with e.Fori(0, BATCH) as b:
                    body(b)

            def rows(b):
                return x[:, bass.ds(b * TPB, TPB), :]

            @block.sync
            def _(sp):
                sp.dma_start(w[:, :], self.a["L0_attn_a_proj_w"]).then_inc(q["w"], 16)
                sp.dma_start(pb[:, 0, :], self.a["L0_attn_a_proj_b"].rearrange("(a n) -> a n", a=1)
                             .broadcast_to([P, P])).then_inc(q["w"], 16)

            @block.gpsimd
            def _(pool):
                pool.wait_ge(q["w"], 32)

                def add_bias(b):
                    pool.tensor_tensor(rows(b), rows(b), pb[:, :, :].broadcast_to([P, TPB, P]), ALU.add).then_inc(q["xb"], 1)

                batches(pool, add_bias)

            @block.scalar
            def _(act):
                act.preload_act_table(ACT.Sigmoid)
                act.wait_ge(q["pw"], 1)
                act.activation(pw[:, :, :], psW[:, :, :], ACT.Copy).then_inc(q["pwc"], 1)
                act.sem_inc(q["gu"], 4)

                def body(b):
                    act.wait_ge(q["gu"], b * 4 + 4)
                    act.activation(qh[:, :], qkT[:, 0, bass.ds(b * SEQ, SEQ)], ACT.Copy).then_inc(q["qh"], 1)
                    for n in range(NC):
                        act.wait_ge(q["gu"], b * 4 + n + 5)
                        act.wait_ge(q["sw"], b * 4 + n + 1)
                        act.activation(sg[:, n % 2, :], psG[:, n % 2, :], ACT.Sigmoid).then_inc(q["sig"], 1)

                batches(act, body)

            @block.tensor
            def _(pe):
                pe.wait_ge(q["w"], 32)
                for n in range(NC):
                    last = pe.matmul(psW[:, n, :], self.projT[:, n * P:n * P + P], w[:, :], start=True, stop=True)
                last.then_inc(q["pw"], 1)
                pe.wait_ge(q["pwc"], 1)

                def gate_up(b, n):
                    pe.wait_ge(q["h"], b * 4 + n + 1)
                    for half, ps_ in ((0, psG), (1, psU)):
                        cols = slice(half * HID + n * P, half * HID + n * P + P)
                        last = mm3(pe, ps_[:, n % 2, :], self.gvh[:, cols], self.gvl[:, cols], qh[:, :], ql[:, :])
                    last.then_inc(q["gu"], 1)

                def output(b):
                    pe.wait_ge(q["h"], b * 4 + 4 + 2)
                    pe.wait_ge(q["x"], b + 1)
                    for t in range(TPB):
                        for n in range(NC):
                            last = pe.matmul(psO[:, t, :], hT[:, n, t * P:t * P + P], pw[:, n, :],
                                             start=(n == 0), stop=(n == NC - 1))
                    last.then_inc(q["o"], 1)

                def body(b, before):
                    pe.wait_ge(q["ql"], b + 1)
                    gate_up(b, 0)
                    if before:
                        output(b - 1)
                    for n in range(1, NC):
                        gate_up(b, n)

                body(0, False)
                with pe.Fori(1, BATCH) as b:
                    body(b, True)
                output(BATCH - 1)

            @block.vector
            def _(dve):
                dve.sem_inc(q["sw"], 2)
                dve.sem_inc(q["h"], 2)
                dve.sem_inc(q["x"], 1)
                dve.sem_inc(q["o"], 1)

                def low(b):
                    dve.wait_ge(q["qh"], b + 1)
                    dve.tensor_tensor(ql[:, :], qkT[:, 0, bass.ds(b * SEQ, SEQ)], qh[:, :].bitcast(F32), ALU.subtract).then_inc(q["ql"], 1)

                def chunks(b):
                    for n in range(NC):
                        dve.wait_ge(q["sig"], b * 4 + n + 1)
                        dve.wait_ge(q["h"], b * 4 + n + 1)
                        dve.tensor_tensor(sw[:, n % 2, :], psG[:, n % 2, :], sg[:, n % 2, :], ALU.mult).then_inc(q["sw"], 1)
                        dve.wait_ge(q["sw"], b * 4 + n + 3)
                        if n == 0:
                            dve.wait_ge(q["o"], b + 1)
                        dve.tensor_tensor(hT[:, n, :], psU[:, n % 2, :], sw[:, n % 2, :], ALU.mult).then_inc(q["h"], 1)

                def add(b):
                    dve.wait_ge(q["o"], b + 2)
                    dve.wait_ge(q["xb"], b + 1)
                    dve.tensor_tensor(rows(b), rows(b), psO[:, :, :], ALU.add).then_inc(q["x"], 1)
                    dve.wait_ge(q["x"], b + 2)
                    for n in range(TPB):
                        self.take_stats(dve, b * TPB + n)

                low(0)
                chunks(0)
                with dve.Fori(1, BATCH) as b:
                    low(b)
                    chunks(b)
                    add(b - 1)
                add(BATCH - 1)


    def moe_phase(self, nth):
        nc, x, ident = self.nc, self.x, self.ident
        own = []

        def sem(n):
            own.append(nc.alloc_semaphore(f"m{nth}_{n}"))
            return own[-1]

        s_var, s_root, s_ln = sem("var"), sem("root"), sem("ln")
        s_xn, s_xT, s_xTs, s_keep, s_L, s_l = (sem(n) for n in ("xn", "xT", "xTs", "keep", "L", "l"))
        s_sh, s_e, s_c, s_wT, s_wTs, s_B, s_xb = (sem(n) for n in ("sh", "e", "c", "wT", "wTs", "B", "xb"))
        s_hi, s_lo, s_E, s_y, s_z, s_z2, s_z3, s_x, s_out = (sem(n) for n in ("hi", "lo", "E", "y", "z", "z2", "z3", "x", "out"))
        s_prio, s_w = sem("prio"), sem("w")
        ACT_E = 4
        with ExitStack() as c:
            sb = lambda n, s, d=F32: c.enter_context(nc.sbuf_tensor(f"m{nth}_{n}_", s, d))
            ps = lambda n, s, d=F32: c.enter_context(nc.psum_tensor(f"m{nth}_{n}_", s, d))
            weh, wel, wg, bg, beh, bel = self.weh, self.wel, self.wg, self.bg, self.beh, self.bel
            xn, xTs, xnT = sb("xn", [P, 2, TPB, P]), sb("xTs", [P, 2, SEQ]), sb("xnT", [P, TOK])
            prio, logit, gate, gate2, eq, sel, sel2, wt = (sb(n, [P, NT, NE]) for n in
                                                           ("prio", "logit", "gate", "gate2", "eq", "sel", "sel2", "wt"))
            m1, m2, pm, tot, rtot = (sb(n, [P, NT]) for n in ("m1", "m2", "pm", "tot", "rtot"))
            wTh, wTl = sb("wTh", [P, P], F32R), sb("wTl", [P, P], F32R)
            xh, xl = sb("xh", [P, 2, P], F32R), sb("xl", [P, 2, P], F32R)
            y, z, z2, z3 = sb("y", [P, 2, NE * P]), sb("z", [P, 2, 4 * P]), sb("z2", [P, 2, 2 * P]), sb("z3", [P, 2, P])
            psT, psL = ps("T", [P, 2, 512]), ps("L", [P, 2, 512])
            psE = ps("E", [P, 2, NE * P])
            block = c.enter_context(nc.Block())
            tile = lambda t: bass.ds(t.i * 2 + t.j, 1)

            @block.sync
            def _(sp):
                if nth == 1:
                    dst = self.out.rearrange("b (t p) d -> p (b t) d", p=P)
                    for g in range(BATCH):
                        sp.wait_ge(s_x, (g + 1) * TPB + 2)
                        sp.dma_start(dst[:, g * TPB:(g + 1) * TPB, :], x[:, g * TPB:(g + 1) * TPB, :]).then_inc(s_out, 16)
                    sp.wait_ge(s_out, 16 * BATCH)

            @block.gpsimd
            def _(pool):
                for n in range(NE):
                    last = pool.memset(prio[:, :, n:n + 1], float(NE - n))
                last.then_inc(s_prio, 1)
                pool.sem_inc(s_keep, 2)

                def keep(g):
                    pool.wait_ge(s_xTs, g.done())
                    split = lambda ap: ap.rearrange("p (t d) -> p t d", d=P)
                    pool.tensor_tensor(split(xnT[:, g.cols(SEQ)]), split(xTs[:, g.ring, :]),
                                       self.ones[:, :].unsqueeze(1).broadcast_to([P, TPB, P]), ALU.mult).then_inc(s_keep, 1)

                pipeline(pool, (0, keep), count=BATCH)()

                def add_half(t):
                    pool.wait_ge(s_y, t.done() + 2)
                    pool.wait_ge(s_w, t.done() + 2)
                    pool.wait_ge(s_z2, t.done())
                    pool.tensor_tensor(z[:, t.ring, :], y[:, t.ring, 0:4 * P], y[:, t.ring, 4 * P:8 * P], ALU.add).then_inc(s_z, 1)

                pool.sem_inc(s_z, 2)
                pipeline(pool, (2, add_half))()

            @block.scalar
            def _(act):
                self.ln_scalar(act, s_var, s_root)

                def copy(t):
                    act.wait_ge(s_xT, t.done() + 2)
                    act.wait_ge(s_keep, t.done())
                    act.wait_ge(s_L, t.done())
                    act.activation(xTs[:, t.ring, :], psT[:, t.ring, :], ACT.Copy).then_inc(s_xTs, 1)

                act.sem_inc(s_L, 2)
                pipeline(act, (0, copy), count=BATCH)()
                act.preload_act_table(ACT.Exp)
                act.wait_ge(s_sh, 1)
                act.activation(gate[:, :, :], logit[:, :, :], ACT.Exp).then_inc(s_e, 1)
                act.wait_ge(s_keep, BATCH + 2)

                def high(t):
                    act.wait_ge(s_E, t.done())
                    act.activation(xh[:, t.ring, :], xnT[:, t.cols()], ACT.Copy).then_inc(s_hi, 1)

                act.sem_inc(s_E, 2)

                def weights_high(t):
                    if isinstance(t.i, int) and t.j == 0:
                        act.wait_ge(s_wT, 1)
                        act.activation(wTh[:, :], psT[:, 0, 0:P], ACT.Copy).then_inc(s_wTs, 1)

                def weigh_last(t):
                    act.wait_ge(s_E, t.done() + 2)
                    act.wait_ge(s_z, t.done())
                    for n in range(NE - ACT_E, NE):
                        cols = slice(n * P, n * P + P)
                        last = act.activation(y[:, t.ring, cols], psE[:, t.ring, cols], ACT.Copy,
                                              scale=wt[:, tile(t), n:n + 1].rearrange("p a e -> p (a e)"))
                    last.then_inc(s_w, 1)

                act.sem_inc(s_w, 2)
                pipeline(act, (0, high), (1, weights_high), (2, weigh_last))()

            @block.tensor
            def _(pe):
                def turn(t):
                    pe.wait_ge(s_xn, t.done())
                    if t.j > 1 or not isinstance(t.i, int):
                        pe.wait_ge(s_xTs, t.done(-1))
                    for n in range(TPB):
                        last = pe.transpose(psT[:, t.ring, n * P:n * P + P], xn[:, t.ring, n, :], ident[:, :])
                    last.then_inc(s_xT, 1)

                def logits(t):
                    pe.wait_ge(s_xTs, t.done())
                    pe.wait_ge(s_l, t.done())
                    for n in range(TPB):
                        last = pe.matmul(psL[:, t.ring, n * NE:n * NE + NE], xTs[:, t.ring, n * P:n * P + P], wg[:, :],
                                         start=True, stop=True)
                    last.then_inc(s_L, 1)

                def weights(t):
                    if isinstance(t.i, int) and t.j == 0:
                        pe.wait_ge(s_c, 1)
                        pe.transpose(psT[:, 0, 0:P], wt[:, :, :].rearrange("p t e -> p (t e)"), ident[:, :]).then_inc(s_wT, 1)
                        pe.wait_ge(s_wTs, 2)
                        for n, bank in enumerate((psT[:, 1, :], psL[:, 0, :], psL[:, 1, :], psT[:, 0, :])):
                            cols = slice(n * SEQ, n * SEQ + SEQ)
                            last = mm3(pe, bank, wTh[:, :], wTl[:, :], beh[:, cols], bel[:, cols])
                        last.then_inc(s_B, 1)

                pipeline(pe, (0, turn), (1, logits), count=BATCH)()

                def experts(t):
                    pe.wait_ge(s_lo, t.done())
                    pe.wait_ge(s_y, t.done())
                    pe.wait_ge(s_w, t.done())
                    for half in range(2):
                        cols = slice(half * 512, half * 512 + 512)
                        last = mm3(pe, psE[:, t.ring, cols], xh[:, t.ring, :], xl[:, t.ring, :], weh[:, cols], wel[:, cols])
                    last.then_inc(s_E, 1)

                pipeline(pe, (0, experts), (1, weights))()

            @block.vector
            def _(dve):
                n = self.ln_vector(dve, s_var, s_root, s_ln)
                dve.sem_inc(s_xT, 2)
                dve.sem_inc(s_l, 2)

                def norm(t):
                    dve.wait_ge(s_xT, t.done())
                    for n in range(TPB):
                        r = bass.ds(t.i * (2 * TPB) + t.j * TPB + n, 1)
                        last = dve.tensor_scalar(xn[:, t.ring, n, :], x[:, r, :].rearrange("p a d -> p (a d)"), self.mean[:, r],
                                                 self.rstd[:, r], ALU.subtract, ALU.mult)
                    last.then_inc(s_xn, 1)

                def bias(t):
                    dve.wait_ge(s_L, t.done() + 2)
                    dve.tensor_tensor(logit[:, bass.ds(t.i * (2 * TPB) + t.j * TPB, TPB), :],
                                      psL[:, t.ring, 0:TPB * NE].rearrange("p (t e) -> p t e", e=NE),
                                      bg[:, :, :].broadcast_to([P, TPB, NE]), ALU.add).then_inc(s_l, 1)

                pipeline(dve, (0, norm), (2, bias), count=BATCH)()
                wide = lambda ap: ap[:, :].unsqueeze(2).broadcast_to([P, NT, NE])
                g = Chain(dve, s_ln, n)
                dve.wait_ge(s_l, BATCH + 2)
                g(dve.tensor_reduce(m1[:, :], logit[:, :, :], AX.X, ALU.max))
                dve.tensor_tensor(logit[:, :, :], logit[:, :, :], wide(m1), ALU.subtract).then_inc(s_sh, 1)
                dve.wait_ge(s_e, 1)
                g(dve.tensor_reduce(tot[:, :], gate[:, :, :], AX.X, ALU.add))
                g(dve.reciprocal(rtot[:, :], tot[:, :]))
                g(dve.tensor_tensor(gate[:, :, :], gate[:, :, :], wide(rtot), ALU.mult))
                dve.wait_ge(s_prio, 1)

                def best(m, src, chosen):
                    g(dve.tensor_reduce(m[:, :], src[:, :, :], AX.X, ALU.max))
                    g(dve.tensor_tensor(eq[:, :, :], src[:, :, :], wide(m), ALU.is_equal))
                    g(dve.tensor_tensor(eq[:, :, :], eq[:, :, :], prio[:, :, :], ALU.mult))
                    g(dve.tensor_reduce(pm[:, :], eq[:, :, :], AX.X, ALU.max))
                    g(dve.tensor_tensor(chosen[:, :, :], eq[:, :, :], wide(pm), ALU.is_equal))

                best(m1, gate, sel)
                g(dve.scalar_tensor_tensor(gate2[:, :, :], sel[:, :, :], -2.0, gate[:, :, :], ALU.mult, ALU.add))
                best(m2, gate2, sel2)
                g(dve.tensor_tensor(tot[:, :], m1[:, :], m2[:, :], ALU.add))
                g(dve.reciprocal(rtot[:, :], tot[:, :]))
                g(dve.tensor_tensor(sel[:, :, :], sel[:, :, :], sel2[:, :, :], ALU.add))
                g(dve.tensor_tensor(sel[:, :, :], sel[:, :, :], gate[:, :, :], ALU.mult))
                dve.tensor_tensor(wt[:, :, :], sel[:, :, :], wide(rtot), ALU.mult).then_inc(s_c, 1)
                dve.wait_ge(s_c, 1)
                dve.sem_inc(s_y, 2)
                dve.sem_inc(s_z2, 2)
                dve.sem_inc(s_z3, 2)
                dve.sem_inc(s_x, 2)

                def low(t):
                    dve.wait_ge(s_hi, t.done())
                    dve.tensor_tensor(xl[:, t.ring, :], xnT[:, t.cols()], xh[:, t.ring, :].bitcast(F32), ALU.subtract).then_inc(s_lo, 1)

                def add_bias(t):
                    if isinstance(t.i, int) and t.j == 0:
                        dve.wait_ge(s_wTs, 1)
                        dve.tensor_tensor(wTl[:, :], psT[:, 0, 0:P], wTh[:, :].bitcast(F32), ALU.subtract).then_inc(s_wTs, 1)
                    if isinstance(t.i, int) and t.j == 2:
                        dve.wait_ge(s_B, 1)
                        for n, bank in enumerate((psT[:, 1, :], psL[:, 0, :], psL[:, 1, :], psT[:, 0, :])):
                            rows = x[:, n * TPB:(n + 1) * TPB, :].rearrange("p t d -> p (t d)")
                            last = dve.tensor_tensor(rows, bank, rows, ALU.add)
                        last.then_inc(s_xb, 1)

                def weigh(t):
                    dve.wait_ge(s_E, t.done() + 2)
                    dve.wait_ge(s_z, t.done())
                    first, cols = NE - ACT_E, slice(0, (NE - ACT_E) * P)
                    dve.tensor_tensor(y[:, t.ring, cols].rearrange("p (e o) -> p e o", o=P),
                                      psE[:, t.ring, cols].rearrange("p (e o) -> p e o", o=P),
                                      wt[:, tile(t), 0:first].rearrange("p a e -> p (a e)").unsqueeze(2).broadcast_to([P, first, P]),
                                      ALU.mult).then_inc(s_y, 1)

                def add_quarter(t):
                    dve.wait_ge(s_z, t.done() + 2)
                    dve.wait_ge(s_z3, t.done())
                    dve.tensor_tensor(z2[:, t.ring, :], z[:, t.ring, 0:2 * P], z[:, t.ring, 2 * P:4 * P], ALU.add).then_inc(s_z2, 1)

                def add_eighth(t):
                    dve.wait_ge(s_z2, t.done() + 2)
                    dve.wait_ge(s_x, t.done())
                    dve.tensor_tensor(z3[:, t.ring, :], z2[:, t.ring, 0:P], z2[:, t.ring, P:2 * P], ALU.add).then_inc(s_z3, 1)

                def add_x(t):
                    dve.wait_ge(s_z3, t.done() + 2)
                    dve.wait_ge(s_xb, 1)
                    dve.tensor_tensor(x[:, tile(t), :], x[:, tile(t), :], z3[:, t.ring, :], ALU.add).then_inc(s_x, 1)

                def stats(t):
                    dve.wait_ge(s_x, t.done() + 2)
                    self.take_stats(dve, t.i * 2 + t.j)

                last = ((6, stats),) if nth == 0 else ()
                pipeline(dve, (0, low), (2, weigh), (1, add_bias), (3, add_quarter), (4, add_eighth), (5, add_x), *last)()

        if nth == 0:
            nc.clear_and_free_semaphores(own)
            nc.all_engine_barrier()


    def attention_phase(self):
        nc, x, ident = self.nc, self.x, self.ident
        names = ("kk xb var root ln cst xn xT xa xh xl V va vd wh wl pr qh kh ql kl S mx ex T ea ed PV nr "
                 "oT oTa oTd out res rs").split()
        t = {n: self.sem("t_" + n) for n in names}
        with ExitStack() as c:
            sb = lambda n, s, d=F32: c.enter_context(nc.sbuf_tensor("t_" + n + "_", s, d))
            ps = lambda n, s, d=F32: c.enter_context(nc.psum_tensor("t_" + n + "_", s, d))
            w, wvh, wvl, wout, bout, lng, lnb = self.wqkv, self.wvh, self.wvl, self.wout, self.bout, self.lng, self.lnb
            mask, identb = sb("mask", [P, P], BF16), sb("identb", [P, P], BF16)
            xn, xT = sb("xn", [P, TPB, P]), sb("xT", [P, SEQ])
            xh, xl = sb("xh", [P, SEQ], F32R), sb("xl", [P, SEQ], F32R)
            v, o = sb("v", [P, TPB, HEADS * DH]), sb("o", [P, TPB, HEADS * DH])
            oT = sb("oT", [P, NP, SEQ])
            wh, wl = sb("wh", [P, 2, 2 * DH], F32R), sb("wl", [P, 2, 2 * DH], F32R)
            qs, ks, kl = sb("qs", [P, 2, SEQ], F32R), sb("ks", [P, 2, SEQ], F32R), sb("kl", [DH, 2, SEQ], F32R)
            pr, pT = sb("p", [P, 8, SEQ]), sb("pT", [P, 4, TPB, P])
            nmax, rsum, rinv = sb("nmax", [P, 2, TPB]), sb("rsum", [P, 2, TPB]), sb("rinv", [P, 2, TPB])
            psS, psT, psO, psP = ps("S", [P, 4, 512]), ps("T", [P, 2, 512]), ps("O", [P, 512]), ps("P", [P, 512])
            ON_ACT = (2, 3)
            block = c.enter_context(nc.Block())
            flat = lambda ap: ap.rearrange("p a d -> p (a d)")

            def first(s):
                return isinstance(s.i, int) and 0 <= s.j < Slot.TURN

            def batches(e, body):
                body(0, False)
                with e.Fori(1, BATCH) as b:
                    body(b, True)

            @block.gpsimd
            def _(pool):
                g = Chain(pool, t["cst"])
                g(pool.memset(mask[:, :], 0.0))
                for n in range(P // FRAME - 1):
                    g(pool.memset(mask[n * FRAME:(n + 1) * FRAME, (n + 1) * FRAME:P], NEG))
                g(pool.tensor_copy(identb[:, :], ident[:, :]))
                pool.sem_inc(t["kk"], 1)

                def w_low(s):
                    if s.u == 0:
                        pool.wait_ge(t["wh"], s.head_done())
                        pool.wait_ge(t["kk"], s.head_done())
                        pool.tensor_tensor(wl[:, s.par, :].rearrange("p (a d) -> p a d", a=2),
                                           w[:, 0:2, :, :].rearrange("p a h d -> p a (h d)")[:, :, s.head_cols()],
                                           wh[:, s.par, :].bitcast(F32).rearrange("p (a d) -> p a d", a=2),
                                           ALU.subtract).then_inc(t["wl"], 1)

                def repeat_k(s):
                    if s.u == 2:
                        pool.wait_ge(t["kh"], s.head_done())
                        pool.wait_ge(t["wl"], s.head_done())
                        pool.tensor_tensor(ks[DH:P, s.par, :].rearrange("p (a d) -> p a d", d=P),
                                           ks[0:DH, s.par, :].bitcast(F32).rearrange("p (a d) -> p a d", d=P),
                                           self.ones[0:DH, :].unsqueeze(1).broadcast_to([DH, TPB, P]), ALU.mult).then_inc(t["kk"], 1)

                def body(b, before):
                    pool.wait_ge(t["xn"], b + 1)
                    rows = x[:, bass.ds(b * TPB, TPB), :]
                    pool.tensor_tensor(rows, rows, bout[:, :, :].broadcast_to([P, TPB, P]), ALU.add).then_inc(t["xb"], 1)
                    slots(pool, b, (-TPB - 1, w_low), (-TPB, repeat_k))

                batches(pool, body)

            @block.scalar
            def _(act):
                self.ln_scalar(act, t["var"], t["root"])
                act.preload_act_table(ACT.Exp)
                act.sem_inc(t["pr"], 2)

                def w_high(s):
                    if s.u == 0:
                        act.wait_ge(t["pr"], s.head_done())
                        act.activation(wh[:, s.par, :].rearrange("p (a d) -> p a d", a=2),
                                       w[:, 0:2, :, :].rearrange("p a h d -> p a (h d)")[:, :, s.head_cols()],
                                       ACT.Copy).then_inc(t["wh"], 1)

                def qk_high(s):
                    if s.u == 2:
                        act.wait_ge(t["pr"], s.head_done() + 2)
                        act.activation(qs[0:DH, s.par, :], psP[0:DH, :], ACT.Copy).then_inc(t["qh"], 1)
                        act.activation(ks[0:DH, s.par, :], psP[DH:P, :], ACT.Copy).then_inc(t["kh"], 1)

                def exps(s):
                    act.wait_ge(t["mx"], s.done())
                    if not isinstance(s.i, int) or s.j > 7:
                        act.wait_ge(t["T"], s.done(-7))
                        if s.u == 0:
                            act.wait_ge(t["rs"], s.head_done(-1))
                    act.activation(pr[:, s.j % 8, 0:s.keys], psS[:, s.j % 4, 0:s.keys], ACT.Exp,
                                   bias=nmax[:, s.par, s.qt:s.qt + 1],
                                   accum_out=rsum[:, s.par, s.qt:s.qt + 1]).then_inc(t["ex"], 1)

                def take_p(s):
                    if s.u in ON_ACT:
                        act.wait_ge(t["T"], s.done())
                        act.activation(flat(pT[:, s.j % 4, 0:s.qt + 1, :]), psT[:, s.j % 2, 0:s.keys], ACT.Copy).then_inc(t["ea"], 1)

                def take_o(b, n):
                    act.wait_ge(t["oT"], b * NP + n + 1)
                    act.activation(oT[:, n, :], psS[:, n % 4, :], ACT.Copy).then_inc(t["oTa"], 1)

                def body(b, before):
                    if before:
                        take_o(b - 1, 0)
                        take_o(b - 1, 2)
                    act.wait_ge(t["xT"], b + 1)
                    act.activation(xT[:, :], psP[:, :], ACT.Identity, bias=lnb[:, :], scale=lng[:, :]).then_inc(t["xa"], 1)
                    act.wait_ge(t["xa"], b + 1)
                    act.activation(xh[:, :], xT[:, :], ACT.Copy).then_inc(t["xh"], 1)
                    if before:
                        take_o(b - 1, 4)
                        take_o(b - 1, 6)
                    for n, bank in ((0, psT[:, :, :]), (2, psS[:, 2:4, :])):
                        act.wait_ge(t["V"], b * 4 + n + 1)
                        act.activation(v[:, n, :].rearrange("p (a d) -> p a d", a=2), bank, ACT.Copy).then_inc(t["va"], 1)
                    slots(act, b, (4, take_p), (-TPB - 1, w_high), (-TPB, qk_high), (1, exps))

                batches(act, body)
                for n in range(0, NP, 2):
                    take_o(BATCH - 1, n)

            @block.tensor
            def _(pe):
                pe.wait_ge(t["cst"], P // FRAME + 1)

                def project(s):
                    if s.u == 1:
                        pe.wait_ge(t["wl"], s.head_done())
                        pe.wait_ge(t["kl"], s.head_done() + 1)
                        mm3(pe, psP[:, :], wh[:, s.par, :], wl[:, s.par, :], xh[:, :], xl[:, :]).then_inc(t["pr"], 1)

                def scores(s):
                    if s.u == 0:
                        pe.wait_ge(t["kl"], s.head_done() + 2)
                        pe.wait_ge(t["kk"], s.head_done() + 1)
                    pe.wait_ge(t["ex"], s.done())
                    rows = slice(s.qt * P, s.qt * P + P)
                    n = max(s.keys, 2 * P)
                    out = psS[:, s.j % 4, 0:n]
                    pe.matmul(out, qs[:, s.par, rows], ks[:, s.par, 0:n], start=True, stop=False)
                    pe.matmul(out, qs[0:DH, s.par, rows], kl[:, s.par, 0:n], start=False, stop=False)
                    pe.matmul(psS[:, s.j % 4, s.keys - P:s.keys], identb[:, :], mask[:, :], start=False, stop=True).then_inc(t["S"], 1)

                def p_out(s):
                    on_act = s.u in ON_ACT
                    return t["ea" if on_act else "ed"], s.head_done(s.u % 2 + 1, 2)

                def turn(s):
                    pe.wait_ge(t["ex"], s.done() + 4)
                    if not isinstance(s.i, int) or s.j > 1:
                        pe.wait_ge(*p_out(Slot(s.b, s.i, s.j - 2)))
                    for n in range(s.qt + 1):
                        last = pe.transpose(psT[:, s.j % 2, n * P:n * P + P], pr[:, s.j % 8, n * P:n * P + P], ident[:, :])
                    last.then_inc(t["T"], 1)

                def weigh(s):
                    pe.wait_ge(*p_out(s))
                    if s.u == 0:
                        pe.wait_ge(t["nr"], s.head_done())
                    for n in range(s.qt + 1):
                        last = pe.matmul(psO[:, s.qt * DH:s.qt * DH + DH], pT[:, s.j % 4, n, :], v[:, n, s.head_cols()],
                                         start=(n == 0), stop=(n == s.qt))
                    last.then_inc(t["PV"], 1)

                def turn_o(b, n):
                    if n >= 4:
                        pe.wait_ge(t[("oTa", "oTd")[n % 2]], b * 4 + n // 2 - 1)
                    for m in range(TPB):
                        last = pe.transpose(psS[:, n % 4, m * P:m * P + P], o[:, m, n * P:n * P + P], ident[:, :])
                    last.then_inc(t["oT"], 1)

                def output(b, m):
                    for n in range(NP):
                        last = pe.matmul(psO[:, m * P:m * P + P], oT[:, n, m * P:m * P + P], wout[:, n, :],
                                         start=(n == 0), stop=(n == NP - 1))
                    last.then_inc(t["out"], 1)

                def body(b, before):
                    if before:
                        pe.wait_ge(t["nr"], b * HEADS + 1)
                        for n in range(4):
                            turn_o(b - 1, n)
                    pe.wait_ge(t["xn"], b + 1)
                    for n in range(TPB):
                        last = pe.transpose(psP[:, n * P:n * P + P], xn[:, n, :], ident[:, :])
                    last.then_inc(t["xT"], 1)
                    if before:
                        for n in range(4, NP):
                            turn_o(b - 1, n)
                    pe.wait_ge(t["xl"], b + 1)
                    for n, bank in enumerate((psT[:, :, :], psS[:, 0:2, :], psS[:, 2:4, :], psT[:, :, :])):
                        if before and n == 1:
                            pe.wait_ge(t["oTa"], b * 4)
                            pe.wait_ge(t["oTd"], b * 4)
                        if n == 3:
                            pe.wait_ge(t["va"], b * 2 + 1)
                        for half in range(2):
                            cols = slice(half * 512, half * 512 + 512)
                            last = mm3(pe, bank[:, half, :], xh[:, n * P:n * P + P], xl[:, n * P:n * P + P], wvh[:, cols], wvl[:, cols])
                        last.then_inc(t["V"], 1)

                    def last_output(s):
                        if before and first(s) and s.j < TPB:
                            output(b - 1, s.j)

                    def v_there(s):
                        if first(s) and s.j == 0:
                            pe.wait_ge(t["va"], b * 2 + 2)
                            pe.wait_ge(t["vd"], b * 2 + 2)

                    def out_added(s):
                        if before and first(s) and s.j == 0:
                            pe.wait_ge(t["res"], b)

                    slots(pe, b, (0, v_there), (0, scores), (-TPB, project), (3, turn), (5, out_added), (5, weigh),
                          (-TPB, last_output))

                batches(pe, body)
                pe.wait_ge(t["nr"], BATCH * HEADS + 1)
                for n in range(NP):
                    turn_o(BATCH - 1, n)
                pe.wait_ge(t["oTa"], BATCH * 4)
                pe.wait_ge(t["oTd"], BATCH * 4)
                for m in range(TPB):
                    output(BATCH - 1, m)

            @block.vector
            def _(dve):
                self.ln_vector(dve, t["var"], t["root"], t["ln"])
                dve.sem_inc(t["kl"], 2)
                dve.sem_inc(t["ex"], 4)
                dve.sem_inc(t["nr"], 1)

                def q_low(s):
                    if s.u == 2:
                        dve.wait_ge(t["kh"], s.head_done())
                        dve.tensor_tensor(qs[DH:P, s.par, :], psP[0:DH, :], qs[0:DH, s.par, :].bitcast(F32), ALU.subtract).then_inc(t["ql"], 1)

                def k_low(s):
                    if s.u == 2:
                        dve.tensor_tensor(kl[:, s.par, :], psP[DH:P, :], ks[0:DH, s.par, :].bitcast(F32), ALU.subtract).then_inc(t["kl"], 1)

                def row_max(s):
                    dve.wait_ge(t["S"], s.done())
                    dve.tensor_reduce(nmax[:, s.par, s.qt:s.qt + 1], psS[:, s.j % 4, 0:s.keys], AX.X, ALU.max, negate=True).then_inc(t["mx"], 1)

                def take_p(s):
                    if s.u not in ON_ACT:
                        dve.wait_ge(t["T"], s.done())
                        dve.tensor_copy(flat(pT[:, s.j % 4, 0:s.qt + 1, :]), psT[:, s.j % 2, 0:s.keys]).then_inc(t["ed"], 1)

                def invert(s):
                    if s.u == 3:
                        dve.wait_ge(t["ex"], s.done() + 4)
                        dve.reciprocal(rinv[:, s.par, :], rsum[:, s.par, :]).then_inc(t["rs"], 1)

                def norm(s):
                    if s.u == 3:
                        dve.wait_ge(t["PV"], s.done())
                        dve.wait_ge(t["rs"], s.head_done())
                        dve.tensor_tensor(o[:, :, s.head_cols()], psO[:, 0:TPB * DH].rearrange("p (t d) -> p t d", t=TPB),
                                          rinv[:, s.par, :].unsqueeze(2).broadcast_to([P, TPB, DH]), ALU.mult).then_inc(t["nr"], 1)

                def take_o(b, n):
                    dve.wait_ge(t["oT"], b * NP + n + 1)
                    dve.tensor_copy(oT[:, n, :], psS[:, n % 4, :]).then_inc(t["oTd"], 1)

                def add_output(b):
                    rows = flat(x[:, bass.ds(b * TPB, TPB), :])
                    dve.wait_ge(t["out"], b * TPB + TPB)
                    dve.wait_ge(t["xb"], b + 1)
                    dve.tensor_tensor(rows, rows, psO[:, :], ALU.add).then_inc(t["res"], 1)
                    dve.wait_ge(t["res"], b + 1)
                    for n in range(TPB):
                        self.take_stats(dve, b * TPB + n)

                def body(b, before):
                    for n in range(TPB):
                        r = bass.ds(b * TPB + n, 1)
                        last = dve.tensor_scalar(xn[:, n, :], x[:, r, :].rearrange("p a d -> p (a d)"), self.mean[:, r],
                                                 self.rstd[:, r], ALU.subtract, ALU.mult)
                    last.then_inc(t["xn"], 1)
                    if before:
                        take_o(b - 1, 1)
                        take_o(b - 1, 3)
                    dve.wait_ge(t["xh"], b + 1)
                    dve.tensor_tensor(xl[:, :], xT[:, :], xh[:, :].bitcast(F32), ALU.subtract).then_inc(t["xl"], 1)
                    if before:
                        take_o(b - 1, 5)
                        take_o(b - 1, 7)
                    for n, bank in ((1, psS[:, 0:2, :]), (3, psT[:, :, :])):
                        dve.wait_ge(t["V"], b * 4 + n + 1)
                        dve.tensor_copy(v[:, n, :].rearrange("p (a d) -> p a d", a=2), bank).then_inc(t["vd"], 1)

                    def add_last(s):
                        if before and first(s) and s.j == 0:
                            add_output(b - 1)

                    slots(dve, b, (6, norm), (4, take_p), (1 - TPB, k_low), (0, row_max), (3, invert), (-TPB, q_low), (1, add_last))

                batches(dve, body)
                for n in range(1, NP, 2):
                    take_o(BATCH - 1, n)
                add_output(BATCH - 1)


def hybrid_block_kernel(nc, *tensors):
    args, out = dict(zip(_INS, tensors)), tensors[len(_INS)]
    with ExitStack() as ctx:
        k = Kernel(nc, ctx, args, out)
        with ExitStack() as first:
            k.first_attention_tensors(first)
            k.qkv_phase()
            k.unit_phase()
            with ExitStack() as sums:
                k.acc = sums.enter_context(nc.psum_tensor("acc", [P, 3, NC, P], F32))
                for step in range(TTT_STEPS):
                    k.gradient_phase(step)
                    k.schulz_phase(step)
            k.query_phase()
        k.moe_phase(0)
        k.attention_phase()
        k.moe_phase(1)


_INS = ["L0_attn_a_x", "L0_attn_a_qkv_w", "L0_attn_a_qkv_b", "L0_attn_a_qn_scale", "L0_attn_a_qn_bias",
        "L0_attn_a_kn_scale", "L0_attn_a_kn_bias", "L0_attn_a_ttt_gate", "L0_attn_a_ttt_val", "L0_attn_a_ttt_proj",
        "L0_attn_a_proj_w", "L0_attn_a_proj_b", "L0_attn_b_g", "L0_attn_b_b", "L0_attn_b_w_qkv", "L0_attn_b_w_out",
        "L0_attn_b_b_out", "L0_ffn_We", "L0_ffn_be", "L0_ffn_Wg", "L0_ffn_bg"]
_OUTS = [((BATCH, SEQ, P), "float32")]


def kernel(**inputs):
    import numpy as _np
    import concourse.bacc as _bacc
    from concourse import mybir as _mybir
    from concourse.bass_utils import run_bass_kernel_spmd as _run

    nc = _bacc.Bacc("TRN2", target_bir_lowering=False, num_devices=1)
    arrays, args = {}, []
    for name in _INS:
        a = _np.ascontiguousarray(inputs[name])
        arrays[f"in_{name}_dram"] = a
        args.append(nc.dram_tensor(f"in_{name}_dram", a.shape, _mybir.dt.from_np(a.dtype), kind="ExternalInput").ap())
    for i, (shape, dtype) in enumerate(_OUTS):
        dt = _mybir.dt.from_np(_np.dtype(dtype))
        args.append(nc.dram_tensor(f"out_{i}_dram", shape, dt, kind="ExternalOutput").ap())
    hybrid_block_kernel(nc, *args)
    r = _run(nc, [arrays], core_ids=[0])
    return r.results[0]["out_0_dram"]
```

```python
from contextlib import ExitStack

import concourse.bass as bass
from concourse import mybir

F32 = mybir.dt.float32
F32R = mybir.dt.float32r
BF16 = mybir.dt.bfloat16
ALU = mybir.AluOpType
ACT = mybir.ActivationFunctionType
AX = mybir.AxisListType

P = 128
BATCH, SEQ = 4, 512
TOK = BATCH * SEQ
NT = TOK // P
TPB = SEQ // P
QH, QD = 16, 8
HID = 4 * P
NC = HID // P
TTT_STEPS = 2
LR = 0.1
NS_A, NS_B, NS_C = 3.4445, -4.775, 2.0315
LOSS_SCALE = 2.0 / (TOK * P)
HEADS, DH = 16, 64
NP = HEADS // 2
FRAME = 32
NE = 8
LN_EPS = 1e-5
NEG = -1e30


class Tile:

    def __init__(self, i, j, base=0):
        self.i, self.j, self.base = i, j, base
        self.ring = j % 2

    def done(self, n=1, k=1):
        return self.i * (2 * k) + (self.j * k + n + self.base * k)

    def cols(self, width=P):
        return bass.ds(self.i * (2 * width) + self.j * width, width)

    def number(self):
        return 2 * self.i + self.j if isinstance(self.i, int) else None


def each_tile(e, body, base=0):
    with e.Fori(0, NT // 2) as i:
        for j in range(2):
            body(Tile(i, j, base))


def pipeline(e, *stages, count=NT):
    last = max(lag for lag, _ in stages)
    start = last + last % 2

    def turn(i, j, base):
        for lag, step in stages:
            if i is not None or 0 <= j - lag < count:
                step(Tile(0 if i is None else i, j - lag, base))

    def run(base=0):
        for s in range(start):
            turn(None, s, base)
        if start < count:
            with e.Fori(start // 2, count // 2) as i:
                for j in range(2):
                    turn(i, j, base)
        for s in range(max(start, count), count + last):
            turn(None, s, base)

    return run


class Slot:

    N = HEADS * TPB
    TURN = 2 * TPB

    def __init__(self, b, i, j):
        self.b, self.i, self.j = b, i, j
        self.u = j % TPB
        self.qt = TPB - 1 - self.u
        self.par = (j // TPB) % 2
        self.keys = (self.qt + 1) * P

    def done(self, n=1):
        return self.i * self.TURN + self.b * self.N + (self.j + n)

    def head_done(self, n=1, k=1):
        return self.i * (2 * k) + self.b * (HEADS * k) + ((self.j // TPB) * k + n)

    def head_cols(self):
        return bass.ds(self.i * (2 * DH) + (self.j // TPB) * DH, DH)


def slots(e, b, *stages):
    lags = [lag for lag, _ in stages]
    first = -(-max(lags) // Slot.TURN)
    last = (Slot.N + min(0, min(lags))) // Slot.TURN

    def at(i, s, whole):
        for lag, step in stages:
            if whole or 0 <= s - lag < Slot.N:
                step(Slot(b, i, s - lag))

    for s in range(min(0, min(lags)), first * Slot.TURN):
        at(0, s, False)
    with e.Fori(first, last) as i:
        for j in range(Slot.TURN):
            at(i, j, True)
    for s in range(last * Slot.TURN, Slot.N + max(lags)):
        at(0, s, False)


class Chain:

    def __init__(self, e, sem, start=0):
        self.e, self.sem, self.n = e, sem, start

    def __call__(self, ins):
        ins.then_inc(self.sem, 1)
        self.n += 1
        self.e.wait_ge(self.sem, self.n)
        return self.n


def mm3(e, out, ah, al, bh, bl, start=True, stop=True):
    e.matmul(out, ah, bh, start=start, stop=False)
    e.matmul(out, ah, bl, start=False, stop=False)
    return e.matmul(out, al, bh, start=False, stop=stop)


class Kernel:
    def __init__(self, nc, ctx, args, out):
        self.nc, self.ctx = nc, ctx
        self.a, self.out = args, out
        sb, ps = self.sb, self.ps
        self.x = sb("x", [P, NT, P])
        self.ident = sb("ident", [P, P])
        self.ones = sb("ones", [P, P])
        self.mean = sb("mean", [P, NT])
        self.rstd = sb("rstd", [P, NT])
        self.stats = sb("stats", [P, NT, 6])
        self.lnw = sb("lnw", [P, 4, NT])
        self.we = sb("we", [P, NE * P])
        self.weh, self.wel = sb("weh", [P, NE * P], F32R), sb("wel", [P, NE * P], F32R)
        self.wg, self.bg = sb("wg", [P, NE]), sb("bg", [NE, 1])
        self.beh, self.bel = sb("beh", [P, NT * P], F32R), sb("bel", [P, NT * P], F32R)
        self.wqkv = sb("wqkv", [P, 3, HEADS, DH])
        self.wvh, self.wvl = sb("wvh", [P, HEADS * DH], F32R), sb("wvl", [P, HEADS * DH], F32R)
        self.wout, self.bout = sb("wout", [P, NP, P]), sb("bout", [P, 1, P])
        self.lng, self.lnb = sb("lng", [P, 1]), sb("lnb", [P, 1])
        self.factor = sb("factor", [P, P])
        self.s_late, self.s_bias, self.s_parts = self.sem("late"), self.sem("bias"), self.sem("parts")
        self.gradient_sems()
        self.schulz_sems()

    def first_attention_tensors(self, ctx):
        sb = lambda name, shape, dt=F32: ctx.enter_context(self.nc.sbuf_tensor(name, shape, dt))
        self.qkv = sb("qkv", [P, NT, 3 * P])
        self.qkT = sb("qkT", [P, 2, TOK])
        self.ssq = sb("ssq", [P, NT * 2 * QH])
        self.gv = sb("gv", [P, 2 * HID])
        self.gvh, self.gvl = sb("gvh", [P, 2 * HID], F32R), sb("gvl", [P, 2 * HID], F32R)
        self.proj, self.projT = sb("proj", [P, NC, P]), sb("projT", [P, HID])
        self.pTh, self.pTl = sb("pTh", [P, HID], F32R), sb("pTl", [P, HID], F32R)
        self.zeros = sb("zeros", [P, HID], BF16)
        self.be = sb("be", [P, NT, P])
        self.pw, self.pb = sb("proj_w", [P, P]), sb("proj_b", [P, 1, P])

    def sb(self, name, shape, dt=F32):
        return self.ctx.enter_context(self.nc.sbuf_tensor(name, shape, dt))

    def ps(self, name, shape, dt=F32):
        return self.ctx.enter_context(self.nc.psum_tensor(name, shape, dt))

    def sem(self, name):
        return self.ctx.enter_context(self.nc.semaphore(name))

    def take_stats(self, e, tile):
        return e.bn_stats(self.stats[:, bass.ds(tile, 1), :], self.x[:, bass.ds(tile, 1), :])

    def ln_vector(self, e, s_var, s_root, s_ln):
        st, w = self.stats, self.lnw
        c = Chain(e, s_ln)
        c(e.tensor_tensor(w[:, 0, :], st[:, :, 1], st[:, :, 4], ALU.subtract))
        c(e.tensor_tensor(w[:, 1, :], w[:, 0, :], w[:, 0, :], ALU.mult))
        c(e.tensor_tensor(w[:, 2, :], st[:, :, 2], st[:, :, 5], ALU.add))
        c(e.scalar_tensor_tensor(w[:, 3, :], w[:, 1, :], P / 4.0, w[:, 2, :], ALU.mult, ALU.add))
        c(e.tensor_scalar(w[:, 3, :], w[:, 3, :], 1.0 / P, LN_EPS, ALU.mult, ALU.add))
        e.sem_inc(s_var, 1)
        c(e.tensor_tensor(w[:, 0, :], st[:, :, 1], st[:, :, 4], ALU.add))
        c(e.tensor_scalar(self.mean[:, :], w[:, 0, :], 0.5, None, ALU.mult))
        e.wait_ge(s_root, 1)
        c(e.reciprocal(self.rstd[:, :], w[:, 1, :]))
        return c.n

    def ln_scalar(self, e, s_var, s_root):
        e.preload_act_table(ACT.Sqrt)
        e.wait_ge(s_var, 1)
        e.activation(self.lnw[:, 1, :], self.lnw[:, 3, :], ACT.Sqrt).then_inc(s_root, 1)

    def qkv_phase(self):
        nc, sem = self.nc, self.sem
        x, qkv, qkT, ident, ssq = self.x, self.qkv, self.qkT, self.ident, self.ssq
        s_x = [sem(f"p_x{g}") for g in range(BATCH)]
        s_w, s_unit, s_fast, s_cst = sem("p_w"), sem("p_unit"), sem("p_fast"), sem("p_cst")
        s_stat, s_var, s_root, s_ln, s_shift = (sem("p_" + n) for n in ("stat", "var", "root", "ln", "shift"))
        s_xn, s_xT, s_xTs, s_qkv, s_out, s_sq, s_ss, s_rt, s_gd, s_inv, s_m, s_s, s_b, s_T, s_e, s_k = (
            sem("p_" + n) for n in "xn xT xTs qkv out sq ss rt gd inv m s b T e k".split())
        s_pt, s_ptc, s_pre = sem("p_pt"), sem("p_ptc"), sem("p_pre")
        with ExitStack() as c:
            sb = lambda n, s, d=F32: c.enter_context(nc.sbuf_tensor("p_" + n + "_", s, d))
            ps = lambda n, s, d=F32: c.enter_context(nc.psum_tensor("p_" + n + "_", s, d))
            w, bias = sb("w", [P, 3 * P]), sb("bias", [P, 3 * P])
            scale, shift_ = sb("scale", [P, 2, QD]), sb("shift", [P, 2, QD])
            scale_all, shift_all = sb("scale_all", [P, 2 * P]), sb("shift_all", [P, 2 * P])
            xn, xTs = sb("xn", [P, 2, P]), sb("xTs", [P, 2, P])
            nmr = sb("nmr", [P, NT])
            inv = sb("inv", [P, NT * 2 * QH])
            sq, m, sc, u = (sb(n, [P, 2, 2 * P]) for n in ("sq", "m", "sc", "u"))
            psX = [ps(f"X{r}", [P, P]) for r in range(2)]
            psQ = [ps(f"Q{r}", [P, 3 * P]) for r in range(2)]
            psT = [ps(f"T{r}", [P, 2, P]) for r in range(2)]
            psP = ps("P", [P, NC, P])
            block = c.enter_context(nc.Block())
            xsrc = self.a["L0_attn_a_x"].rearrange("b (t p) d -> p (b t) d", p=P)
            row = lambda name: self.a[name].rearrange("(a n) -> a n", a=1)
            tile = lambda t: bass.ds(t.i * 2 + t.j, 1)
            heads = lambda t: bass.ds(t.i * (4 * QH) + t.j * (2 * QH), 2 * QH)

            @block.sync
            def _(sp):
                for g in range(BATCH):
                    sp.dma_start(x[:, TPB * g:TPB * (g + 1), :], xsrc[:, TPB * g:TPB * (g + 1), :]).then_inc(s_x[g], 16)
                sp.dma_start(w[:, :], self.a["L0_attn_a_qkv_w"]).then_inc(s_w, 16)
                sp.dma_start(bias[:, :], row("L0_attn_a_qkv_b").broadcast_to([P, 3 * P])).then_inc(s_w, 16)
                sp.dma_start(self.proj[:, :, :], self.a["L0_attn_a_ttt_proj"].rearrange("(c p) d -> p c d", p=P)).then_inc(s_fast, 16)
                for n, name in enumerate(("qn", "kn")):
                    for dst, what in ((scale, "scale"), (shift_, "bias")):
                        sp.dma_start(dst[:, n, :], row(f"L0_attn_a_{name}_{what}").broadcast_to([P, QD])).then_inc(s_unit, 16)
                sp.dma_start(self.gv[:, 0:HID], self.a["L0_attn_a_ttt_gate"]).then_inc(s_unit, 16)
                sp.dma_start(self.gv[:, HID:2 * HID], self.a["L0_attn_a_ttt_val"]).then_inc(s_unit, 16)

            @block.gpsimd
            def _(pool):
                pool.memset(self.ones[:, :], 1.0).then_inc(s_cst, 1)
                pool.memset(ident[:, :], 0.0).then_inc(s_cst, 1)
                pool.wait_ge(s_cst, 2)
                pool.affine_select(out=ident[:, :], in_=ident[:, :], compare_op=ALU.not_equal, fill=1.0, base=0,
                                   pattern=[[-1, P]], channel_multiplier=1).then_inc(s_cst, 1)
                pool.memset(self.be[:, :, :], 0.0).then_inc(self.s_bias, 1)
                pool.memset(self.factor[:, :], DH ** -0.5).then_inc(self.s_bias, 1)
                pool.wait_ge(s_cst, 3)
                pool.wait_ge(s_unit, 6 * 16)
                g = Chain(pool, s_pre)
                per_head = lambda ap, n: ap[:, n * P:n * P + P].rearrange("p (g d) -> p g d", d=QD)
                for dst, src in ((scale_all, scale), (shift_all, shift_)):
                    for n in range(2):
                        g(pool.tensor_tensor(per_head(dst, n), per_head(self.ones, 0), src[:, n:n + 1, :].broadcast_to([P, QH, QD]), ALU.mult))
                wide = lambda ap: ap.rearrange("p (a d) -> p a d", d=P)
                g(pool.tensor_tensor(wide(self.gvh[:, :]), wide(self.gv[:, :]),
                                     self.ones[:, :].unsqueeze(1).broadcast_to([P, 2 * NC, P]), ALU.mult))
                g(pool.tensor_tensor(self.gvl[:, :], self.gv[:, :], self.gvh[:, :].bitcast(F32), ALU.subtract))
                pool.wait_ge(s_ptc, 2)
                g(pool.tensor_tensor(self.pTl[:, :], self.projT[:, :], self.pTh[:, :].bitcast(F32), ALU.subtract))
                pool.sem_inc(s_s, 2)
                pool.sem_inc(s_b, 2)

                def unit(t):
                    pool.wait_ge(s_inv, t.done())
                    pool.wait_ge(s_s, t.done())
                    pool.tensor_tensor(m[:, t.ring, :].rearrange("p (g d) -> p g d", d=QD),
                                       qkv[:, tile(t), 0:2 * P].rearrange("p a (g d) -> p (a g) d", d=QD),
                                       inv[:, heads(t)].unsqueeze(2).broadcast_to([P, 2 * QH, QD]), ALU.mult).then_inc(s_m, 1)

                def scaled(t):
                    pool.wait_ge(s_m, t.done())
                    pool.wait_ge(s_b, t.done())
                    pool.tensor_tensor(sc[:, t.ring, :], m[:, t.ring, :], scale_all[:, :], ALU.mult).then_inc(s_s, 1)

                pipeline(pool, (0, unit), (1, scaled))()

            @block.scalar
            def _(act):
                act.preload_act_table(ACT.Sqrt)
                act.wait_ge(s_pt, 1)
                act.activation(self.projT[:, :], psP[:, :, :].rearrange("p c d -> p (c d)"), ACT.Copy).then_inc(s_ptc, 1)
                act.activation(self.pTh[:, :], psP[:, :, :].rearrange("p c d -> p (c d)"), ACT.Copy).then_inc(s_ptc, 1)
                self.ln_scalar(act, s_var, s_root)
                act.wait_ge(s_shift, 1)

                def norm(t):
                    act.wait_ge(s_xT, t.done())
                    act.activation(xn[:, t.ring, :], x[:, tile(t), :].rearrange("p a d -> p (a d)"), ACT.Identity,
                                   bias=nmr[:, tile(t)], scale=self.rstd[:, tile(t)]).then_inc(s_xn, 1)

                def copy(t):
                    act.wait_ge(s_xT, t.done() + 2)
                    act.activation(xTs[:, t.ring, :], psX[t.ring][:, :], ACT.Copy).then_inc(s_xTs, 1)

                def square(t):
                    act.wait_ge(s_out, t.done() + 2)
                    act.wait_ge(s_ss, t.done())
                    act.activation(sq[:, t.ring, :], qkv[:, tile(t), 0:2 * P], ACT.Square).then_inc(s_sq, 1)

                def root(t):
                    act.wait_ge(s_ss, t.done() + 2)
                    act.activation(ssq[:, heads(t)], ssq[:, heads(t)], ACT.Sqrt).then_inc(s_rt, 1)

                def take(t):
                    act.wait_ge(s_T, t.done() + 2)
                    act.activation(qkT[:, :, t.cols()], psT[t.ring][:, :, :], ACT.Copy).then_inc(s_e, 1)

                def keep(t):
                    act.wait_ge(s_b, t.done() + 2)
                    act.activation(qkv[:, tile(t), P:2 * P], u[:, t.ring, P:2 * P], ACT.Copy).then_inc(s_k, 1)

                act.sem_inc(s_e, 2)
                act.sem_inc(s_k, 2)
                pipeline(act, (0, norm), (1, copy), (3, square), (4, root), (9, take), (9, keep))()

            @block.tensor
            def _(pe):
                pe.wait_ge(s_cst, 3)
                pe.wait_ge(s_fast, 16)
                for n in range(NC):
                    last = pe.transpose(psP[:, n, :], self.proj[:, n, :], ident[:, :])
                last.then_inc(s_pt, 1)
                pe.wait_ge(s_w, 32)

                def turn_x(t):
                    pe.wait_ge(s_xn, t.done())
                    pe.transpose(psX[t.ring][:, :], xn[:, t.ring, :], ident[:, :]).then_inc(s_xT, 1)

                def project(t):
                    pe.wait_ge(s_xTs, t.done())
                    pe.wait_ge(s_out, t.done())
                    pe.matmul(psQ[t.ring][:, :], xTs[:, t.ring, :], w[:, :], start=True, stop=True).then_inc(s_qkv, 1)

                def turn(t):
                    pe.wait_ge(s_b, t.done() + 2)
                    pe.wait_ge(s_e, t.done())
                    pe.transpose(psT[t.ring][:, 0, :], u[:, t.ring, 0:P], ident[:, :])
                    pe.transpose(psT[t.ring][:, 1, :], u[:, t.ring, P:2 * P], ident[:, :]).then_inc(s_T, 1)

                pipeline(pe, (0, turn_x), (1, project), (8, turn))()

            @block.vector
            def _(dve):
                for g in range(BATCH):
                    dve.wait_ge(s_x[g], 16)
                    for n in range(TPB):
                        self.take_stats(dve, g * TPB + n).then_inc(s_stat, 1)
                dve.wait_ge(s_stat, NT)
                self.ln_vector(dve, s_var, s_root, s_ln)
                dve.scalar_tensor_tensor(nmr[:, :], self.mean[:, :], -1.0, self.rstd[:, :], ALU.mult, ALU.mult).then_inc(s_shift, 1)
                dve.sem_inc(s_xT, 2)
                dve.sem_inc(s_out, 2)
                dve.sem_inc(s_ss, 2)
                dve.sem_inc(s_T, 2)
                dve.wait_ge(s_w, 32)
                dve.wait_ge(s_pre, 4)

                def bias_add(t):
                    dve.wait_ge(s_qkv, t.done())
                    dve.tensor_tensor(qkv[:, tile(t), :], psQ[t.ring][:, :], bias[:, :], ALU.add).then_inc(s_out, 1)

                def sumsq(t):
                    dve.wait_ge(s_sq, t.done())
                    dve.tensor_reduce(ssq[:, heads(t)], sq[:, t.ring, :].rearrange("p (g d) -> p g d", d=QD),
                                      AX.X, ALU.add).then_inc(s_ss, 1)

                def guard(t):
                    dve.wait_ge(s_rt, t.done())
                    dve.tensor_scalar(ssq[:, heads(t)], ssq[:, heads(t)], 1e-6, None, ALU.add).then_inc(s_gd, 1)

                def invert(t):
                    dve.wait_ge(s_gd, t.done())
                    dve.reciprocal(inv[:, heads(t)], ssq[:, heads(t)]).then_inc(s_inv, 1)

                def shift(t):
                    dve.wait_ge(s_s, t.done() + 2)
                    dve.wait_ge(s_T, t.done())
                    dve.wait_ge(s_k, t.done())
                    dve.tensor_tensor(u[:, t.ring, :], sc[:, t.ring, :], shift_all[:, :], ALU.add).then_inc(s_b, 1)

                pipeline(dve, (2, bias_add), (3, sumsq), (4, guard), (8, shift), (5, invert))()

    def gradient_sems(self):
        names = "kh kl F sig u sw h t1 sp w1 HT hT PR d DT dTh dTl DH du dg G zero".split()
        self.g = {n: self.sem("g_" + n) for n in names}

    def gradient_phase(self, step):
        nc, qkv, qkT, g = self.nc, self.qkv, self.qkT, self.g
        base = step * NT
        with ExitStack() as c:
            sb = lambda n, s, d=F32: c.enter_context(nc.sbuf_tensor(f"g{step}_{n}", s, d))
            ps = lambda n, s, d=F32: c.enter_context(nc.psum_tensor(f"g{step}_{n}", s, d))
            kh, kl = sb("kh", [P, 2, P], F32R), sb("kl", [P, 2, P], F32R)
            s_, u_, sw, h, t1, sp_, w1, hT, du, dg = (sb(n, [P, 2, HID]) for n in
                                                      ("s", "u", "sw", "h", "t1", "sp", "w1", "hT", "du", "dg"))
            d = sb("d", [P, 2, P])
            dTh, dTl = sb("dTh", [P, 2, P], F32R), sb("dTl", [P, 2, P], F32R)
            psG, psU, psH, psD = (ps(n, [P, HID]) for n in ("G", "U", "H", "D"))
            psPT = ps("PT", [P, 4, P])
            pred, dTp = psPT[:, 0, :], psPT[:, 1, :]
            gvh, gvl = self.gvh, self.gvl
            block = c.enter_context(nc.Block())

            @block.sync
            def _(sp):
                if step == 0:
                    self.load_later_weights(sp)

            @block.gpsimd
            def _(pool):
                if step == 0:
                    pool.sem_inc(g["sp"], 2)
                    pool.sem_inc(g["w1"], 2)
                    pool.memset(self.zeros[:, :], 0.0).then_inc(g["zero"], 1)

                def k_low(t):
                    pool.wait_ge(g["kh"], t.done())
                    pool.tensor_tensor(kl[:, t.ring, :], qkT[:, 1, t.cols()], kh[:, t.ring, :].bitcast(F32),
                                       ALU.subtract).then_inc(g["kl"], 1)

                def slope(t):
                    pool.wait_ge(g["t1"], t.done())
                    pool.tensor_tensor(sp_[:, t.ring, :], s_[:, t.ring, :], t1[:, t.ring, :], ALU.subtract).then_inc(g["sp"], 1)

                def gate_factor(t):
                    pool.wait_ge(g["sp"], t.done() + 2)
                    if step or t.number() != 0:
                        pool.wait_ge(g["dg"], t.done(0))
                    pool.tensor_tensor(w1[:, t.ring, :], u_[:, t.ring, :], sp_[:, t.ring, :], ALU.mult).then_inc(g["w1"], 1)

                pipeline(pool, (0, k_low), (1, slope), (1, gate_factor))(base)

            @block.scalar
            def _(act):
                if step == 0:
                    act.sem_inc(g["u"], 1)
                    act.sem_inc(g["hT"], 1)
                act.preload_act_table(ACT.Sigmoid)

                def k_high(t):
                    act.wait_ge(g["F"], t.done(2, 2))
                    act.activation(kh[:, t.ring, :], qkT[:, 1, t.cols()], ACT.Copy).then_inc(g["kh"], 1)

                def sigmoid(t):
                    act.wait_ge(g["F"], t.done(1, 2) + 4)
                    act.wait_ge(g["sp"], t.done())
                    act.activation(s_[:, t.ring, :], psG[:, :], ACT.Sigmoid).then_inc(g["sig"], 1)

                def keep_u(t):
                    act.wait_ge(g["F"], t.done(2, 2) + 4)
                    act.wait_ge(g["w1"], t.done())
                    act.activation(u_[:, t.ring, :], psU[:, :], ACT.Copy).then_inc(g["u"], 1)

                def keep_hT(t):
                    act.wait_ge(g["HT"], t.done())
                    act.activation(hT[:, t.ring, :], psH[:, :], ACT.Copy).then_inc(g["hT"], 1)

                def dT_high(t):
                    act.wait_ge(g["DT"], t.done())
                    act.activation(dTh[:, t.ring, :], dTp, ACT.Copy).then_inc(g["dTh"], 1)

                pipeline(act, (2, keep_hT), (0, k_high), (1, sigmoid), (1, keep_u), (2, dT_high))(base)

            @block.tensor
            def _(pe):
                if step == 0:
                    pe.sem_inc(g["F"], 4)
                    pe.sem_inc(g["G"], 6)
                pe.wait_ge(g["zero"], 1)
                for n in range(3):
                    pe.matmul(self.acc[:, n, :, :].rearrange("p c d -> p (c d)"), self.zeros[:, 0:P], self.zeros[:, :],
                              start=True, stop=False, skip_group_check=True)

                def forward(t):
                    pe.wait_ge(g["kh"], t.done())
                    pe.wait_ge(g["kl"], t.done())
                    a, b = kh[:, t.ring, :], kl[:, t.ring, :]
                    pe.wait_ge(g["sw"], t.done())
                    mm3(pe, psG[:, :], a, b, gvh[:, 0:HID], gvl[:, 0:HID]).then_inc(g["F"], 1)
                    pe.wait_ge(g["u"], t.done())
                    mm3(pe, psU[:, :], a, b, gvh[:, HID:2 * HID], gvl[:, HID:2 * HID]).then_inc(g["F"], 1)

                def turn_h(t):
                    pe.wait_ge(g["h"], t.done())
                    pe.wait_ge(g["hT"], t.done())
                    for n in range(NC):
                        last = pe.transpose(psH[:, n * P:n * P + P], h[:, t.ring, n * P:n * P + P], self.ident[:, :])
                    last.then_inc(g["HT"], 1)

                def predict(t):
                    pe.wait_ge(g["hT"], t.done() + 1)
                    pe.wait_ge(g["dTl"], t.done())
                    for n in range(NC):
                        last = pe.matmul(pred, hT[:, t.ring, n * P:n * P + P], self.proj[:, n, :],
                                         start=(n == 0), stop=(n == NC - 1))
                    last.then_inc(g["PR"], 1)

                def turn_d(t):
                    pe.wait_ge(g["d"], t.done())
                    pe.transpose(dTp, d[:, t.ring, :], self.ident[:, :]).then_inc(g["DT"], 1)

                def back(t):
                    pe.wait_ge(g["dTh"], t.done())
                    pe.wait_ge(g["dTl"], t.done() + 1)
                    pe.wait_ge(g["dg"], t.done())
                    mm3(pe, psD[:, :], dTh[:, t.ring, :], dTl[:, t.ring, :], self.pTh[:, :], self.pTl[:, :]).then_inc(g["DH"], 1)

                def add(n, src, ready):
                    def step_(t):
                        pe.wait_ge(*ready(t))
                        k = qkv[:, bass.ds(t.i * 2 + t.j, 1), P:2 * P]
                        for m in range(NC):
                            last = pe.matmul(self.acc[:, n, m, :], src[:, t.ring, m * P:m * P + P],
                                             d[:, t.ring, :] if n == 2 else k, start=False, stop=False, skip_group_check=True)
                        last.then_inc(g["G"], 1)
                    return step_

                add_proj = add(2, h, lambda t: (g["d"], t.done()))
                add_val = add(1, du, lambda t: (g["du"], t.done() + 2))
                add_gate = add(0, dg, lambda t: (g["dg"], t.done() + 1))
                pipeline(pe, (2, turn_h), (3, add_proj), (1, forward), (2, predict), (3, add_gate), (2, turn_d),
                         (3, add_val), (2, back))(base)

            @block.vector
            def _(dve):
                if step == 0:
                    for n in ("sw", "dTl", "dg"):
                        dve.sem_inc(g[n], 1)
                    dve.sem_inc(g["du"], 2)

                def swish(t):
                    dve.wait_ge(g["sig"], t.done())
                    dve.wait_ge(g["du"], t.done())
                    dve.tensor_tensor(sw[:, t.ring, :], psG[:, :], s_[:, t.ring, :], ALU.mult).then_inc(g["sw"], 1)

                def hidden(t):
                    dve.wait_ge(g["u"], t.done() + 1)
                    dve.wait_ge(g["sw"], t.done() + 1)
                    dve.wait_ge(g["G"], t.done(1, 3))
                    dve.tensor_tensor(h[:, t.ring, :], sw[:, t.ring, :], u_[:, t.ring, :], ALU.mult).then_inc(g["h"], 1)

                def fall(t):
                    dve.scalar_tensor_tensor(t1[:, t.ring, :], s_[:, t.ring, :], 1.0, sw[:, t.ring, :],
                                             ALU.subtract, ALU.mult).then_inc(g["t1"], 1)

                def error(t):
                    dve.wait_ge(g["PR"], t.done())
                    dve.tensor_tensor(d[:, t.ring, :], pred, qkv[:, bass.ds(t.i * 2 + t.j, 1), 2 * P:3 * P],
                                      ALU.subtract).then_inc(g["d"], 1)

                def dT_low(t):
                    dve.wait_ge(g["dTh"], t.done())
                    dve.tensor_tensor(dTl[:, t.ring, :], dTp, dTh[:, t.ring, :].bitcast(F32), ALU.subtract).then_inc(g["dTl"], 1)

                def grad_val(t):
                    dve.wait_ge(g["DH"], t.done())
                    dve.tensor_tensor(du[:, t.ring, :], psD[:, :], sw[:, t.ring, :], ALU.mult).then_inc(g["du"], 1)

                def grad_gate(t):
                    dve.wait_ge(g["w1"], t.done() + 2)
                    dve.tensor_tensor(dg[:, t.ring, :], psD[:, :], w1[:, t.ring, :], ALU.mult).then_inc(g["dg"], 1)

                pipeline(dve, (1, swish), (2, error), (1, hidden), (2, dT_low), (1, fall), (2, grad_val), (2, grad_gate))(base)


    USED = ("xt", "x", "scaled", "p0", "t0", "a1", "p1", "q1", "xt2", "x2", "a2",
            "p2", "t2", "a3", "p3", "t3", "a4", "p4", "q4", "new", "newT")

    LATE_LOADS = 10 + NT

    def load_later_weights(self, sp):
        row = lambda name: self.a[name].rearrange("(a n) -> a n", a=1)
        loads = [
            (self.we[:, :].rearrange("d (e o) -> d e o", e=NE), self.a["L0_ffn_We"].rearrange("e d o -> d e o")),
            (self.wqkv[:, :, :, :].rearrange("p a h d -> p (a h d)"), self.a["L0_attn_b_w_qkv"]),
            (self.wout[:, :, :], self.a["L0_attn_b_w_out"].rearrange("(n p) d -> p n d", p=P)),
            (self.wg[:, :], self.a["L0_ffn_Wg"]),
            (self.bg[:, :], self.a["L0_ffn_bg"].rearrange("(n a) -> n a", a=1)),
            (self.bout[:, 0, :], row("L0_attn_b_b_out").broadcast_to([P, P])),
            (self.lng[:, :], self.a["L0_attn_b_g"].rearrange("a b d -> d (a b)")),
            (self.lnb[:, :], self.a["L0_attn_b_b"].rearrange("a b d -> d (a b)")),
            (self.pw[:, :], self.a["L0_attn_a_proj_w"]),
            (self.pb[:, 0, :], row("L0_attn_a_proj_b").broadcast_to([P, P])),
        ]
        for dst, src in loads:
            sp.dma_start(dst, src).then_inc(self.s_late, 16)
        sp.wait_ge(self.s_bias, 2)
        for t in range(NT):
            sp.dma_start(self.be[t * NE:(t + 1) * NE, t, :], self.a["L0_ffn_be"]).then_inc(self.s_late, 16)

    def part_later_weights(self, pool):
        wide = lambda ap: ap.rearrange("p (a d) -> p a d", d=P)
        times = lambda ap, n=NE: ap[:, :].unsqueeze(1).broadcast_to([P, n, P])
        wq, wv = (self.wqkv[:, n, :, :].rearrange("p h d -> p (h d)") for n in (0, 2))
        pool.wait_ge(self.s_late, 16 * self.LATE_LOADS)
        c = Chain(pool, self.s_parts)
        for src, high, low in ((self.we[:, :], self.weh, self.wel), (wv, self.wvh, self.wvl)):
            c(pool.tensor_tensor(wide(high[:, :]), wide(src), times(self.ones), ALU.mult))
            c(pool.tensor_tensor(low[:, :], src, high[:, :].bitcast(F32), ALU.subtract))
        be = self.be[:, :, :].rearrange("p t d -> p (t d)")
        c(pool.tensor_tensor(wide(self.beh[:, :]), self.be[:, :, :], times(self.ones, NT), ALU.mult))
        c(pool.tensor_tensor(self.bel[:, :], be, self.beh[:, :].bitcast(F32), ALU.subtract))
        c(pool.tensor_tensor(wide(wq), wide(wq), times(self.factor), ALU.mult))

    def schulz_sems(self):
        self.used = [self.sem(f"ns_used{m}") for m in range(3)]
        self.made = [self.sem(f"ns_made{m}") for m in range(3)]
        self.s_trace, self.s_norm, self.s_root, self.s_rate, self.s_nsv = (
            self.sem("ns_" + n) for n in ("trace", "norm", "root", "rate", "v"))
        self.s_gh, self.s_ph, self.s_lo = self.sem("ns_gh"), self.sem("ns_ph"), self.sem("ns_lo")

    def schulz_phase(self, step):
        nc, acc, ident = self.nc, self.acc, self.ident
        used, made = self.used, self.made

        def after(m, name):
            names = self.USED[:len(self.USED) - (m < 2)]
            return step * len(names) + names.index(name) + 1

        def result(m, name):
            names = [n for n in self.USED[:len(self.USED) - (m < 2)] if n not in ("xt", "scaled")]
            return step * len(names) + names.index(name) + 1

        with ExitStack() as c:
            sb = lambda n, s, d=F32: c.enter_context(nc.sbuf_tensor(f"n{step}_{n}", s, d))
            XT, X, XT2, X2 = (sb(n, [P, 3, NC, P]) for n in ("XT", "X", "XT2", "X2"))
            A, T1, T, Q = (sb(n, [P, 3, P]) for n in ("A", "T1", "T", "Q"))
            Pm = sb("P", [P, 2, 3, P])
            aI, junk = sb("aI", [P, P]), sb("junk", [P, P])
            tr, nrm, r, r2, rate = (sb(n, [P, 3]) for n in ("tr", "nrm", "r", "r2", "rate"))
            small = [c.enter_context(nc.psum_tensor(f"n{step}_small{m}", [P, 4, P], F32)) for m in range(3)]
            big = [acc[:, m, :, :] for m in range(3)]
            flat = lambda ap: ap.rearrange("p c d -> p (c d)")
            block = c.enter_context(nc.Block())

            @block.gpsimd
            def _(pool):
                if step == TTT_STEPS - 1:
                    self.part_later_weights(pool)
                for m in range(2):
                    half = slice(m * HID, (m + 1) * HID)
                    pool.wait_ge(self.s_gh, 2 * step + m + 1)
                    pool.tensor_tensor(self.gvl[:, half], self.gv[:, half], self.gvh[:, half].bitcast(F32),
                                       ALU.subtract).then_inc(self.s_lo, 1)

            @block.tensor
            def _(pe):
                def gram(m, src, name):
                    for n in range(NC):
                        last = pe.matmul(small[m][:, 0, :], src[:, m, n, :], src[:, m, n, :], start=(n == 0), stop=(n == NC - 1))
                    return last

                def square(k):
                    for m in range(3):
                        pe.wait_ge(used[m], after(m, f"a{k}" if k else "scaled"))
                        pe.matmul(small[m][:, 1, :], A[:, m, :], A[:, m, :], start=True, stop=True).then_inc(made[m], 1)

                def times_a(k, with_q=False):
                    for m in range(3):
                        pe.wait_ge(used[m], after(m, f"p{k}"))
                        if with_q:
                            pe.matmul(small[m][:, 3, :], Pm[:, k % 2, m, :], Pm[:, 1 - k % 2, m, :], start=True, stop=True)
                        pe.matmul(small[m][:, 2, :], Pm[:, k % 2, m, :], A[:, m, :], start=True, stop=True).then_inc(made[m], 1)

                def next_a(k):
                    for m in range(3):
                        pe.wait_ge(used[m], after(m, f"t{k}"))
                        pe.matmul(small[m][:, 0, :], Pm[:, k % 2, m, :], T[:, m, :], start=True, stop=True).then_inc(made[m], 1)

                def last_q(k, before):
                    for m in range(3):
                        pe.wait_ge(used[m], after(m, f"p{k}"))
                        pe.matmul(small[m][:, 3, :], Pm[:, k % 2, m, :], before(m), start=True, stop=True).then_inc(made[m], 1)

                for m in range(3):
                    pe.wait_ge(used[m], after(m, "xt"))
                    gram(m, XT, "trace").then_inc(self.s_norm, 1)
                for m in range(3):
                    for n in range(NC):
                        last = pe.transpose(big[m][:, n, :], XT[:, m, n, :], ident[:, :])
                    last.then_inc(made[m], 1)
                pe.wait_ge(self.s_trace, 3 * step + 3)
                pe.matmul(small[0][:, 3, 0:3], self.ones[:, :], tr[:, :], start=True, stop=True).then_inc(self.s_norm, 1)
                square(0)
                times_a(0)
                next_a(0)
                square(1)
                last_q(1, lambda m: Pm[:, 0, m, :])
                for m in range(3):
                    pe.wait_ge(used[m], after(m, "q1"))
                    for n in range(NC):
                        last = pe.matmul(big[m][:, n, :], X[:, m, n, :], Q[:, m, :], start=True, stop=True)
                    last.then_inc(made[m], 1)
                for m in range(3):
                    pe.wait_ge(used[m], after(m, "xt2"))
                    pe.matmul(flat(big[m]), Q[:, m, :], flat(X[:, m, :, :]), start=True, stop=True).then_inc(made[m], 1)
                for m in range(3):
                    pe.wait_ge(used[m], after(m, "x2"))
                    gram(m, XT2, "a2").then_inc(made[m], 1)
                square(2)
                times_a(2)
                next_a(2)
                square(3)
                times_a(3, True)
                next_a(3)
                square(4)
                last_q(4, lambda m: Q[:, m, :])
                for m in range(3):
                    pe.wait_ge(used[m], after(m, "q4"))
                    pe.matmul(flat(big[m]), Q[:, m, :], flat(X2[:, m, :, :]), start=True, stop=True).then_inc(made[m], 1)
                for n in range(NC):
                    last = pe.matmul(small[0][:, n, :], X2[:, 2, n, :], Q[:, 2, :], start=True, stop=True)
                last.then_inc(made[2], 1)

            @block.scalar
            def _(act):
                def copy(m, dst, src, name):
                    if name != "xt":
                        act.wait_ge(made[m], result(m, name))
                    act.activation(dst, src, ACT.Copy).then_inc(used[m], 1)

                for m in (0, 2):
                    copy(m, flat(XT[:, m, :, :]), flat(big[m]), "xt")
                act.preload_act_table(ACT.Sqrt)
                for m in range(3):
                    copy(m, flat(X[:, m, :, :]), flat(big[m]), "x")
                act.wait_ge(self.s_norm, 4 * step + 4)
                act.activation(nrm[:, :], small[0][:, 3, 0:3], ACT.Sqrt).then_inc(self.s_root, 1)

                def small_copy(dst, slot, name):
                    for m in range(3):
                        copy(m, dst[:, m, :], small[m][:, slot, :], name)

                small_copy(T, 2, "t0")
                small_copy(Q, 3, "q1")
                for name, dst in (("xt2", XT2), ("x2", X2)):
                    for m in range(3):
                        copy(m, flat(dst[:, m, :, :]), flat(big[m]), name)
                small_copy(T, 2, "t2")
                for m in range(3):
                    act.wait_ge(made[m], result(m, "t3"))
                    act.activation(Q[:, m, :], small[m][:, 3, :], ACT.Copy)
                    act.activation(T[:, m, :], small[m][:, 2, :], ACT.Copy).then_inc(used[m], 1)
                small_copy(Q, 3, "q4")
                for m in range(2):
                    act.wait_ge(used[m], after(m, "new"))
                    half = slice(m * HID, (m + 1) * HID)
                    act.activation(self.gvh[:, half], self.gv[:, half], ACT.Copy).then_inc(self.s_gh, 1)
                act.wait_ge(used[2], after(2, "new"))
                act.activation(self.pTh[:, :], self.projT[:, :], ACT.Copy).then_inc(self.s_ph, 1)

            @block.vector
            def _(dve):
                dve.tensor_copy(flat(XT[:, 1, :, :]), flat(big[1])).then_inc(used[1], 1)
                dve.tensor_scalar(aI[:, :], ident[:, :], NS_A, None, ALU.mult).then_inc(self.s_nsv, 1)
                for m in range(3):
                    dve.wait_ge(self.s_norm, 4 * step + m + 1)
                    if m:
                        dve.wait_ge(self.s_trace, 3 * step + m)
                    dve.tensor_tensor_reduce(junk[:, :], small[m][:, 0, :], ident[:, :], 1.0, 0.0, ALU.mult, ALU.add,
                                             tr[:, m:m + 1]).then_inc(self.s_trace, 1)
                dve.wait_ge(self.s_root, step + 1)
                c = Chain(dve, self.s_nsv, 4 * step + 1)
                c(dve.tensor_scalar(nrm[:, :], nrm[:, :], 1e-7 / LOSS_SCALE, None, ALU.add))
                c(dve.reciprocal(r[:, :], nrm[:, :]))
                dve.tensor_scalar(rate[:, :], r[:, :], -LR, None, ALU.mult).then_inc(self.s_rate, 1)
                c(dve.tensor_tensor(r2[:, :], r[:, :], r[:, :], ALU.mult))

                def scaled(m, name):
                    dve.wait_ge(made[m], result(m, name))
                    dve.tensor_scalar(A[:, m, :], small[m][:, 0, :], r2[:, m:m + 1], None, ALU.mult).then_inc(self.s_rate, 1)

                def mixed(m):
                    dve.scalar_tensor_tensor(T1[:, m, :], A[:, m, :], NS_B, aI[:, :], ALU.mult, ALU.add).then_inc(used[m], 1)

                def scale_all(name, done):
                    for m in range(3):
                        scaled(m, name)
                    for m in range(3):
                        dve.wait_ge(self.s_rate, 7 * step + 1 + done + m + 1)
                        mixed(m)

                def poly(k):
                    for m in range(3):
                        dve.wait_ge(made[m], result(m, f"p{k}"))
                        dve.scalar_tensor_tensor(Pm[:, k % 2, m, :], small[m][:, 1, :], NS_C, T1[:, m, :],
                                                 ALU.mult, ALU.add).then_inc(used[m], 1)

                def next_a(k):
                    for m in range(3):
                        dve.wait_ge(made[m], result(m, f"a{k}"))
                        dve.scalar_tensor_tensor(T1[:, m, :], small[m][:, 0, :], NS_B, aI[:, :], ALU.mult, ALU.add)
                        dve.tensor_copy(A[:, m, :], small[m][:, 0, :]).then_inc(used[m], 1)

                for m in range(3):
                    dve.wait_ge(used[m], after(m, "x"))
                scale_all("x", 0)
                poly(0)
                next_a(1)
                poly(1)
                scale_all("a2", 3)
                poly(2)
                next_a(3)
                poly(3)
                next_a(4)
                poly(4)
                for m in range(3):
                    dve.wait_ge(made[m], result(m, "new"))
                    dst = self.gv[:, m * HID:(m + 1) * HID] if m < 2 else self.projT[:, :]
                    dve.scalar_tensor_tensor(dst, flat(big[m]), rate[:, m:m + 1], dst, ALU.mult, ALU.add).then_inc(used[m], 1)
                dve.wait_ge(made[2], result(2, "newT"))
                dve.scalar_tensor_tensor(flat(self.proj[:, :, :]), flat(small[0][:, :, :]), rate[:, 2:3], flat(self.proj[:, :, :]),
                                         ALU.mult, ALU.add).then_inc(used[2], 1)
                dve.wait_ge(self.s_ph, step + 1)
                dve.tensor_tensor(self.pTl[:, :], self.projT[:, :], self.pTh[:, :].bitcast(F32), ALU.subtract).then_inc(self.s_lo, 1)


    def query_phase(self):
        nc, sem, x, qkT = self.nc, self.sem, self.x, self.qkT
        names = "pw pwc qh ql gu sig sw h o xb x".split()
        q = {n: sem("q_" + n) for n in names}
        with ExitStack() as c:
            sb = lambda n, s, d=F32: c.enter_context(nc.sbuf_tensor("q_" + n + "_", s, d))
            ps = lambda n, s, d=F32: c.enter_context(nc.psum_tensor("q_" + n + "_", s, d))
            pw = sb("pw", [P, NC, P])
            qh, ql = sb("qh", [P, 2, SEQ], F32R), sb("ql", [P, 2, SEQ], F32R)
            sg, sw, hT = sb("sg", [P, 2, SEQ]), sb("sw", [P, 2, SEQ]), sb("hT", [P, 2, NC, SEQ])
            psG, psU = ps("G", [P, 2, SEQ]), ps("U", [P, 2, SEQ])
            psO, psW = ps("O", [P, TPB, P]), ps("W", [P, NC, P])
            block = c.enter_context(nc.Block())
            rows = lambda b: x[:, b.cols(TPB), :]
            chunked = lambda lag, step: [(lag, lambda b, n=n: step(b, n)) for n in range(NC)]

            @block.gpsimd
            def _(pool):
                def add_bias(b):
                    pool.tensor_tensor(rows(b), rows(b), self.pb[:, :, :].broadcast_to([P, TPB, P]), ALU.add).then_inc(q["xb"], 1)

                pipeline(pool, (0, add_bias), count=BATCH)()

            @block.scalar
            def _(act):
                act.preload_act_table(ACT.Sigmoid)
                act.sem_inc(q["gu"], 2 * NC)

                def high(b):
                    act.wait_ge(q["gu"], b.done(0, NC) + NC)
                    act.activation(qh[:, b.ring, :], qkT[:, 0, b.cols(SEQ)], ACT.Copy).then_inc(q["qh"], 1)

                def sigmoid(b, n):
                    act.wait_ge(q["gu"], b.done(n + 1, NC) + 2 * NC)
                    act.wait_ge(q["sw"], b.done(n + 1, NC))
                    act.activation(sg[:, n % 2, :], psG[:, n % 2, :], ACT.Sigmoid).then_inc(q["sig"], 1)

                def fold(b):
                    if b.number() == 0:
                        act.wait_ge(q["pw"], 1)
                        act.activation(pw[:, :, :], psW[:, :, :], ACT.Copy).then_inc(q["pwc"], 1)

                pipeline(act, (0, high), (0, fold), *chunked(1, sigmoid), count=BATCH)()

            @block.tensor
            def _(pe):
                for n in range(NC):
                    last = pe.matmul(psW[:, n, :], self.projT[:, n * P:n * P + P], self.pw[:, :], start=True, stop=True)
                last.then_inc(q["pw"], 1)

                def gate_up(b, n):
                    if n == 0:
                        pe.wait_ge(q["ql"], b.done())
                    pe.wait_ge(q["h"], b.done(n + 1, NC))
                    for half, ps_ in ((0, psG), (1, psU)):
                        cols = slice(half * HID + n * P, half * HID + n * P + P)
                        last = mm3(pe, ps_[:, n % 2, :], self.gvh[:, cols], self.gvl[:, cols], qh[:, b.ring, :], ql[:, b.ring, :])
                    last.then_inc(q["gu"], 1)

                def output(b, t):
                    if t == 0:
                        pe.wait_ge(q["pwc"], 1)
                        pe.wait_ge(q["x"], b.done())
                        pe.wait_ge(q["h"], b.done(NC, NC) + 2)
                    for n in range(NC):
                        last = pe.matmul(psO[:, t, :], hT[:, b.ring, n, t * P:t * P + P], pw[:, n, :],
                                         start=(n == 0), stop=(n == NC - 1))
                    last.then_inc(q["o"], 1)

                stages = []
                for up, out in zip(chunked(1, gate_up), chunked(2, output)):
                    stages += [up, out]
                pipeline(pe, *stages, count=BATCH)()

            @block.vector
            def _(dve):
                dve.sem_inc(q["sw"], 2)
                dve.sem_inc(q["h"], 2)
                dve.sem_inc(q["x"], 1)

                def low(b):
                    dve.wait_ge(q["qh"], b.done())
                    dve.tensor_tensor(ql[:, b.ring, :], qkT[:, 0, b.cols(SEQ)], qh[:, b.ring, :].bitcast(F32),
                                      ALU.subtract).then_inc(q["ql"], 1)

                def swish(b, n):
                    dve.wait_ge(q["sig"], b.done(n + 1, NC))
                    dve.wait_ge(q["h"], b.done(n + 1, NC))
                    dve.tensor_tensor(sw[:, n % 2, :], psG[:, n % 2, :], sg[:, n % 2, :], ALU.mult).then_inc(q["sw"], 1)

                def hidden(b, n):
                    dve.wait_ge(q["sw"], b.done(n + 1, NC) + 2)
                    if n == 0 and b.number() not in (0, 1):
                        dve.wait_ge(q["o"], b.done(NC, NC) - 2 * NC)
                    dve.tensor_tensor(hT[:, b.ring, n, :], psU[:, n % 2, :], sw[:, n % 2, :], ALU.mult).then_inc(q["h"], 1)

                def add(b):
                    dve.wait_ge(q["o"], b.done(NC, NC))
                    dve.wait_ge(q["xb"], b.done())
                    dve.tensor_tensor(rows(b), rows(b), psO[:, :, :], ALU.add).then_inc(q["x"], 1)

                def stats(b):
                    dve.wait_ge(q["x"], b.done() + 1)
                    for n in range(TPB):
                        self.take_stats(dve, b.i * (2 * TPB) + b.j * TPB + n)

                stages = []
                for a, b in zip(chunked(1, swish), chunked(1, hidden)):
                    stages += [a, b]
                pipeline(dve, (0, low), *stages, (2, add), (2, stats), count=BATCH)()


    def moe_phase(self, nth):
        nc, x, ident = self.nc, self.x, self.ident
        own = []

        def sem(n):
            own.append(nc.alloc_semaphore(f"m{nth}_{n}"))
            return own[-1]

        s_var, s_root, s_ln = sem("var"), sem("root"), sem("ln")
        s_xn, s_xT, s_xTs, s_keep, s_L, s_l = (sem(n) for n in ("xn", "xT", "xTs", "keep", "L", "l"))
        s_sh, s_e, s_c, s_wT, s_wTs, s_B, s_xb = (sem(n) for n in ("sh", "e", "c", "wT", "wTs", "B", "xb"))
        s_hi, s_lo, s_E, s_y, s_z, s_z2, s_z3, s_x, s_out = (sem(n) for n in ("hi", "lo", "E", "y", "z", "z2", "z3", "x", "out"))
        s_prio, s_w, s_lT, s_lTs = sem("prio"), sem("w"), sem("lT"), sem("lTs")
        ACT_E = 4
        with ExitStack() as c:
            sb = lambda n, s, d=F32: c.enter_context(nc.sbuf_tensor(f"m{nth}_{n}_", s, d))
            ps = lambda n, s, d=F32: c.enter_context(nc.psum_tensor(f"m{nth}_{n}_", s, d))
            weh, wel, wg, bg, beh, bel = self.weh, self.wel, self.wg, self.bg, self.beh, self.bel
            xn, xTs, xnT = sb("xn", [P, 2, TPB, P]), sb("xTs", [P, 2, SEQ]), sb("xnT", [P, TOK])
            prio, logit, gate, gate2, eq, sel, sel2, wt = (sb(n, [P, NT, NE]) for n in
                                                           ("prio", "logit", "gate", "gate2", "eq", "sel", "sel2", "wt"))
            m1, m2, pm, tot, rtot = (sb(n, [P, NT]) for n in ("m1", "m2", "pm", "tot", "rtot"))
            lTs = sb("lTs", [NE, 2, SEQ])
            wTh, wTl = sb("wTh", [P, P], F32R), sb("wTl", [P, P], F32R)
            xh, xl = sb("xh", [P, 2, P], F32R), sb("xl", [P, 2, P], F32R)
            y, z, z2, z3 = sb("y", [P, 2, NE * P]), sb("z", [P, 2, 4 * P]), sb("z2", [P, 2, 2 * P]), sb("z3", [P, 2, P])
            psT, psL = ps("T", [P, 2, 512]), ps("L", [P, 2, 512])
            psE = ps("E", [P, 2, NE * P])
            block = c.enter_context(nc.Block())
            tile = lambda t: bass.ds(t.i * 2 + t.j, 1)
            FIRST = [Tile(0, j) for j in range(2)]
            later = lambda step: lambda t: None if t.number() in (0, 1) else step(t)

            @block.sync
            def _(sp):
                if nth == 1:
                    dst = self.out.rearrange("b (t p) d -> p (b t) d", p=P)
                    for g in range(BATCH):
                        sp.wait_ge(s_x, (g + 1) * TPB + 2)
                        sp.dma_start(dst[:, g * TPB:(g + 1) * TPB, :], x[:, g * TPB:(g + 1) * TPB, :]).then_inc(s_out, 16)
                    sp.wait_ge(s_out, 16 * BATCH)

            @block.gpsimd
            def _(pool):
                for n in range(NE):
                    last = pool.memset(prio[:, :, n:n + 1], float(NE - n))
                last.then_inc(s_prio, 1)
                pool.sem_inc(s_keep, 2)

                def keep(g):
                    pool.wait_ge(s_xTs, g.done())
                    split = lambda ap: ap.rearrange("p (t d) -> p t d", d=P)
                    pool.tensor_tensor(split(xnT[:, g.cols(SEQ)]), split(xTs[:, g.ring, :]),
                                       self.ones[:, :].unsqueeze(1).broadcast_to([P, TPB, P]), ALU.mult).then_inc(s_keep, 1)

                pipeline(pool, (0, keep), count=BATCH)()

                def add_half(t):
                    pool.wait_ge(s_y, t.done() + 2)
                    pool.wait_ge(s_w, t.done() + 2)
                    pool.wait_ge(s_z2, t.done())
                    pool.tensor_tensor(z[:, t.ring, :], y[:, t.ring, 0:4 * P], y[:, t.ring, 4 * P:8 * P], ALU.add).then_inc(s_z, 1)

                def low(t):
                    pool.wait_ge(s_hi, t.done())
                    pool.tensor_tensor(xl[:, t.ring, :], xnT[:, t.cols()], xh[:, t.ring, :].bitcast(F32), ALU.subtract).then_inc(s_lo, 1)

                pool.sem_inc(s_z, 2)
                pipeline(pool, (0, low), (2, add_half))()

            @block.scalar
            def _(act):
                self.ln_scalar(act, s_var, s_root)

                def copy(t):
                    act.wait_ge(s_xT, t.done() + 2)
                    act.wait_ge(s_keep, t.done())
                    act.wait_ge(s_lT, t.done())
                    act.activation(xTs[:, t.ring, :], psT[:, t.ring, :], ACT.Copy).then_inc(s_xTs, 1)

                def take_logits(g):
                    act.wait_ge(s_lT, g.done() + 2)
                    act.wait_ge(s_L, g.done())
                    act.activation(lTs[:, g.ring, :], psL[0:NE, g.ring, :], ACT.Identity, bias=bg[:, :]).then_inc(s_lTs, 1)

                act.sem_inc(s_lT, 2)
                act.sem_inc(s_L, 2)
                act.sem_inc(s_lTs, 2)
                pipeline(act, (0, copy), (1, take_logits), count=BATCH)()

                def high(t):
                    act.wait_ge(s_E, t.done())
                    act.activation(xh[:, t.ring, :], xnT[:, t.cols()], ACT.Copy).then_inc(s_hi, 1)

                act.sem_inc(s_E, 2)
                act.sem_inc(s_w, 2)
                act.preload_act_table(ACT.Exp)
                act.wait_ge(s_keep, 1 + 2)
                for t in FIRST:
                    high(t)
                act.wait_ge(s_sh, 1)
                act.activation(gate[:, :, :], logit[:, :, :], ACT.Exp).then_inc(s_e, 1)
                act.wait_ge(s_keep, BATCH + 2)

                def weights_high(t):
                    if t.number() == 0:
                        act.wait_ge(s_wT, 1)
                        act.activation(wTh[:, :], psT[:, 0, 0:P], ACT.Copy).then_inc(s_wTs, 1)

                def weigh_last(t):
                    act.wait_ge(s_E, t.done() + 2)
                    act.wait_ge(s_z, t.done())
                    for n in range(NE - ACT_E, NE):
                        cols = slice(n * P, n * P + P)
                        last = act.activation(y[:, t.ring, cols], psE[:, t.ring, cols], ACT.Copy,
                                              scale=wt[:, tile(t), n:n + 1].rearrange("p a e -> p (a e)"))
                    last.then_inc(s_w, 1)

                pipeline(act, (0, later(high)), (1, weights_high), (2, weigh_last))()

            @block.tensor
            def _(pe):
                def turn(t):
                    pe.wait_ge(s_xn, t.done())
                    if t.number() not in (0, 1):
                        pe.wait_ge(s_xTs, t.done(-1))
                    for n in range(TPB):
                        last = pe.transpose(psT[:, t.ring, n * P:n * P + P], xn[:, t.ring, n, :], ident[:, :])
                    last.then_inc(s_xT, 1)

                def logits(g):
                    pe.wait_ge(s_xTs, g.done())
                    pe.wait_ge(s_lTs, g.done())
                    pe.matmul(psL[0:NE, g.ring, :], wg[:, :], xTs[:, g.ring, :], start=True, stop=True).then_inc(s_lT, 1)

                def turn_logits(g):
                    pe.wait_ge(s_lTs, g.done() + 2)
                    pe.wait_ge(s_l, g.done())
                    for n in range(TPB):
                        last = pe.transpose(psE[:, g.ring, n * NE:n * NE + NE], lTs[:, g.ring, n * P:n * P + P], ident[0:NE, 0:NE])
                    last.then_inc(s_L, 1)

                def weights(t):
                    if t.number() == 0:
                        pe.wait_ge(s_c, 1)
                        pe.transpose(psT[:, 0, 0:P], wt[:, :, :].rearrange("p t e -> p (t e)"), ident[:, :]).then_inc(s_wT, 1)
                        pe.wait_ge(s_wTs, 2)
                        for n, bank in enumerate((psT[:, 1, :], psL[:, 0, :], psL[:, 1, :], psT[:, 0, :])):
                            cols = slice(n * SEQ, n * SEQ + SEQ)
                            last = mm3(pe, bank, wTh[:, :], wTl[:, :], beh[:, cols], bel[:, cols])
                        last.then_inc(s_B, 1)

                pipeline(pe, (0, turn), (1, logits), (2, turn_logits), count=BATCH)()
                pe.wait_ge(s_l, BATCH + 2)

                def experts(t):
                    pe.wait_ge(s_lo, t.done())
                    pe.wait_ge(s_y, t.done())
                    pe.wait_ge(s_w, t.done())
                    for half in range(2):
                        cols = slice(half * 512, half * 512 + 512)
                        last = mm3(pe, psE[:, t.ring, cols], xh[:, t.ring, :], xl[:, t.ring, :], weh[:, cols], wel[:, cols])
                    last.then_inc(s_E, 1)

                pipeline(pe, (0, experts), (1, weights))()

            @block.vector
            def _(dve):
                n = self.ln_vector(dve, s_var, s_root, s_ln)
                dve.sem_inc(s_xT, 2)
                dve.sem_inc(s_l, 2)
                dve.sem_inc(s_y, 2)

                def norm(t):
                    dve.wait_ge(s_xT, t.done())
                    for n in range(TPB):
                        r = bass.ds(t.i * (2 * TPB) + t.j * TPB + n, 1)
                        last = dve.tensor_scalar(xn[:, t.ring, n, :], x[:, r, :].rearrange("p a d -> p (a d)"), self.mean[:, r],
                                                 self.rstd[:, r], ALU.subtract, ALU.mult)
                    last.then_inc(s_xn, 1)

                def keep_logits(g):
                    dve.wait_ge(s_L, g.done() + 2)
                    dve.tensor_copy(logit[:, bass.ds(g.i * (2 * TPB) + g.j * TPB, TPB), :],
                                    psE[:, g.ring, 0:TPB * NE].rearrange("p (t e) -> p t e", e=NE)).then_inc(s_l, 1)

                pipeline(dve, (0, norm), (3, keep_logits), count=BATCH)()
                wide = lambda ap: ap[:, :].unsqueeze(2).broadcast_to([P, NT, NE])
                g = Chain(dve, s_ln, n)
                dve.wait_ge(s_l, BATCH + 2)
                g(dve.tensor_reduce(m1[:, :], logit[:, :, :], AX.X, ALU.max))
                dve.tensor_tensor(logit[:, :, :], logit[:, :, :], wide(m1), ALU.subtract).then_inc(s_sh, 1)
                dve.wait_ge(s_e, 1)
                g(dve.tensor_reduce(tot[:, :], gate[:, :, :], AX.X, ALU.add))
                g(dve.reciprocal(rtot[:, :], tot[:, :]))
                g(dve.tensor_tensor(gate[:, :, :], gate[:, :, :], wide(rtot), ALU.mult))
                dve.wait_ge(s_prio, 1)

                def best(m, src, chosen):
                    g(dve.tensor_reduce(m[:, :], src[:, :, :], AX.X, ALU.max))
                    g(dve.tensor_tensor(eq[:, :, :], src[:, :, :], wide(m), ALU.is_equal))
                    g(dve.tensor_tensor(eq[:, :, :], eq[:, :, :], prio[:, :, :], ALU.mult))
                    g(dve.tensor_reduce(pm[:, :], eq[:, :, :], AX.X, ALU.max))
                    g(dve.tensor_tensor(chosen[:, :, :], eq[:, :, :], wide(pm), ALU.is_equal))

                best(m1, gate, sel)
                g(dve.scalar_tensor_tensor(gate2[:, :, :], sel[:, :, :], -2.0, gate[:, :, :], ALU.mult, ALU.add))
                best(m2, gate2, sel2)
                g(dve.tensor_tensor(tot[:, :], m1[:, :], m2[:, :], ALU.add))
                g(dve.reciprocal(rtot[:, :], tot[:, :]))
                g(dve.tensor_tensor(sel[:, :, :], sel[:, :, :], sel2[:, :, :], ALU.add))
                g(dve.tensor_tensor(sel[:, :, :], sel[:, :, :], gate[:, :, :], ALU.mult))
                dve.tensor_tensor(wt[:, :, :], sel[:, :, :], wide(rtot), ALU.mult).then_inc(s_c, 1)
                dve.wait_ge(s_c, 1)
                dve.sem_inc(s_z2, 2)
                dve.sem_inc(s_z3, 2)
                dve.sem_inc(s_x, 2)

                def add_bias(t):
                    if t.number() == 0:
                        dve.wait_ge(s_wTs, 1)
                        dve.tensor_tensor(wTl[:, :], psT[:, 0, 0:P], wTh[:, :].bitcast(F32), ALU.subtract).then_inc(s_wTs, 1)
                    if t.number() == 2:
                        dve.wait_ge(s_B, 1)
                        for n, bank in enumerate((psT[:, 1, :], psL[:, 0, :], psL[:, 1, :], psT[:, 0, :])):
                            rows = x[:, n * TPB:(n + 1) * TPB, :].rearrange("p t d -> p (t d)")
                            last = dve.tensor_tensor(rows, bank, rows, ALU.add)
                        last.then_inc(s_xb, 1)

                def weigh(t):
                    dve.wait_ge(s_E, t.done() + 2)
                    dve.wait_ge(s_z, t.done())
                    first, cols = NE - ACT_E, slice(0, (NE - ACT_E) * P)
                    dve.tensor_tensor(y[:, t.ring, cols].rearrange("p (e o) -> p e o", o=P),
                                      psE[:, t.ring, cols].rearrange("p (e o) -> p e o", o=P),
                                      wt[:, tile(t), 0:first].rearrange("p a e -> p (a e)").unsqueeze(2).broadcast_to([P, first, P]),
                                      ALU.mult).then_inc(s_y, 1)

                def add_quarter(t):
                    dve.wait_ge(s_z, t.done() + 2)
                    dve.wait_ge(s_z3, t.done())
                    dve.tensor_tensor(z2[:, t.ring, :], z[:, t.ring, 0:2 * P], z[:, t.ring, 2 * P:4 * P], ALU.add).then_inc(s_z2, 1)

                def add_eighth(t):
                    dve.wait_ge(s_z2, t.done() + 2)
                    dve.wait_ge(s_x, t.done())
                    dve.tensor_tensor(z3[:, t.ring, :], z2[:, t.ring, 0:P], z2[:, t.ring, P:2 * P], ALU.add).then_inc(s_z3, 1)

                def add_x(t):
                    dve.wait_ge(s_z3, t.done() + 2)
                    dve.wait_ge(s_xb, 1)
                    dve.tensor_tensor(x[:, tile(t), :], x[:, tile(t), :], z3[:, t.ring, :], ALU.add).then_inc(s_x, 1)

                def stats(t):
                    dve.wait_ge(s_x, t.done() + 2)
                    self.take_stats(dve, t.i * 2 + t.j)

                last = ((6, stats),) if nth == 0 else ()
                pipeline(dve, (2, weigh), (1, add_bias), (3, add_quarter), (4, add_eighth), (5, add_x), *last)()

        if nth == 0:
            nc.clear_and_free_semaphores(own)
            nc.all_engine_barrier()


    def attention_phase(self):
        nc, x, ident = self.nc, self.x, self.ident
        names = ("kk xb var root ln cst xn xT xa xh xl V va vd wh wl pr qh kh ql kl S mx ex T ea ed PV nr "
                 "oT oTa oTd out res rs").split()
        t = {n: self.sem("t_" + n) for n in names}
        with ExitStack() as c:
            sb = lambda n, s, d=F32: c.enter_context(nc.sbuf_tensor("t_" + n + "_", s, d))
            ps = lambda n, s, d=F32: c.enter_context(nc.psum_tensor("t_" + n + "_", s, d))
            w, wvh, wvl, wout, bout, lng, lnb = self.wqkv, self.wvh, self.wvl, self.wout, self.bout, self.lng, self.lnb
            mask, identb = sb("mask", [P, P], BF16), sb("identb", [P, P], BF16)
            xn, xT = sb("xn", [P, TPB, P]), sb("xT", [P, SEQ])
            xh, xl = sb("xh", [P, SEQ], F32R), sb("xl", [P, SEQ], F32R)
            v, o = sb("v", [P, TPB, HEADS * DH]), sb("o", [P, TPB, HEADS * DH])
            oT = sb("oT", [P, NP, SEQ])
            wh, wl = sb("wh", [P, 2, 2 * DH], F32R), sb("wl", [P, 2, 2 * DH], F32R)
            qs, ks, kl = sb("qs", [P, 2, SEQ], F32R), sb("ks", [P, 2, SEQ], F32R), sb("kl", [DH, 2, SEQ], F32R)
            pr, pT = sb("p", [P, 8, SEQ]), sb("pT", [P, 4, TPB, P])
            nmax, rsum, rinv = sb("nmax", [P, 2, TPB]), sb("rsum", [P, 2, TPB]), sb("rinv", [P, 2, TPB])
            psS, psT, psO, psP = ps("S", [P, 4, 512]), ps("T", [P, 2, 512]), ps("O", [P, 512]), ps("P", [P, 512])
            ON_ACT = (2, 3)
            block = c.enter_context(nc.Block())
            flat = lambda ap: ap.rearrange("p a d -> p (a d)")

            def first(s):
                return isinstance(s.i, int) and 0 <= s.j < Slot.TURN

            def batches(e, body):
                body(0, False)
                with e.Fori(1, BATCH) as b:
                    body(b, True)

            @block.gpsimd
            def _(pool):
                g = Chain(pool, t["cst"])
                g(pool.memset(mask[:, :], 0.0))
                for n in range(P // FRAME - 1):
                    g(pool.memset(mask[n * FRAME:(n + 1) * FRAME, (n + 1) * FRAME:P], NEG))
                g(pool.tensor_copy(identb[:, :], ident[:, :]))
                pool.sem_inc(t["kk"], 1)

                def w_low(s):
                    if s.u == 0:
                        pool.wait_ge(t["wh"], s.head_done())
                        pool.wait_ge(t["kk"], s.head_done())
                        pool.tensor_tensor(wl[:, s.par, :].rearrange("p (a d) -> p a d", a=2),
                                           w[:, 0:2, :, :].rearrange("p a h d -> p a (h d)")[:, :, s.head_cols()],
                                           wh[:, s.par, :].bitcast(F32).rearrange("p (a d) -> p a d", a=2),
                                           ALU.subtract).then_inc(t["wl"], 1)

                def repeat_k(s):
                    if s.u == 2:
                        pool.wait_ge(t["kh"], s.head_done())
                        pool.wait_ge(t["wl"], s.head_done())
                        pool.tensor_tensor(ks[DH:P, s.par, :].rearrange("p (a d) -> p a d", d=P),
                                           ks[0:DH, s.par, :].bitcast(F32).rearrange("p (a d) -> p a d", d=P),
                                           self.ones[0:DH, :].unsqueeze(1).broadcast_to([DH, TPB, P]), ALU.mult).then_inc(t["kk"], 1)

                def body(b, before):
                    pool.wait_ge(t["xn"], b + 1)
                    rows = x[:, bass.ds(b * TPB, TPB), :]
                    pool.tensor_tensor(rows, rows, bout[:, :, :].broadcast_to([P, TPB, P]), ALU.add).then_inc(t["xb"], 1)
                    slots(pool, b, (-TPB - 1, w_low), (-TPB, repeat_k))

                batches(pool, body)

            @block.scalar
            def _(act):
                self.ln_scalar(act, t["var"], t["root"])
                act.preload_act_table(ACT.Exp)
                act.sem_inc(t["pr"], 2)

                def w_high(s):
                    if s.u == 0:
                        act.wait_ge(t["pr"], s.head_done())
                        act.activation(wh[:, s.par, :].rearrange("p (a d) -> p a d", a=2),
                                       w[:, 0:2, :, :].rearrange("p a h d -> p a (h d)")[:, :, s.head_cols()],
                                       ACT.Copy).then_inc(t["wh"], 1)

                def qk_high(s):
                    if s.u == 1:
                        act.wait_ge(t["pr"], s.head_done() + 2)
                        act.activation(qs[0:DH, s.par, :], psP[0:DH, :], ACT.Copy).then_inc(t["qh"], 1)
                        act.activation(ks[0:DH, s.par, :], psP[DH:P, :], ACT.Copy).then_inc(t["kh"], 1)

                def exps(s):
                    act.wait_ge(t["mx"], s.done())
                    if not isinstance(s.i, int) or s.j > 7:
                        act.wait_ge(t["T"], s.done(-6))
                        if s.u == 0:
                            act.wait_ge(t["rs"], s.head_done(-1))
                    act.activation(pr[:, s.j % 8, 0:s.keys], psS[:, s.j % 4, 0:s.keys], ACT.Exp,
                                   bias=nmax[:, s.par, s.qt:s.qt + 1],
                                   accum_out=rsum[:, s.par, s.qt:s.qt + 1]).then_inc(t["ex"], 1)

                def take_p(s):
                    if s.u in ON_ACT:
                        act.wait_ge(t["T"], s.done())
                        act.activation(flat(pT[:, s.j % 4, 0:s.qt + 1, :]), psT[:, s.j % 2, 0:s.keys], ACT.Copy).then_inc(t["ea"], 1)

                def take_o(b, n):
                    act.wait_ge(t["oT"], b * NP + n + 1)
                    act.activation(oT[:, n, :], psS[:, n % 4, :], ACT.Copy).then_inc(t["oTa"], 1)

                def body(b, before):
                    if before:
                        take_o(b - 1, 0)
                        take_o(b - 1, 2)
                    act.wait_ge(t["xT"], b + 1)
                    act.activation(xT[:, :], psP[:, :], ACT.Identity, bias=lnb[:, :], scale=lng[:, :]).then_inc(t["xa"], 1)
                    act.wait_ge(t["xa"], b + 1)
                    act.activation(xh[:, :], xT[:, :], ACT.Copy).then_inc(t["xh"], 1)
                    if before:
                        take_o(b - 1, 4)
                        take_o(b - 1, 6)
                    for n, bank in ((0, psT[:, :, :]), (2, psS[:, 2:4, :])):
                        act.wait_ge(t["V"], b * 4 + n + 1)
                        act.activation(v[:, n, :].rearrange("p (a d) -> p a d", a=2), bank, ACT.Copy).then_inc(t["va"], 1)
                    slots(act, b, (4, take_p), (-TPB - 1, w_high), (1, exps), (-TPB, qk_high))

                batches(act, body)
                for n in range(0, NP, 2):
                    take_o(BATCH - 1, n)

            @block.tensor
            def _(pe):
                pe.wait_ge(t["cst"], P // FRAME + 1)

                def project(s):
                    if s.u == 1:
                        pe.wait_ge(t["wl"], s.head_done())
                        pe.wait_ge(t["kl"], s.head_done() + 1)
                        mm3(pe, psP[:, :], wh[:, s.par, :], wl[:, s.par, :], xh[:, :], xl[:, :]).then_inc(t["pr"], 1)

                def scores(s):
                    if s.u == 0:
                        pe.wait_ge(t["kl"], s.head_done() + 2)
                        pe.wait_ge(t["kk"], s.head_done() + 1)
                    pe.wait_ge(t["ex"], s.done())
                    rows = slice(s.qt * P, s.qt * P + P)
                    n = max(s.keys, 2 * P)
                    out = psS[:, s.j % 4, 0:n]
                    pe.matmul(out, qs[:, s.par, rows], ks[:, s.par, 0:n], start=True, stop=False)
                    pe.matmul(out, qs[0:DH, s.par, rows], kl[:, s.par, 0:n], start=False, stop=False)
                    pe.matmul(psS[:, s.j % 4, s.keys - P:s.keys], identb[:, :], mask[:, :], start=False, stop=True).then_inc(t["S"], 1)

                def p_out(s):
                    same = [u for u in range(TPB) if (u in ON_ACT) == (s.u in ON_ACT)]
                    return t["ea" if s.u in ON_ACT else "ed"], s.head_done(same.index(s.u) + 1, len(same))

                def turn(s):
                    pe.wait_ge(t["ex"], s.done() + 4)
                    if not isinstance(s.i, int) or s.j > 1:
                        pe.wait_ge(*p_out(Slot(s.b, s.i, s.j - 2)))
                    for n in range(s.qt + 1):
                        last = pe.transpose(psT[:, s.j % 2, n * P:n * P + P], pr[:, s.j % 8, n * P:n * P + P], ident[:, :])
                    last.then_inc(t["T"], 1)

                def weigh(s):
                    pe.wait_ge(*p_out(s))
                    if s.u == 0:
                        pe.wait_ge(t["nr"], s.head_done())
                    for n in range(s.qt + 1):
                        last = pe.matmul(psO[:, s.qt * DH:s.qt * DH + DH], pT[:, s.j % 4, n, :], v[:, n, s.head_cols()],
                                         start=(n == 0), stop=(n == s.qt))
                    last.then_inc(t["PV"], 1)

                def turn_o(b, n):
                    if n >= 4:
                        pe.wait_ge(t[("oTa", "oTd")[n % 2]], b * 4 + n // 2 - 1)
                    for m in range(TPB):
                        last = pe.transpose(psS[:, n % 4, m * P:m * P + P], o[:, m, n * P:n * P + P], ident[:, :])
                    last.then_inc(t["oT"], 1)

                def output(b, m):
                    for n in range(NP):
                        last = pe.matmul(psO[:, m * P:m * P + P], oT[:, n, m * P:m * P + P], wout[:, n, :],
                                         start=(n == 0), stop=(n == NP - 1))
                    last.then_inc(t["out"], 1)

                def body(b, before):
                    if before:
                        pe.wait_ge(t["nr"], b * HEADS + 1)
                        for n in range(4):
                            turn_o(b - 1, n)
                    pe.wait_ge(t["xn"], b + 1)
                    for n in range(TPB):
                        last = pe.transpose(psP[:, n * P:n * P + P], xn[:, n, :], ident[:, :])
                    last.then_inc(t["xT"], 1)
                    if before:
                        for n in range(4, NP):
                            turn_o(b - 1, n)
                    pe.wait_ge(t["xl"], b + 1)
                    for n, bank in enumerate((psT[:, :, :], psS[:, 0:2, :], psS[:, 2:4, :], psT[:, :, :])):
                        if before and n == 1:
                            pe.wait_ge(t["oTa"], b * 4)
                            pe.wait_ge(t["oTd"], b * 4)
                        if n == 3:
                            pe.wait_ge(t["va"], b * 2 + 1)
                        for half in range(2):
                            cols = slice(half * 512, half * 512 + 512)
                            last = mm3(pe, bank[:, half, :], xh[:, n * P:n * P + P], xl[:, n * P:n * P + P], wvh[:, cols], wvl[:, cols])
                        last.then_inc(t["V"], 1)

                    def last_output(s):
                        if before and first(s) and s.j < TPB:
                            output(b - 1, s.j)

                    def v_there(s):
                        if first(s) and s.j == 0:
                            pe.wait_ge(t["va"], b * 2 + 2)
                            pe.wait_ge(t["vd"], b * 2 + 2)

                    def out_added(s):
                        if before and first(s) and s.j == 0:
                            pe.wait_ge(t["res"], b)

                    slots(pe, b, (0, v_there), (0, scores), (3, turn), (-TPB, project), (5, out_added), (5, weigh),
                          (-2, last_output))

                batches(pe, body)
                pe.wait_ge(t["nr"], BATCH * HEADS + 1)
                for n in range(NP):
                    turn_o(BATCH - 1, n)
                pe.wait_ge(t["oTa"], BATCH * 4)
                pe.wait_ge(t["oTd"], BATCH * 4)
                for m in range(TPB):
                    output(BATCH - 1, m)

            @block.vector
            def _(dve):
                self.ln_vector(dve, t["var"], t["root"], t["ln"])
                dve.sem_inc(t["kl"], 2)
                dve.sem_inc(t["ex"], 4)
                dve.sem_inc(t["nr"], 1)

                def q_low(s):
                    if s.u == 2:
                        dve.wait_ge(t["kh"], s.head_done())
                        dve.tensor_tensor(qs[DH:P, s.par, :], psP[0:DH, :], qs[0:DH, s.par, :].bitcast(F32), ALU.subtract).then_inc(t["ql"], 1)

                def k_low(s):
                    if s.u == 2:
                        dve.tensor_tensor(kl[:, s.par, :], psP[DH:P, :], ks[0:DH, s.par, :].bitcast(F32), ALU.subtract).then_inc(t["kl"], 1)

                def row_max(s):
                    dve.wait_ge(t["S"], s.done())
                    dve.tensor_reduce(nmax[:, s.par, s.qt:s.qt + 1], psS[:, s.j % 4, 0:s.keys], AX.X, ALU.max, negate=True).then_inc(t["mx"], 1)

                def take_p(s):
                    if s.u not in ON_ACT:
                        dve.wait_ge(t["T"], s.done())
                        dve.tensor_copy(flat(pT[:, s.j % 4, 0:s.qt + 1, :]), psT[:, s.j % 2, 0:s.keys]).then_inc(t["ed"], 1)

                def invert(s):
                    if s.u == 3:
                        dve.wait_ge(t["ex"], s.done() + 4)
                        dve.reciprocal(rinv[:, s.par, :], rsum[:, s.par, :]).then_inc(t["rs"], 1)

                def norm(s):
                    if s.u == 3:
                        dve.wait_ge(t["PV"], s.done())
                        dve.wait_ge(t["rs"], s.head_done())
                        dve.tensor_tensor(o[:, :, s.head_cols()], psO[:, 0:TPB * DH].rearrange("p (t d) -> p t d", t=TPB),
                                          rinv[:, s.par, :].unsqueeze(2).broadcast_to([P, TPB, DH]), ALU.mult).then_inc(t["nr"], 1)

                def take_o(b, n):
                    dve.wait_ge(t["oT"], b * NP + n + 1)
                    dve.tensor_copy(oT[:, n, :], psS[:, n % 4, :]).then_inc(t["oTd"], 1)

                def add_output(b):
                    rows = flat(x[:, bass.ds(b * TPB, TPB), :])
                    dve.wait_ge(t["out"], b * TPB + TPB)
                    dve.wait_ge(t["xb"], b + 1)
                    dve.tensor_tensor(rows, rows, psO[:, :], ALU.add).then_inc(t["res"], 1)

                def stats(b):
                    dve.wait_ge(t["res"], b + 1)
                    for n in range(TPB):
                        self.take_stats(dve, b * TPB + n)

                def body(b, before):
                    for n in range(TPB):
                        r = bass.ds(b * TPB + n, 1)
                        last = dve.tensor_scalar(xn[:, n, :], x[:, r, :].rearrange("p a d -> p (a d)"), self.mean[:, r],
                                                 self.rstd[:, r], ALU.subtract, ALU.mult)
                    last.then_inc(t["xn"], 1)
                    if before:
                        take_o(b - 1, 1)
                        take_o(b - 1, 3)
                    dve.wait_ge(t["xh"], b + 1)
                    dve.tensor_tensor(xl[:, :], xT[:, :], xh[:, :].bitcast(F32), ALU.subtract).then_inc(t["xl"], 1)
                    if before:
                        take_o(b - 1, 5)
                        take_o(b - 1, 7)
                    for n, bank in ((1, psS[:, 0:2, :]), (3, psT[:, :, :])):
                        dve.wait_ge(t["V"], b * 4 + n + 1)
                        dve.tensor_copy(v[:, n, :].rearrange("p (a d) -> p a d", a=2), bank).then_inc(t["vd"], 1)

                    def add_last(s):
                        if before and first(s) and s.j == 1:
                            add_output(b - 1)
                        if before and first(s) and s.j == 4:
                            stats(b - 1)

                    slots(dve, b, (6, norm), (4, take_p), (-TPB, q_low), (-TPB, k_low), (0, row_max), (3, invert), (1, add_last))

                batches(dve, body)
                for n in range(1, NP, 2):
                    take_o(BATCH - 1, n)
                add_output(BATCH - 1)
                stats(BATCH - 1)


def hybrid_block_kernel(nc, *tensors):
    args, out = dict(zip(_INS, tensors)), tensors[len(_INS)]
    with ExitStack() as ctx:
        k = Kernel(nc, ctx, args, out)
        with ExitStack() as first:
            k.first_attention_tensors(first)
            k.qkv_phase()
            with ExitStack() as sums:
                k.acc = sums.enter_context(nc.psum_tensor("acc", [P, 3, NC, P], F32))
                for step in range(TTT_STEPS):
                    k.gradient_phase(step)
                    k.schulz_phase(step)
            k.query_phase()
        k.moe_phase(0)
        k.attention_phase()
        k.moe_phase(1)


_INS = ["L0_attn_a_x", "L0_attn_a_qkv_w", "L0_attn_a_qkv_b", "L0_attn_a_qn_scale", "L0_attn_a_qn_bias",
        "L0_attn_a_kn_scale", "L0_attn_a_kn_bias", "L0_attn_a_ttt_gate", "L0_attn_a_ttt_val", "L0_attn_a_ttt_proj",
        "L0_attn_a_proj_w", "L0_attn_a_proj_b", "L0_attn_b_g", "L0_attn_b_b", "L0_attn_b_w_qkv", "L0_attn_b_w_out",
        "L0_attn_b_b_out", "L0_ffn_We", "L0_ffn_be", "L0_ffn_Wg", "L0_ffn_bg"]
_OUTS = [((BATCH, SEQ, P), "float32")]


def kernel(**inputs):
    import numpy as _np
    import concourse.bacc as _bacc
    from concourse import mybir as _mybir
    from concourse.bass_utils import run_bass_kernel_spmd as _run

    nc = _bacc.Bacc("TRN2", target_bir_lowering=False, num_devices=1)
    arrays, args = {}, []
    for name in _INS:
        a = _np.ascontiguousarray(inputs[name])
        arrays[f"in_{name}_dram"] = a
        args.append(nc.dram_tensor(f"in_{name}_dram", a.shape, _mybir.dt.from_np(a.dtype), kind="ExternalInput").ap())
    for i, (shape, dtype) in enumerate(_OUTS):
        dt = _mybir.dt.from_np(_np.dtype(dtype))
        args.append(nc.dram_tensor(f"out_{i}_dram", shape, dt, kind="ExternalOutput").ap())
    hybrid_block_kernel(nc, *args)
    r = _run(nc, [arrays], core_ids=[0])
    return r.results[0]["out_0_dram"]
```
